# Optimizing a Trainium2 kernel written in Bass

```python
import numpy as np
import jax
import jax.numpy as jnp

def _softmax(x, axis=-1):
    return jax.nn.softmax(x, axis=axis)

def _gelu(x):
    return jax.nn.gelu(x, approximate=True)

def _silu(x):
    return jax.nn.silu(x)

def _sigmoid(x):
    return jax.nn.sigmoid(x)

def _layernorm(x, axis=-1, eps=1e-05):
    m = jnp.mean(x, axis=axis, keepdims=True)
    v = jnp.var(x, axis=axis, keepdims=True)
    return (x - m) / jnp.sqrt(v + eps)

def _scatter_add(tgt, idx, src, axis=0):
    return tgt.at[idx].add(src)

def _segment_sum(src, seg, n):
    return jax.ops.segment_sum(src, seg, n)
kernel_name = 'mk_perceiver_d4_seqx_r4_d2d5de'

def setup_inputs(seed: int=0):
    np.random.seed(seed)
    _w = jnp.asarray

    def _rec_inputs():
        import jax
        import jax.numpy as jnp
        _rk = jax.random.key(seed)
        x = 7.22e-05 + 1 * jax.random.normal(jax.random.fold_in(_rk, 1), (1, 128, 256), jnp.float32)
        _lenS = 128 - jax.random.randint(jax.random.fold_in(_rk, 7), (1,), 0, max(1, 128 // 4) + 1, jnp.int32)
        _lenS2 = 12544 - jax.random.randint(jax.random.fold_in(_rk, 8), (1,), 0, max(1, 12544 // 4) + 1, jnp.int32)
        _ctx_768P = jax.random.normal(jax.random.fold_in(_rk, 11), (1, 16, 192), jnp.float32)
        _ctx_768c = jax.random.dirichlet(jax.random.fold_in(_rk, 511), 0.3 * jnp.ones((16,), jnp.float32), (1, 12544))
        _ctx_768t = jnp.einsum('bsk,bkd->bsd', _ctx_768c, _ctx_768P)
        _ctx_768t = _ctx_768t * jax.lax.rsqrt(jnp.mean(jnp.square(_ctx_768t)) + 1e-12) * 0.953939
        ctx_768 = -0.000191848 + 0.999787 * (_ctx_768t + 0.3 * jax.random.normal(jax.random.fold_in(_rk, 611), (1, 12544, 192), jnp.float32))
        _validS = jnp.arange(128)[None, :] < _lenS[:, None]
        _validS2 = jnp.arange(12544)[None, :] < _lenS2[:, None]
        _causal = jnp.tril(jnp.ones((128, 128), dtype=bool))
        mask_BxS2_bk0 = jnp.logical_not(jnp.broadcast_to(_validS2[:, :], (1, 12544)))
        return (x, ctx_768, mask_BxS2_bk0)
    x, ctx_768, mask_BxS2_bk0 = _rec_inputs()

    def _L0_xattn_setup():
        import jax, jax.numpy as jnp
        import numpy as np
        HEADS = 8
        DIM_HEAD = 64
        QUERY_DIM = 256
        CONTEXT_DIM = 192
        INNER = HEADS * DIM_HEAD
        key = jax.random.key(seed)
        ks = jax.random.split(key, 8)
        b, n, j = (4, 512, 512)
        x = jax.random.normal(ks[0], (b, n, QUERY_DIM), dtype=jnp.float32)
        context = jax.random.normal(ks[1], (b, j, CONTEXT_DIM), dtype=jnp.float32)
        mask = jax.random.randint(ks[2], (b, j), 0, 2).astype(jnp.bool_)
        W_q = jax.random.normal(ks[3], (QUERY_DIM, INNER), dtype=jnp.float32) / np.sqrt(QUERY_DIM)
        W_k = jax.random.normal(ks[4], (CONTEXT_DIM, INNER), dtype=jnp.float32) / np.sqrt(CONTEXT_DIM)
        W_v = jax.random.normal(ks[5], (CONTEXT_DIM, INNER), dtype=jnp.float32) / np.sqrt(CONTEXT_DIM)
        W_o = jax.random.normal(ks[6], (INNER, QUERY_DIM), dtype=jnp.float32) / np.sqrt(INNER)
        b_o = jax.random.normal(ks[7], (QUERY_DIM,), dtype=jnp.float32) * 0.01
        return {'x': x, 'context': context, 'mask': mask, 'W_q': W_q, 'W_k': W_k, 'W_v': W_v, 'W_o': W_o, 'b_o': b_o}
    _L0_xattn_all = _L0_xattn_setup()
    _L0_xattn_in = {k: v for k, v in _L0_xattn_all.items() if k in ('W_q', 'W_k', 'W_v', 'W_o', 'b_o')}
    del _L0_xattn_all

    def _L0_attn_setup():
        import jax, jax.numpy as jnp
        import numpy as np
        HEAD = 8
        BLOCK = 64
        D_MODEL = 256
        key = jax.random.key(seed)
        ks = jax.random.split(key, 9)
        d = D_MODEL
        s = 0.02
        return {'src': jax.random.normal(ks[0], (4, 1024, d), dtype=jnp.float32), 'Wq': jax.random.normal(ks[1], (d, d), dtype=jnp.float32) * s, 'bq': jax.random.normal(ks[2], (d,), dtype=jnp.float32) * s, 'Wk': jax.random.normal(ks[3], (d, d), dtype=jnp.float32) * s, 'bk': jax.random.normal(ks[4], (d,), dtype=jnp.float32) * s, 'Wv': jax.random.normal(ks[5], (d, d), dtype=jnp.float32) * s, 'bv': jax.random.normal(ks[6], (d,), dtype=jnp.float32) * s, 'Wo': jax.random.normal(ks[7], (d, d), dtype=jnp.float32) * s, 'bo': jax.random.normal(ks[8], (d,), dtype=jnp.float32) * s}
    _L0_attn_all = _L0_attn_setup()
    _L0_attn_in = {k: v for k, v in _L0_attn_all.items() if k in ('Wq', 'bq', 'Wk', 'bk', 'Wv', 'bv', 'Wo', 'bo')}
    del _L0_attn_all

    def _L0_ffn_setup():
        import jax, jax.numpy as jnp
        import numpy as np
        TOP_K = 2
        key = jax.random.key(seed)
        ks = jax.random.split(key, 8)
        B, S, H, F, E = (1, 256, 256, 256, 8)
        Fs = 2 * F
        s = lambda k, shape, scale: jax.random.normal(k, shape, dtype=jnp.float32) * scale
        return {'x': s(ks[0], (B, S, H), 1.0), 'router_w': s(ks[1], (H, E), 0.02), 'gate_w': s(ks[2], (E, H, F), 0.02), 'up_w': s(ks[3], (E, H, F), 0.02), 'down_w': s(ks[4], (E, F, H), 0.02), 'shared_gate_w': s(ks[5], (H, Fs), 0.02), 'shared_up_w': s(ks[6], (H, Fs), 0.02), 'shared_down_w': s(ks[7], (Fs, H), 0.02)}
    _L0_ffn_all = _L0_ffn_setup()
    _L0_ffn_in = {k: v for k, v in _L0_ffn_all.items() if k in ('router_w', 'gate_w', 'up_w', 'down_w', 'shared_gate_w', 'shared_up_w', 'shared_down_w')}
    del _L0_ffn_all

    def _L1_xattn_setup():
        import jax, jax.numpy as jnp
        import numpy as np
        NUM_HEADS = 16
        HEAD_DIM = 64
        INNER = NUM_HEADS * HEAD_DIM
        QUERY_DIM = 256
        CONTEXT_DIM = 192
        SCALE = HEAD_DIM ** (-0.5)
        key = jax.random.key(seed)
        ks = jax.random.split(key, 6)
        B, NQ, NKV = (8, 256, 512)
        query = jax.random.normal(ks[0], (B, NQ, QUERY_DIM), dtype=jnp.float32)
        context = jax.random.normal(ks[1], (B, NKV, CONTEXT_DIM), dtype=jnp.float32)
        w_q = jax.random.normal(ks[2], (QUERY_DIM, INNER), dtype=jnp.float32) * QUERY_DIM ** (-0.5)
        w_kv = jax.random.normal(ks[3], (CONTEXT_DIM, 2 * INNER), dtype=jnp.float32) * CONTEXT_DIM ** (-0.5)
        w_out = jax.random.normal(ks[4], (INNER, QUERY_DIM), dtype=jnp.float32) * INNER ** (-0.5)
        b_out = jax.random.normal(ks[5], (QUERY_DIM,), dtype=jnp.float32) * 0.01
        return {'query': query, 'context': context, 'w_q': w_q, 'w_kv': w_kv, 'w_out': w_out, 'b_out': b_out}
    _L1_xattn_all = _L1_xattn_setup()
    _L1_xattn_in = {k: v for k, v in _L1_xattn_all.items() if k in ('w_q', 'w_kv', 'w_out', 'b_out')}
    del _L1_xattn_all

    def _L1_attn_setup():
        import jax, jax.numpy as jnp
        import numpy as np
        EMBED_DIM = 256
        WINDOW = 64
        NUM_HEADS = 16
        HEAD_DIM = EMBED_DIM // NUM_HEADS
        SCALE = HEAD_DIM ** (-0.5)
        key = jax.random.key(seed)
        ks = jax.random.split(key, 9)
        B, S, E = (4, 1024, EMBED_DIM)
        std = E ** (-0.5)
        x = jax.random.normal(ks[0], (B, S, E), dtype=jnp.float32)
        Wq = jax.random.normal(ks[1], (E, E), dtype=jnp.float32) * std
        Wk = jax.random.normal(ks[2], (E, E), dtype=jnp.float32) * std
        Wv = jax.random.normal(ks[3], (E, E), dtype=jnp.float32) * std
        Wo = jax.random.normal(ks[4], (E, E), dtype=jnp.float32) * std
        bq = jax.random.normal(ks[5], (E,), dtype=jnp.float32) * 0.01
        bk = jax.random.normal(ks[6], (E,), dtype=jnp.float32) * 0.01
        bv = jax.random.normal(ks[7], (E,), dtype=jnp.float32) * 0.01
        bo = jax.random.normal(ks[8], (E,), dtype=jnp.float32) * 0.01
        return {'x': x, 'Wq': Wq, 'bq': bq, 'Wk': Wk, 'bk': bk, 'Wv': Wv, 'bv': bv, 'Wo': Wo, 'bo': bo}
    _L1_attn_all = _L1_attn_setup()
    _L1_attn_in = {k: v for k, v in _L1_attn_all.items() if k in ('Wq', 'bq', 'Wk', 'bk', 'Wv', 'bv', 'Wo', 'bo')}
    del _L1_attn_all

    def _L1_ffn_setup():
        import jax, jax.numpy as jnp
        import numpy as np
        TOP_K = 2
        key = jax.random.key(seed)
        k1, k2, k3 = jax.random.split(key, 3)
        B, S, H, E, D = (4, 256, 256, 32, 256)
        x = jax.random.normal(k1, (B, S, H), dtype=jnp.float32)
        router_w = jax.random.normal(k2, (E, H), dtype=jnp.float32) * (1.0 / np.sqrt(H))
        bound = float(np.sqrt(6.0 / ((1.0 + 0.01 ** 2) * H)))
        expert_weights = jax.random.uniform(k3, (E, H, D), dtype=jnp.float32, minval=-bound, maxval=bound)
        return {'x': x, 'router_w': router_w, 'expert_weights': expert_weights}
    _L1_ffn_all = _L1_ffn_setup()
    _L1_ffn_in = {k: v for k, v in _L1_ffn_all.items() if k in ('router_w', 'expert_weights')}
    del _L1_ffn_all

    def _L2_xattn_setup():
        import jax, jax.numpy as jnp
        import numpy as np
        NUM_HEADS = 16
        CLAMP = 10000.0
        key = jax.random.key(seed)
        ks = jax.random.split(key, 8)
        B, Nq, Nkv, Cq, Ckv = (4, 512, 512, 256, 192)
        s_q = 1.0 / np.sqrt(Cq)
        s_kv = 1.0 / np.sqrt(Ckv)
        return {'query': jax.random.normal(ks[0], (B, Nq, Cq), jnp.float32), 'key_value': jax.random.normal(ks[1], (B, Nkv, Ckv), jnp.float32), 'Wq': jax.random.normal(ks[2], (Cq, Cq), jnp.float32) * s_q, 'bq': jnp.zeros((Cq,), jnp.float32), 'Wk': jax.random.normal(ks[3], (Ckv, Cq), jnp.float32) * s_kv, 'bk': jnp.zeros((Cq,), jnp.float32), 'Wv': jax.random.normal(ks[4], (Ckv, Cq), jnp.float32) * s_kv, 'bv': jnp.zeros((Cq,), jnp.float32), 'Wo': jax.random.normal(ks[5], (Cq, Cq), jnp.float32) * s_q, 'bo': jnp.zeros((Cq,), jnp.float32)}
    _L2_xattn_all = _L2_xattn_setup()
    _L2_xattn_in = {k: v for k, v in _L2_xattn_all.items() if k in ('Wq', 'bq', 'Wk', 'bk', 'Wv', 'bv', 'Wo', 'bo')}
    del _L2_xattn_all

    def _L2_attn_setup():
        import math
        import jax, jax.numpy as jnp
        import numpy as np
        NUM_HEADS = 16
        WINDOW = 64
        NEG_INF = -1e+30
        key = jax.random.key(seed)
        ks = jax.random.split(key, 5)
        B, L, D = (2, 512, 256)
        x = jax.random.normal(ks[0], (B, L, D), dtype=jnp.float32)
        s = 0.02
        Wq = jax.random.normal(ks[1], (D, D), dtype=jnp.float32) * s
        Wk = jax.random.normal(ks[2], (D, D), dtype=jnp.float32) * s
        Wv = jax.random.normal(ks[3], (D, D), dtype=jnp.float32) * s
        Wo = jax.random.normal(ks[4], (D, D), dtype=jnp.float32) * s
        return {'x': x, 'Wq': Wq, 'Wk': Wk, 'Wv': Wv, 'Wo': Wo, 'sep_gate': jnp.float32(0.1), 'align_gate': jnp.float32(0.1), 'coh_gate': jnp.float32(0.1)}
    _L2_attn_all = _L2_attn_setup()
    _L2_attn_in = {k: v for k, v in _L2_attn_all.items() if k in ('Wq', 'Wk', 'Wv', 'Wo', 'sep_gate', 'align_gate', 'coh_gate')}
    del _L2_attn_all

    def _L2_ffn_setup():
        import jax, jax.numpy as jnp
        import numpy as np
        B, S, D = (1, 512, 256)
        E, K, F = (64, 8, 192)
        SF = 192
        C = 128
        ROUTED_SCALE = 1.0

        def _moe_forward(x, router_w, w_gate, w_up, w_down, ws_gate_up, ws_down):
            T = x.shape[0]
            logits = x.astype(jnp.float32) @ router_w.T
            probs = jax.nn.softmax(logits, axis=-1)
            topk_w, topk_ids = jax.lax.top_k(probs, K)
            topk_w = topk_w / jnp.sum(topk_w, axis=-1, keepdims=True)
            topk_w = topk_w.astype(x.dtype)
            N = T * K
            flat_e = topk_ids.reshape(-1)
            flat_w = topk_w.reshape(-1)
            tok = jnp.arange(N) // K
            onehot = flat_e[:, None] == jnp.arange(E)[None, :]
            pos = jnp.cumsum(onehot, axis=0)[jnp.arange(N), flat_e] - 1
            valid = pos < C
            idx = jnp.where(valid, flat_e * C + pos, E * C)
            x_buf = jnp.zeros((E * C + 1, x.shape[1]), x.dtype).at[idx].set(x[tok])
            xb = x_buf[:E * C].reshape(E, C, -1)
            g = jnp.einsum('ecd,edf->ecf', xb, w_gate)
            u = jnp.einsum('ecd,edf->ecf', xb, w_up)
            h = jax.nn.silu(g) * u
            y = jnp.einsum('ecf,efd->ecd', h, w_down).reshape(E * C, -1)
            safe = jnp.where(valid, idx, 0)
            contrib = y[safe] * (flat_w * valid.astype(flat_w.dtype))[:, None]
            routed = jax.ops.segment_sum(contrib, tok, num_segments=T)
            routed = routed * ROUTED_SCALE
            gu = x @ ws_gate_up
            sg, su = (gu[:, :SF], gu[:, SF:])
            shared = jax.nn.silu(sg) * su @ ws_down
            return routed + shared
        key = jax.random.key(seed)
        ks = jax.random.split(key, 7)
        w = 0.02
        return {'hidden_states': jax.random.normal(ks[0], (B, S, D), jnp.float32), 'router_w': jax.random.normal(ks[1], (E, D), jnp.float32) * w, 'w_gate': jax.random.normal(ks[2], (E, D, F), jnp.float32) * w, 'w_up': jax.random.normal(ks[3], (E, D, F), jnp.float32) * w, 'w_down': jax.random.normal(ks[4], (E, F, D), jnp.float32) * w, 'ws_gate_up': jax.random.normal(ks[5], (D, 2 * SF), jnp.float32) * w, 'ws_down': jax.random.normal(ks[6], (SF, D), jnp.float32) * w}
    _L2_ffn_all = _L2_ffn_setup()
    _L2_ffn_in = {k: v for k, v in _L2_ffn_all.items() if k in ('router_w', 'w_gate', 'w_up', 'w_down', 'ws_gate_up', 'ws_down')}
    del _L2_ffn_all

    def _L3_xattn_setup():
        import jax, jax.numpy as jnp
        import numpy as np
        N_HEADS = 16
        D_EMBED = 256
        D_CROSS = 192
        D_HEAD = D_EMBED // N_HEADS
        key = jax.random.key(seed)
        ks = jax.random.split(key, 10)
        B, SQ, SKV = (8, 1024, 77)
        s_e = 1.0 / np.sqrt(D_EMBED)
        s_c = 1.0 / np.sqrt(D_CROSS)
        return {'x': jax.random.normal(ks[0], (B, SQ, D_EMBED), jnp.float32), 'y': jax.random.normal(ks[1], (B, SKV, D_CROSS), jnp.float32), 'wq': jax.random.normal(ks[2], (D_EMBED, D_EMBED), jnp.float32) * s_e, 'bq': jnp.zeros((D_EMBED,), jnp.float32), 'wk': jax.random.normal(ks[3], (D_CROSS, D_EMBED), jnp.float32) * s_c, 'bk': jnp.zeros((D_EMBED,), jnp.float32), 'wv': jax.random.normal(ks[4], (D_CROSS, D_EMBED), jnp.float32) * s_c, 'bv': jnp.zeros((D_EMBED,), jnp.float32), 'wo': jax.random.normal(ks[5], (D_EMBED, D_EMBED), jnp.float32) * s_e, 'bo': jnp.zeros((D_EMBED,), jnp.float32)}
    _L3_xattn_all = _L3_xattn_setup()
    _L3_xattn_in = {k: v for k, v in _L3_xattn_all.items() if k in ('wq', 'bq', 'wk', 'bk', 'wv', 'bv', 'wo', 'bo')}
    del _L3_xattn_all

    def _L3_attn_setup():
        import jax, jax.numpy as jnp
        import numpy as np
        D_MODEL = 256
        NHEAD = 16
        D_K = D_MODEL // NHEAD
        MAX_REL = 256
        key = jax.random.key(seed)
        ks = jax.random.split(key, 6)
        B, S = (4, 512)
        s = 1.0 / np.sqrt(D_MODEL)
        x = jax.random.normal(ks[0], (B, S, D_MODEL), dtype=jnp.float32)
        W_qkv = jax.random.normal(ks[1], (D_MODEL, 3 * D_MODEL), dtype=jnp.float32) * s
        b_qkv = jnp.zeros((3 * D_MODEL,), dtype=jnp.float32)
        W_out = jax.random.normal(ks[2], (D_MODEL, D_MODEL), dtype=jnp.float32) * s
        b_out = jnp.zeros((D_MODEL,), dtype=jnp.float32)
        rel_bias = jax.random.normal(ks[3], (2 * MAX_REL + 1, NHEAD), dtype=jnp.float32) * 0.02
        return {'x': x, 'W_qkv': W_qkv, 'b_qkv': b_qkv, 'W_out': W_out, 'b_out': b_out, 'rel_bias': rel_bias}
    _L3_attn_all = _L3_attn_setup()
    _L3_attn_in = {k: v for k, v in _L3_attn_all.items() if k in ('W_qkv', 'b_qkv', 'W_out', 'b_out', 'rel_bias')}
    del _L3_attn_all

    def _L3_ffn_setup():
        import jax, jax.numpy as jnp
        import numpy as np
        D_MODEL = 256
        D_FF = 1024
        N_EXPERTS = 8
        D_EXPERT = D_FF // N_EXPERTS
        TOP_K = 2
        LB_WEIGHT = 0.01
        B, S = (4, 512)

        def _top_k_softmax(logits, k):
            vals, _ = jax.lax.top_k(logits, k)
            thresh = vals[..., -1:]
            masked = jnp.where(logits >= thresh, logits, -jnp.inf)
            return jax.nn.softmax(masked, axis=-1)
        key = jax.random.key(seed)
        ks = jax.random.split(key, 8)
        x = jax.random.normal(ks[0], (B, S, D_MODEL), dtype=jnp.float32)
        w1 = jax.random.normal(ks[1], (N_EXPERTS, D_MODEL, D_EXPERT), dtype=jnp.float32) * (1.0 / np.sqrt(D_MODEL))
        b1 = jnp.zeros((N_EXPERTS, D_EXPERT), dtype=jnp.float32)
        w2 = jax.random.normal(ks[2], (N_EXPERTS, D_EXPERT, D_MODEL), dtype=jnp.float32) * (1.0 / np.sqrt(D_EXPERT))
        b2 = jnp.zeros((N_EXPERTS, D_MODEL), dtype=jnp.float32)
        centroids = jax.random.normal(ks[3], (N_EXPERTS, D_MODEL), dtype=jnp.float32) * 0.02
        w_route = jax.random.normal(ks[4], (N_EXPERTS, D_MODEL), dtype=jnp.float32) * (1.0 / np.sqrt(D_MODEL))
        return {'x': x, 'w1': w1, 'b1': b1, 'w2': w2, 'b2': b2, 'centroids': centroids, 'w_route': w_route}
    _L3_ffn_all = _L3_ffn_setup()
    _L3_ffn_in = {k: v for k, v in _L3_ffn_all.items() if k in ('w1', 'b1', 'w2', 'b2', 'centroids', 'w_route')}
    del _L3_ffn_all
    return {'x': x, 'ctx_768': ctx_768, 'mask_BxS2_bk0': mask_BxS2_bk0, 'L0_xattn_W_q': _L0_xattn_in['W_q'], 'L0_xattn_W_k': _L0_xattn_in['W_k'], 'L0_xattn_W_v': _L0_xattn_in['W_v'], 'L0_xattn_W_o': _L0_xattn_in['W_o'], 'L0_xattn_b_o': _L0_xattn_in['b_o'], 'L0_attn_Wq': _L0_attn_in['Wq'], 'L0_attn_bq': _L0_attn_in['bq'], 'L0_attn_Wk': _L0_attn_in['Wk'], 'L0_attn_bk': _L0_attn_in['bk'], 'L0_attn_Wv': _L0_attn_in['Wv'], 'L0_attn_bv': _L0_attn_in['bv'], 'L0_attn_Wo': _L0_attn_in['Wo'], 'L0_attn_bo': _L0_attn_in['bo'], 'L0_ffn_router_w': _L0_ffn_in['router_w'], 'L0_ffn_gate_w': _L0_ffn_in['gate_w'], 'L0_ffn_up_w': _L0_ffn_in['up_w'], 'L0_ffn_down_w': _L0_ffn_in['down_w'], 'L0_ffn_shared_gate_w': _L0_ffn_in['shared_gate_w'], 'L0_ffn_shared_up_w': _L0_ffn_in['shared_up_w'], 'L0_ffn_shared_down_w': _L0_ffn_in['shared_down_w'], 'L1_xattn_w_q': _L1_xattn_in['w_q'], 'L1_xattn_w_kv': _L1_xattn_in['w_kv'], 'L1_xattn_w_out': _L1_xattn_in['w_out'], 'L1_xattn_b_out': _L1_xattn_in['b_out'], 'L1_attn_Wq': _L1_attn_in['Wq'], 'L1_attn_bq': _L1_attn_in['bq'], 'L1_attn_Wk': _L1_attn_in['Wk'], 'L1_attn_bk': _L1_attn_in['bk'], 'L1_attn_Wv': _L1_attn_in['Wv'], 'L1_attn_bv': _L1_attn_in['bv'], 'L1_attn_Wo': _L1_attn_in['Wo'], 'L1_attn_bo': _L1_attn_in['bo'], 'L1_ffn_router_w': _L1_ffn_in['router_w'], 'L1_ffn_expert_weights': _L1_ffn_in['expert_weights'], 'L2_xattn_Wq': _L2_xattn_in['Wq'], 'L2_xattn_bq': _L2_xattn_in['bq'], 'L2_xattn_Wk': _L2_xattn_in['Wk'], 'L2_xattn_bk': _L2_xattn_in['bk'], 'L2_xattn_Wv': _L2_xattn_in['Wv'], 'L2_xattn_bv': _L2_xattn_in['bv'], 'L2_xattn_Wo': _L2_xattn_in['Wo'], 'L2_xattn_bo': _L2_xattn_in['bo'], 'L2_attn_Wq': _L2_attn_in['Wq'], 'L2_attn_Wk': _L2_attn_in['Wk'], 'L2_attn_Wv': _L2_attn_in['Wv'], 'L2_attn_Wo': _L2_attn_in['Wo'], 'L2_attn_sep_gate': _L2_attn_in['sep_gate'], 'L2_attn_align_gate': _L2_attn_in['align_gate'], 'L2_attn_coh_gate': _L2_attn_in['coh_gate'], 'L2_ffn_router_w': _L2_ffn_in['router_w'], 'L2_ffn_w_gate': _L2_ffn_in['w_gate'], 'L2_ffn_w_up': _L2_ffn_in['w_up'], 'L2_ffn_w_down': _L2_ffn_in['w_down'], 'L2_ffn_ws_gate_up': _L2_ffn_in['ws_gate_up'], 'L2_ffn_ws_down': _L2_ffn_in['ws_down'], 'L3_xattn_wq': _L3_xattn_in['wq'], 'L3_xattn_bq': _L3_xattn_in['bq'], 'L3_xattn_wk': _L3_xattn_in['wk'], 'L3_xattn_bk': _L3_xattn_in['bk'], 'L3_xattn_wv': _L3_xattn_in['wv'], 'L3_xattn_bv': _L3_xattn_in['bv'], 'L3_xattn_wo': _L3_xattn_in['wo'], 'L3_xattn_bo': _L3_xattn_in['bo'], 'L3_attn_W_qkv': _L3_attn_in['W_qkv'], 'L3_attn_b_qkv': _L3_attn_in['b_qkv'], 'L3_attn_W_out': _L3_attn_in['W_out'], 'L3_attn_b_out': _L3_attn_in['b_out'], 'L3_attn_rel_bias': _L3_attn_in['rel_bias'], 'L3_ffn_w1': _L3_ffn_in['w1'], 'L3_ffn_b1': _L3_ffn_in['b1'], 'L3_ffn_w2': _L3_ffn_in['w2'], 'L3_ffn_b2': _L3_ffn_in['b2'], 'L3_ffn_centroids': _L3_ffn_in['centroids'], 'L3_ffn_w_route': _L3_ffn_in['w_route']}

def reference(x, ctx_768, mask_BxS2_bk0, L0_xattn_W_q, L0_xattn_W_k, L0_xattn_W_v, L0_xattn_W_o, L0_xattn_b_o, L0_attn_Wq, L0_attn_bq, L0_attn_Wk, L0_attn_bk, L0_attn_Wv, L0_attn_bv, L0_attn_Wo, L0_attn_bo, L0_ffn_router_w, L0_ffn_gate_w, L0_ffn_up_w, L0_ffn_down_w, L0_ffn_shared_gate_w, L0_ffn_shared_up_w, L0_ffn_shared_down_w, L1_xattn_w_q, L1_xattn_w_kv, L1_xattn_w_out, L1_xattn_b_out, L1_attn_Wq, L1_attn_bq, L1_attn_Wk, L1_attn_bk, L1_attn_Wv, L1_attn_bv, L1_attn_Wo, L1_attn_bo, L1_ffn_router_w, L1_ffn_expert_weights, L2_xattn_Wq, L2_xattn_bq, L2_xattn_Wk, L2_xattn_bk, L2_xattn_Wv, L2_xattn_bv, L2_xattn_Wo, L2_xattn_bo, L2_attn_Wq, L2_attn_Wk, L2_attn_Wv, L2_attn_Wo, L2_attn_sep_gate, L2_attn_align_gate, L2_attn_coh_gate, L2_ffn_router_w, L2_ffn_w_gate, L2_ffn_w_up, L2_ffn_w_down, L2_ffn_ws_gate_up, L2_ffn_ws_down, L3_xattn_wq, L3_xattn_bq, L3_xattn_wk, L3_xattn_bk, L3_xattn_wv, L3_xattn_bv, L3_xattn_wo, L3_xattn_bo, L3_attn_W_qkv, L3_attn_b_qkv, L3_attn_W_out, L3_attn_b_out, L3_attn_rel_bias, L3_ffn_w1, L3_ffn_b1, L3_ffn_w2, L3_ffn_b2, L3_ffn_centroids, L3_ffn_w_route):
    import jax
    import jax.numpy as jnp

    def _L0_xattn_ref(x, context, mask, W_q, W_k, W_v, W_o, b_o):
        import jax, jax.numpy as jnp
        import numpy as np
        HEADS = 8
        DIM_HEAD = 64
        QUERY_DIM = 256
        CONTEXT_DIM = 192
        INNER = HEADS * DIM_HEAD
        b, n, _ = x.shape
        j = context.shape[1]
        scale = DIM_HEAD ** (-0.5)
        q = (x @ W_q).reshape(b, n, HEADS, DIM_HEAD)
        k = (context @ W_k).reshape(b, j, HEADS, DIM_HEAD)
        v = (context @ W_v).reshape(b, j, HEADS, DIM_HEAD)
        sim = jnp.einsum('bihd,bjhd->bhij', q, k) * scale
        max_neg = -jnp.finfo(sim.dtype).max
        sim = jnp.where(mask[:, None, None, :], sim, max_neg)
        attn = jax.nn.softmax(sim, axis=-1)
        out = jnp.einsum('bhij,bjhd->bihd', attn, v).reshape(b, n, INNER)
        return out @ W_o + b_o

    def _L0_attn_ref(src, Wq, bq, Wk, bk, Wv, bv, Wo, bo):
        import jax, jax.numpy as jnp
        import numpy as np
        HEAD = 8
        BLOCK = 64
        D_MODEL = 256
        B, S, D = src.shape
        H, bs = (HEAD, BLOCK)
        dk = D // H
        nb = S // bs
        q = (src @ Wq + bq).reshape(B, nb, bs, H, dk)
        k = (src @ Wk + bk).reshape(B, nb, bs, H, dk)
        v = (src @ Wv + bv).reshape(B, nb, bs, H, dk)
        scores = jnp.einsum('bnqhd,bnkhd->bhnqk', q, k) * dk ** (-0.5)
        probs = jax.nn.softmax(scores, axis=-1)
        out = jnp.einsum('bhnqk,bnkhd->bnqhd', probs, v).reshape(B, S, D)
        return out @ Wo + bo

    def _L0_ffn_ref(x, router_w, gate_w, up_w, down_w, shared_gate_w, shared_up_w, shared_down_w):
        import jax, jax.numpy as jnp
        import numpy as np
        TOP_K = 2
        B, S, H = x.shape
        N = B * S
        xf = x.reshape(N, H)
        scores = jax.nn.softmax(xf @ router_w, axis=-1)
        topk_scores, topk_idx = jax.lax.top_k(scores, TOP_K)
        E = scores.shape[-1]
        combine = jnp.zeros((N, E), dtype=x.dtype).at[jnp.arange(N)[:, None], topk_idx].add(topk_scores)
        g = jnp.einsum('nh,ehf->enf', xf, gate_w)
        u = jnp.einsum('nh,ehf->enf', xf, up_w)
        y = jnp.einsum('enf,efh->enh', jax.nn.silu(g) * u, down_w)
        routed = jnp.einsum('enh,ne->nh', y, combine)
        shared = jax.nn.silu(xf @ shared_gate_w) * (xf @ shared_up_w) @ shared_down_w
        return (shared + routed).reshape(B, S, H)

    def _L1_xattn_ref(query, context, w_q, w_kv, w_out, b_out):
        import jax, jax.numpy as jnp
        import numpy as np
        NUM_HEADS = 16
        HEAD_DIM = 64
        INNER = NUM_HEADS * HEAD_DIM
        QUERY_DIM = 256
        CONTEXT_DIM = 192
        SCALE = HEAD_DIM ** (-0.5)
        B, NQ, _ = query.shape
        NKV = context.shape[1]
        q = query @ w_q
        kv = context @ w_kv
        k, v = jnp.split(kv, 2, axis=-1)
        q = q.reshape(B, NQ, NUM_HEADS, HEAD_DIM).transpose(0, 2, 1, 3)
        k = k.reshape(B, NKV, NUM_HEADS, HEAD_DIM).transpose(0, 2, 1, 3)
        v = v.reshape(B, NKV, NUM_HEADS, HEAD_DIM).transpose(0, 2, 1, 3)
        scores = jnp.einsum('bhqd,bhkd->bhqk', q, k) * SCALE
        attn = jax.nn.softmax(scores, axis=-1)
        out = jnp.einsum('bhqk,bhkd->bhqd', attn, v)
        out = out.transpose(0, 2, 1, 3).reshape(B, NQ, INNER)
        return out @ w_out + b_out

    def _L1_attn_ref(x, Wq, bq, Wk, bk, Wv, bv, Wo, bo):
        import jax, jax.numpy as jnp
        import numpy as np
        EMBED_DIM = 256
        WINDOW = 64
        NUM_HEADS = 16
        HEAD_DIM = EMBED_DIM // NUM_HEADS
        SCALE = HEAD_DIM ** (-0.5)
        B, S, E = x.shape
        W = WINDOW
        nw = S // W
        q = x @ Wq.T + bq
        k = x @ Wk.T + bk
        v = x @ Wv.T + bv
        qw = q.reshape(B, nw, W, E)
        kw = k.reshape(B, nw, W, E)
        vw = v.reshape(B, nw, W, E)
        scores = jnp.einsum('bnqe,bnke->bnqk', qw, kw) * SCALE
        causal = jnp.tril(jnp.ones((W, W), dtype=bool))
        scores = jnp.where(causal, scores, -jnp.inf)
        attn = jax.nn.softmax(scores, axis=-1)
        out = jnp.einsum('bnqk,bnke->bnqe', attn, vw).reshape(B, S, E)
        out = out @ Wo.T + bo
        return out + x

    def _L1_ffn_ref(x, router_w, expert_weights):
        import jax, jax.numpy as jnp
        import numpy as np
        TOP_K = 2
        B, S, H = x.shape
        E = router_w.shape[0]
        T = B * S
        logits = jnp.einsum('bsh,eh->bse', x, router_w)
        rw = jax.nn.softmax(logits, axis=-1).reshape(T, E)
        x_flat = x.reshape(T, H)
        vals, idx = jax.lax.top_k(rw, TOP_K)
        w_masked = jnp.zeros_like(rw).at[jnp.arange(T)[:, None], idx].set(vals)

        def body(acc, we):
            w_e, W_e = we
            return (acc + x_flat * w_e[:, None] @ W_e, None)
        out_flat, _ = jax.lax.scan(body, jnp.zeros((T, H), dtype=x.dtype), (w_masked.T, expert_weights))
        return out_flat.reshape(B, S, H)

    def _L2_xattn_ref(query, key_value, Wq, bq, Wk, bk, Wv, bv, Wo, bo):
        import jax, jax.numpy as jnp
        import numpy as np
        NUM_HEADS = 16
        CLAMP = 10000.0
        B, Nq, Cq = query.shape
        Nkv = key_value.shape[1]
        H = NUM_HEADS
        D = Cq // H
        scale = D ** (-0.5)
        q = (query @ Wq + bq).reshape(B, Nq, H, D).transpose(0, 2, 1, 3)
        k = (key_value @ Wk + bk).reshape(B, Nkv, H, D).transpose(0, 2, 1, 3)
        v = (key_value @ Wv + bv).reshape(B, Nkv, H, D).transpose(0, 2, 1, 3)
        attn = jnp.einsum('bhqd,bhkd->bhqk', q, k) * scale
        attn = jnp.clip(attn, -CLAMP, CLAMP)
        attn = jax.nn.softmax(attn, axis=-1)
        attn = jnp.where(jnp.any(jnp.isnan(attn)), jnp.asarray(1.0 / Nkv, attn.dtype), attn)
        x = jnp.einsum('bhqk,bhkd->bqhd', attn, v).reshape(B, Nq, Cq)
        return x @ Wo + bo

    def _L2_attn_ref(x, Wq, Wk, Wv, Wo, sep_gate, align_gate, coh_gate):
        import math
        import jax, jax.numpy as jnp
        import numpy as np
        NUM_HEADS = 16
        WINDOW = 64
        NEG_INF = -1e+30
        B, L, D = x.shape
        H = NUM_HEADS
        hd = D // H
        scale = math.sqrt(hd)

        def proj(W):
            return (x @ W.T).reshape(B, L, H, hd).transpose(0, 2, 1, 3)
        q, k, v = (proj(Wq), proj(Wk), proj(Wv))
        scores = jnp.einsum('bhqd,bhkd->bhqk', q, k) / scale
        similarity = jax.nn.sigmoid(scores)
        separation = -sep_gate * similarity ** 2
        alignment = align_gate * scores
        score_mean = jnp.mean(scores, axis=-1, keepdims=True)
        cohesion = -coh_gate * jnp.abs(scores - score_mean)
        scores = scores + separation + alignment + cohesion
        i = jnp.arange(L)[:, None]
        j = jnp.arange(L)[None, :]
        dist = i - j
        masked = (dist < 0) | (dist >= WINDOW)
        scores = jnp.where(masked[None, None, :, :], NEG_INF, scores)
        attn = jax.nn.softmax(scores, axis=-1)
        out = jnp.einsum('bhqk,bhkd->bhqd', attn, v)
        out = out.transpose(0, 2, 1, 3).reshape(B, L, D)
        return out @ Wo.T

    def _L2_ffn_ref(hidden_states, router_w, w_gate, w_up, w_down, ws_gate_up, ws_down):
        import jax, jax.numpy as jnp
        import numpy as np
        B, S, D = (1, 512, 256)
        E, K, F = (64, 8, 192)
        SF = 192
        C = 128
        ROUTED_SCALE = 1.0

        def _moe_forward(x, router_w, w_gate, w_up, w_down, ws_gate_up, ws_down):
            T = x.shape[0]
            logits = x.astype(jnp.float32) @ router_w.T
            probs = jax.nn.softmax(logits, axis=-1)
            topk_w, topk_ids = jax.lax.top_k(probs, K)
            topk_w = topk_w / jnp.sum(topk_w, axis=-1, keepdims=True)
            topk_w = topk_w.astype(x.dtype)
            N = T * K
            flat_e = topk_ids.reshape(-1)
            flat_w = topk_w.reshape(-1)
            tok = jnp.arange(N) // K
            onehot = flat_e[:, None] == jnp.arange(E)[None, :]
            pos = jnp.cumsum(onehot, axis=0)[jnp.arange(N), flat_e] - 1
            valid = pos < C
            idx = jnp.where(valid, flat_e * C + pos, E * C)
            x_buf = jnp.zeros((E * C + 1, x.shape[1]), x.dtype).at[idx].set(x[tok])
            xb = x_buf[:E * C].reshape(E, C, -1)
            g = jnp.einsum('ecd,edf->ecf', xb, w_gate)
            u = jnp.einsum('ecd,edf->ecf', xb, w_up)
            h = jax.nn.silu(g) * u
            y = jnp.einsum('ecf,efd->ecd', h, w_down).reshape(E * C, -1)
            safe = jnp.where(valid, idx, 0)
            contrib = y[safe] * (flat_w * valid.astype(flat_w.dtype))[:, None]
            routed = jax.ops.segment_sum(contrib, tok, num_segments=T)
            routed = routed * ROUTED_SCALE
            gu = x @ ws_gate_up
            sg, su = (gu[:, :SF], gu[:, SF:])
            shared = jax.nn.silu(sg) * su @ ws_down
            return routed + shared
        b, s, d = hidden_states.shape
        x = hidden_states.reshape(-1, d)
        out = _moe_forward(x, router_w, w_gate, w_up, w_down, ws_gate_up, ws_down)
        return out.reshape(b, s, d)

    def _L3_xattn_ref(x, y, wq, bq, wk, bk, wv, bv, wo, bo):
        import jax, jax.numpy as jnp
        import numpy as np
        N_HEADS = 16
        D_EMBED = 256
        D_CROSS = 192
        D_HEAD = D_EMBED // N_HEADS
        B, SQ, _ = x.shape
        SKV = y.shape[1]
        q = (x @ wq + bq).reshape(B, SQ, N_HEADS, D_HEAD)
        k = (y @ wk + bk).reshape(B, SKV, N_HEADS, D_HEAD)
        v = (y @ wv + bv).reshape(B, SKV, N_HEADS, D_HEAD)
        scores = jnp.einsum('bqhd,bkhd->bhqk', q, k) / jnp.sqrt(jnp.asarray(D_HEAD, x.dtype))
        attn = jax.nn.softmax(scores, axis=-1)
        out = jnp.einsum('bhqk,bkhd->bqhd', attn, v).reshape(B, SQ, D_EMBED)
        return out @ wo + bo

    def _L3_attn_ref(x, W_qkv, b_qkv, W_out, b_out, rel_bias):
        import jax, jax.numpy as jnp
        import numpy as np
        D_MODEL = 256
        NHEAD = 16
        D_K = D_MODEL // NHEAD
        MAX_REL = 256
        B, S, D = x.shape
        qkv = x @ W_qkv + b_qkv
        qkv = qkv.reshape(B, S, 3, NHEAD, D_K)
        q, k, v = (qkv[:, :, 0], qkv[:, :, 1], qkv[:, :, 2])
        scores = jnp.einsum('bihd,bjhd->bhij', q, k) / jnp.sqrt(jnp.float32(D_K))
        idxs = jnp.arange(S)
        rel = jnp.clip(idxs[:, None] - idxs[None, :] + MAX_REL, 0, 2 * MAX_REL)
        bias = rel_bias[rel]
        scores = scores + jnp.transpose(bias, (2, 0, 1))[None]
        attn = jax.nn.softmax(scores, axis=-1)
        out = jnp.einsum('bhij,bjhd->bihd', attn, v).reshape(B, S, D)
        return out @ W_out + b_out

    def _L3_ffn_ref(x, w1, b1, w2, b2, centroids, w_route):
        import jax, jax.numpy as jnp
        import numpy as np
        D_MODEL = 256
        D_FF = 1024
        N_EXPERTS = 8
        D_EXPERT = D_FF // N_EXPERTS
        TOP_K = 2
        LB_WEIGHT = 0.01
        B, S = (4, 512)

        def _top_k_softmax(logits, k):
            vals, _ = jax.lax.top_k(logits, k)
            thresh = vals[..., -1:]
            masked = jnp.where(logits >= thresh, logits, -jnp.inf)
            return jax.nn.softmax(masked, axis=-1)
        eps = 1e-12
        x_norm = x / jnp.maximum(jnp.linalg.norm(x, axis=-1, keepdims=True), eps)
        c_norm = centroids / jnp.maximum(jnp.linalg.norm(centroids, axis=-1, keepdims=True), eps)
        cos_scores = jnp.einsum('bsd,ed->bse', x_norm, c_norm)
        route_scores = jnp.einsum('bsd,ed->bse', x, w_route)
        logits = cos_scores + route_scores
        gates = _top_k_softmax(logits, TOP_K)
        h = jax.nn.gelu(jnp.einsum('bsd,edh->bseh', x, w1) + b1, approximate=False)
        expert_out = jnp.einsum('bseh,ehd->bsed', h, w2) + b2
        out = jnp.einsum('bse,bsed->bsd', gates, expert_out)
        return out
    x = x + _L0_xattn_ref(_layernorm(x, axis=-1), ctx_768, mask_BxS2_bk0, L0_xattn_W_q, L0_xattn_W_k, L0_xattn_W_v, L0_xattn_W_o, L0_xattn_b_o)
    x = x + _L0_attn_ref(_layernorm(x, axis=-1), L0_attn_Wq, L0_attn_bq, L0_attn_Wk, L0_attn_bk, L0_attn_Wv, L0_attn_bv, L0_attn_Wo, L0_attn_bo)
    x = x + _L0_ffn_ref(_layernorm(x, axis=-1), L0_ffn_router_w, L0_ffn_gate_w, L0_ffn_up_w, L0_ffn_down_w, L0_ffn_shared_gate_w, L0_ffn_shared_up_w, L0_ffn_shared_down_w)
    x = x + _L1_xattn_ref(_layernorm(x, axis=-1), ctx_768, L1_xattn_w_q, L1_xattn_w_kv, L1_xattn_w_out, L1_xattn_b_out)
    x = x + _L1_attn_ref(_layernorm(x, axis=-1), L1_attn_Wq, L1_attn_bq, L1_attn_Wk, L1_attn_bk, L1_attn_Wv, L1_attn_bv, L1_attn_Wo, L1_attn_bo)
    x = x + _L1_ffn_ref(_layernorm(x, axis=-1), L1_ffn_router_w, L1_ffn_expert_weights)
    x = x + _L2_xattn_ref(_layernorm(x, axis=-1), ctx_768, L2_xattn_Wq, L2_xattn_bq, L2_xattn_Wk, L2_xattn_bk, L2_xattn_Wv, L2_xattn_bv, L2_xattn_Wo, L2_xattn_bo)
    x = x + _L2_attn_ref(_layernorm(x, axis=-1), L2_attn_Wq, L2_attn_Wk, L2_attn_Wv, L2_attn_Wo, L2_attn_sep_gate, L2_attn_align_gate, L2_attn_coh_gate)
    x = x + _L2_ffn_ref(_layernorm(x, axis=-1), L2_ffn_router_w, L2_ffn_w_gate, L2_ffn_w_up, L2_ffn_w_down, L2_ffn_ws_gate_up, L2_ffn_ws_down)
    x = x + _L3_xattn_ref(_layernorm(x, axis=-1), ctx_768, L3_xattn_wq, L3_xattn_bq, L3_xattn_wk, L3_xattn_bk, L3_xattn_wv, L3_xattn_bv, L3_xattn_wo, L3_xattn_bo)
    x = x + _L3_attn_ref(_layernorm(x, axis=-1), L3_attn_W_qkv, L3_attn_b_qkv, L3_attn_W_out, L3_attn_b_out, L3_attn_rel_bias)
    x = x + _L3_ffn_ref(_layernorm(x, axis=-1), L3_ffn_w1, L3_ffn_b1, L3_ffn_w2, L3_ffn_b2, L3_ffn_centroids, L3_ffn_w_route)
    return x

_drawn_inputs = setup_inputs


def setup_inputs(seed=0):
    import zlib

    import numpy as np

    out = dict(_drawn_inputs(seed))
    spreads = {'L2_xattn_bq': (0.0, 2.0),
     'L2_xattn_bk': (0.0, 2.0),
     'L2_xattn_bv': (0.0, 0.435),
     'L2_xattn_bo': (0.0, 0.456),
     'L3_xattn_bq': (0.0, 2.0),
     'L3_xattn_bk': (0.0, 2.0),
     'L3_xattn_bv': (0.0, 0.8),
     'L3_xattn_bo': (0.0, 0.8),
     'L3_attn_b_qkv': (0.0, 0.8),
     'L3_attn_b_out': (0.0, 0.8),
     'L3_ffn_b1': (0.0, 2.0),
     'L3_ffn_b2': (0.0, 1.647)}
    factors = {'L0_xattn_b_o': 5.891,
     'L0_attn_Wq': 8.0,
     'L0_attn_bq': 8.0,
     'L0_attn_Wk': 8.0,
     'L0_attn_bk': 200.0,
     'L0_attn_bv': 8.0,
     'L0_ffn_router_w': 8.0,
     'L0_ffn_gate_w': 8.0,
     'L0_ffn_up_w': 8.0,
     'L0_ffn_down_w': 8.0,
     'L1_xattn_b_out': 22.459,
     'L1_attn_bq': 28.346,
     'L1_attn_bk': 200.0,
     'L1_attn_bv': 31.1,
     'L1_attn_bo': 29.847,
     'L2_attn_Wq': 33.188,
     'L2_attn_Wk': 30.151,
     'L2_ffn_router_w': 8.0,
     'L2_ffn_w_gate': 8.0,
     'L2_ffn_w_up': 8.0,
     'L2_ffn_w_down': 8.0,
     'L2_ffn_ws_gate_up': 8.0,
     'L2_ffn_ws_down': 8.0,
     'L3_attn_rel_bias': 64.0,
     'L0_ffn_shared_gate_w': 8.0,
     'L0_ffn_shared_up_w': 8.0,
     'L0_ffn_shared_down_w': 8.0,
     'L2_attn_Wv': 3.74,
     'L2_attn_Wo': 3.702,
     'L3_xattn_wq': 3.679,
     'L3_xattn_wk': 3.214,
     'L3_attn_W_qkv': 3.936,
     'L3_attn_W_out': 3.555,
     'L3_ffn_centroids': 42.606,
     'L3_ffn_w1': 2.862}
    for name, (base, spread) in spreads.items():
        noise = np.random.default_rng([zlib.crc32(name.encode()), seed]).standard_normal(out[name].shape)
        drawn = base * np.exp(spread * noise) if base else spread * noise
        out[name] = jnp.asarray(drawn.astype(out[name].dtype))
    for name, factor in factors.items():
        out[name] = (out[name] * factor).astype(out[name].dtype)
    return out
```

```python
from contextlib import ExitStack

import concourse.bass as bass
from concourse import mybir

ALU = mybir.AluOpType
ACT = mybir.ActivationFunctionType
AX_X = mybir.AxisListType.X
F32 = mybir.dt.float32
BF16 = mybir.dt.bfloat16
U8 = mybir.dt.uint8
U32 = mybir.dt.uint32
RMAX = bass.bass_isa.ReduceOp.max

P = 128
D = 256
DC = D // P
C = 192
CB = C - P
KEYS = 12544
TILES = KEYS // P
G = 7
GROUPS = TILES // G
BODY = 2 * G
ITERS = GROUPS // 2
HG = 8
QC = HG * P
BANK = 512

S_A, S_D, S_B, S_C, S_R, S_ONE, S_L = 0, 128, 256, 384, 512, 704, 706
S_W = S_L + C
S_P1 = 256
BIAS_HI, BIAS_LO = 64, 96

NEG = -1.7e38
NEG_ATTN = -1e30
CLAMP = 10000.0
MAX_REL = 256
EPS = 1e-5
RING = 4

XH = [8, 16, 16, 16]
XD = [64, 64, 16, 16]
SWEEPS = [h // HG for h in XH]
SWEEP0 = [sum(SWEEPS[:i]) for i in range(4)]
AH = [8, 2, 16, 16]
AD = [32, 128, 16, 16]
AS = [8, 1, 16, 16]
ASCALE = [32 ** -0.5, 0.25, 0.25, 0.25]
NE = [10, 16, 65, 8]
NE0 = [sum(NE[:i]) for i in range(5)]
FW = [256, 0, 192, 0]
LAYERS = 4


def sweep_loop(eng, body, peel_first, peel_last):
    lo, hi = int(peel_first), ITERS - int(peel_last)
    for it in range(lo):
        body(it)
    with eng.Fori(lo, hi) as it:
        body(it)
    for it in range(hi, ITERS):
        body(it)


def wait_count(eng, sem, count):
    if isinstance(count, int) and count <= 0:
        return
    eng.wait_ge(sem, count)


def build(nc, io, out, stages=12):
    with ExitStack() as ctx:
        def sb(name, shape, dt=F32):
            return ctx.enter_context(nc.sbuf_tensor(name, shape, dt))

        named = {}

        def sem(name):
            if name not in named:
                named[name] = ctx.enter_context(nc.semaphore(name))
            return named[name]

        ps = ctx.enter_context(nc.psum_tensor("ps", [P, 8, BANK], F32))
        psf = ps[:].rearrange("p b n -> p (b n)")

        def bank(b, n=1):
            return psf[:, b * BANK:(b + n) * BANK]

        stream = nc.dram_tensor("ctx_stream", [GROUPS, P, G, S_W], BF16, kind="Internal").ap()

        ident = sb("ident", [P, P])
        ones = sb("ones", [P, P])
        zrow = sb("zrow", [P, BANK], BF16)
        win_block = sb("win_block", [P, P])
        win_causal = sb("win_causal", [P, P])
        win_band = sb("win_band", [P, P])
        windows = [win_block, win_causal, win_band]
        x = sb("x_res", [P, D])
        xn = sb("xn", [P, D])
        xnT = sb("xnT", [P, DC, P])
        stats = sb("stats", [P, 6])
        mv = sb("mv", [P, 2])
        rstd = sb("rstd", [P, 1])
        o_rows = sb("o_rows", [P, 16, C])
        ctx_in = o_rows[:].rearrange("p h c -> p (h c)")[:, 0:2 * G * C].rearrange("p (b g c) -> p b g c", b=2, g=G)
        sbuf2 = sb("stream_buf", [P, 2, G, S_W], BF16)
        sbuf1 = sb("stream_buf_max", [P, 2, G, S_P1], BF16)
        keep_u8 = sb("keep_u8", [P, TILES], U8)
        keep = sb("keep", [P, TILES])
        maskneg = sb("maskneg", [P, TILES])
        any_keep = sb("any_keep", [P, 1])
        alive = sb("alive", [P, 1])
        qscale0 = sb("qscale0", [P, 1])
        ctx_mean = sb("ctx_mean", [P, C])
        xwq = sb("xwq", [P, DC, 1024])
        xwk = sb("xwk", [64, 16, C + 1])
        xwva = sb("xwva", [P, 1024])
        xwvb = sb("xwvb", [CB, 1024])
        xwo = sb("xwo", [64, 16, D])
        xbq = sb("xbq", [16, 2, 16])
        xbv = sb("xbv", [16, 2, 16])
        bo_all = sb("bo_all", [P, 8, D])
        qT = sb("qT", [64, 16, P])
        qf_a = sb("qf_a", [P, QC])
        qf_b = sb("qf_b", [P, QC])
        qh_a = sb("qh_a", [P, QC], BF16)
        ql_a = sb("ql_a", [P, QC], BF16)
        q_bb = sb("q_bb", [P, QC], BF16)
        q_d1 = sb("q_d1", [P, QC], BF16)
        q_d2 = sb("q_d2", [P, QC], BF16)
        runmax = sb("runmax", [P, 2, QC])
        maxall = sb("maxall", [P, QC])
        p32 = sb("p32", [P, 2, QC])
        phi = sb("phi", [P, 2, QC], BF16)
        plo = sb("plo", [P, 2, QC], BF16)
        clip = sb("clip", [P, 2, QC])
        den = sb("den", [P, 16])
        rden = sb("rden", [P, 16])
        nanf = sb("nanf", [P, 16])
        nan1 = sb("nan1", [P, 1])
        nana = sb("nana", [P, 1])
        oT_a = qf_a[:].rearrange("p (b n) -> p b n", b=2)
        oT_b = qf_b[0:CB, :].rearrange("p (b n) -> p b n", b=2)
        avT = maxall[0:64, :].rearrange("p (b n) -> p b n", b=2)
        aw = sb("aw", [P, DC, 4 * D])
        abq = sb("abq", [P, 4, 16])
        abk = sb("abk", [P, 4, 16])
        abv = sb("abv", [P, 4, D])
        gates = sb("gates", [P, 3])
        ngates = sb("ngates", [P, 3])
        rel = o_rows[:].rearrange("p h c -> p (h c)")[:, 0:16 * P].rearrange("p (h n) -> p h n", h=16)
        a_m = sb("a_m", [P, 16])
        a_s = sb("a_s", [P, 16])
        a_v = qh_a[:].bitcast(F32)[:, 0:D]
        a_o = ql_a[:].bitcast(F32)[:, 0:D]
        a_oT = q_bb[:].bitcast(F32)[:, 0:D].rearrange("p (c n) -> p c n", c=DC)
        xnT_rev = q_bb[:].bitcast(F32)[:, D:2 * D].rearrange("p (c n) -> p c n", c=DC)
        qk_buf = sbuf2[:].rearrange("p a g w -> p (a g w)").bitcast(F32)
        a_q = qk_buf[:, 0:2048]
        a_k = qk_buf[:, 2048:4096]
        a_S = p32[:].rearrange("p a n -> p (a n)")
        a_T = clip[:].rearrange("p a n -> p (a n)")
        a_U = runmax[:].rearrange("p a n -> p (a n)")
        ring = sb("ring", [P, RING, 1536])
        rw = sb("rw", [P, LAYERS, DC, 64])
        logit = sb("logit", [P, 64])
        prob = sb("prob", [P, 72])
        probr = sb("probr", [P, 72])
        top8 = sb("top8", [P, 8])
        rmax = sb("rmax", [P, 1])
        rsum = sb("rsum", [P, 1])
        rinv = sb("rinv", [P, 1])
        comb = sb("comb", [P, 66])
        g_s = phi[:, 0].bitcast(F32).rearrange("p (b n) -> p b n", b=2)
        h_s = phi[:, 1].bitcast(F32).rearrange("p (b n) -> p b n", b=2)
        hT = plo[:, 0].bitcast(F32).rearrange("p (b n) -> p b n", b=2)
        y_acc = plo[:, 1].bitcast(F32).rearrange("p (b n) -> p b n", b=2)
        xsq = g_s[:, 0, :]
        b1T = sb("b1T", [P, 8])
        b2r = sb("b2r", [8, D])
        csq = sb("csq", [P, DC, 8])
        cnorm = sb("cnorm", [P, 8])
        gT = qT[0:8, 0, :]

        in_landed = [sem("ctx_in_landed0"), sem("ctx_in_landed1")]
        stream_out = [sem("stream_written0"), sem("stream_written1")]
        p1_landed = [sem("max_stream_landed0"), sem("max_stream_landed1")]
        p2_landed = [sem("stream_landed0"), sem("stream_landed1")]
        ring_landed = [sem(f"ring_landed{i}") for i in range(RING)]
        xw_landed = sem("xattn_weights_landed")
        aw_landed = sem("attn_weights_landed")
        const_landed = sem("consts_landed")
        XW_DMAS = [5, 5, 5, 5]
        AW_DMAS = [4, 4, 4, 4]
        xw_at = [16 * sum(XW_DMAS[:i + 1]) for i in range(4)]
        aw_at = [16 * sum(AW_DMAS[:i + 1]) for i in range(4)]
        const_count = [0]

        block = ctx.enter_context(nc.Block())

        def plain_wait(eng, s, count):
            if isinstance(count, int):
                if count > 0:
                    eng.wait_ge(s, count)
                return
            count = eng.snap(count)
            eng.wait_ge(s, count)
            eng.sem_inc(sem("waits_passed"), 1)
        ctx_rows = io["ctx"].rearrange("(p t) c -> p t c", t=TILES)
        layers = (stages + 2) // 3

        def has(kind, layer):
            return 3 * layer + kind < stages

        consts = [
            (x[:], io["x"]),
            (keep_u8[:], io["mask"].rearrange("(p t) -> p t", t=TILES)),
        ]
        for i, n in enumerate(["L0_xattn_b_o", "L1_xattn_b_out", "L2_xattn_bo", "L3_xattn_bo"]):
            consts.append((bo_all[:, i, :], io[n].partition_broadcast(P)))
        for i, n in enumerate(["L0_attn_bo", "L1_attn_bo", None, "L3_attn_b_out"]):
            if n:
                consts.append((bo_all[:, 4 + i, :], io[n].partition_broadcast(P)))
        for i, n in enumerate(["L2_xattn", "L3_xattn"]):
            consts.append((xbq[:, i, :], io[n + "_bqT"]))
            consts.append((xbv[:, i, :], io[n + "_bvT"]))
        for i in (0, 1, 3):
            consts.append((abq[0:AD[i], i, 0:AH[i]], io[f"a{i}_bqT"]))
            consts.append((abk[0:AD[i], i, 0:AH[i]], io[f"a{i}_bkT"]))
            consts.append((abv[:, i, :], io[f"a{i}_bv"].partition_broadcast(P)))
        for i, n in enumerate(["sep", "align", "coh"]):
            consts.append((gates[:, i:i + 1], io[f"L2_attn_{n}_gate"].partition_broadcast(P)))
        for i, (n, e) in enumerate([("L0_ffn_router_w", 8), ("L1_ffn_router_wT", 32), ("L2_ffn_router_wT", 64)]):
            consts.append((rw[:, i, :, 0:e], io[n].rearrange("(c p) e -> p c e", p=P)))
        consts.append((rw[:, 3, :, 0:8], io["L3_ffn_centroidsT"].rearrange("(c p) e -> p c e", p=P)))
        consts.append((rw[:, 3, :, 8:16], io["L3_ffn_w_routeT"].rearrange("(c p) e -> p c e", p=P)))
        consts.append((b1T[:], io["L3_ffn_b1T"]))
        consts.append((b2r[:], io["L3_ffn_b2"]))
        relT = io["L3_attn_rel_biasT"]
        rel_loads = [(rel, bass.AP(relT.tensor, MAX_REL - P + 1, [[1, P], [2 * MAX_REL + 1, 16], [1, P]]))]
        CONSTS_ALL = 16 * len(consts)
        EARLY = 2

        def load_xw(sp, L):
            h, d = XH[L], XD[L]
            inner = h * d
            sp.dma_start(xwq[:, :, 0:inner], io[f"x{L}_wq"].rearrange("(c p) n -> p c n", p=P)).then_inc(xw_landed, 16)
            sp.dma_start(xwk[0:d, 0:h, :], io[f"x{L}_wkT"]).then_inc(xw_landed, 16)
            sp.dma_start(xwva[:, 0:inner], io[f"x{L}_wv"][0:P, :]).then_inc(xw_landed, 16)
            sp.dma_start(xwvb[:, 0:inner], io[f"x{L}_wv"][P:C, :]).then_inc(xw_landed, 16)
            sp.dma_start(xwo[0:d, 0:h, :], io[f"x{L}_wo"].rearrange("(h d) n -> d h n", d=d)).then_inc(xw_landed, 16)

        def load_aw(sp, L):
            for j, n in enumerate("qkvo"):
                sp.dma_start(aw[:, :, j * D:(j + 1) * D],
                             io[f"a{L}_w{n}"].rearrange("(c p) n -> p c n", p=P)).then_inc(aw_landed, 16)

        def ring_parts(L, e):
            if L == 0:
                f = FW[0]
                if e < 8:
                    g, u, d = io["L0_ffn_gate_w"][e], io["L0_ffn_up_w"][e], io["L0_ffn_down_w"][e]
                else:
                    o = (e - 8) * f
                    g, u = io["L0_ffn_shared_gate_w"][:, o:o + f], io["L0_ffn_shared_up_w"][:, o:o + f]
                    d = io["L0_ffn_shared_down_w"][o:o + f, :]
                return g, u, d
            if L == 2:
                return (io["L2_ffn_w_gate"][e], io["L2_ffn_w_up"][e], io["L2_ffn_w_down"][e])

        def gu_view(slot, f):
            return ring[:, slot, 0:2 * DC * f].rearrange("p (c n) -> p c n", c=DC)

        def dn_view(slot, f):
            return ring[0:f // 2, slot, 1024:1024 + 2 * D].rearrange("p (c n) -> p c n", c=2)

        RING_DMAS = [3, 2, 3, 2]

        def ring_slot_at(L, e):
            return (NE0[L] + e) % RING

        def landed_before(slot, L):
            n = 0
            for l in range(L):
                n += 16 * RING_DMAS[l] * len([e for e in range(NE[l]) if (NE0[l] + e) % RING == slot])
            return n

        def landed_at(L, e):
            slot = (NE0[L] + e) % RING
            k = len([i for i in range(e + 1) if (NE0[L] + i) % RING == slot])
            return landed_before(slot, L) + 16 * RING_DMAS[L] * k

        def load_ring(sp, L, e):
            n = NE0[L] + e
            slot = n % RING
            wait_count(sp, sem("ring_used"), n - RING + 1)
            s = ring_landed[slot]
            if L in (0, 2):
                f = FW[L]
                if L == 2 and e == 64:
                    gu = io["L2_ffn_ws_gate_up"]
                    g, u, d = gu[:, 0:f], gu[:, f:2 * f], io["L2_ffn_ws_down"]
                else:
                    g, u, d = ring_parts(L, e)
                v = gu_view(slot, f)
                sp.dma_start(v[:, :, 0:f], g.rearrange("(c p) n -> p c n", p=P)).then_inc(s, 16)
                sp.dma_start(v[:, :, f:2 * f], u.rearrange("(c p) n -> p c n", p=P)).then_inc(s, 16)
                sp.dma_start(dn_view(slot, f), d.rearrange("(c p) n -> p c n", p=f // 2)).then_inc(s, 16)
            elif L == 1:
                v = gu_view(slot, 256)
                for j in range(2):
                    sp.dma_start(v[:, :, j * D:(j + 1) * D],
                                 io["L1_ffn_expert_weights"][2 * e + j].rearrange("(c p) n -> p c n", p=P)
                                 ).then_inc(s, 16)
            else:
                sp.dma_start(ring[:, slot, 0:DC * P].rearrange("p (c n) -> p c n", c=DC),
                             io["L3_ffn_w1"][e].rearrange("(c p) n -> p c n", p=P)).then_inc(s, 16)
                sp.dma_start(ring[:, slot, 1024:1024 + D], io["L3_ffn_w2"][e]).then_inc(s, 16)

        def load_ring2_loop(sp):
            with sp.Fori(1, 16) as it:
                for j in range(RING):
                    slot = (NE0[2] + j) % RING
                    s = ring_landed[slot]
                    f = FW[2]
                    plain_wait(sp, sem("ring_used"), it * RING + (NE0[2] + j - RING + 1))
                    v = gu_view(slot, f)
                    e = it * RING + j
                    sp.dma_start(v[:, :, 0:f], io["L2_ffn_w_gate"][bass.ds(e, 1)].rearrange(
                        "o (c p) n -> p (o c) n", p=P)).then_inc(s, 16)
                    sp.dma_start(v[:, :, f:2 * f], io["L2_ffn_w_up"][bass.ds(e, 1)].rearrange(
                        "o (c p) n -> p (o c) n", p=P)).then_inc(s, 16)
                    sp.dma_start(dn_view(slot, f), io["L2_ffn_w_down"][bass.ds(e, 1)].rearrange(
                        "o (c p) n -> p (o c) n", p=f // 2)).then_inc(s, 16)

        @block.sync
        def _(sp):
            for d, s in consts[:EARLY]:
                sp.dma_start(d, s).then_inc(sem("early_landed"), 16)

            def ctx_load(g, b):
                sp.dma_start(ctx_in[:, b], ctx_rows[:, bass.ds(g * G, G), :]).then_inc(in_landed[b], 16)

            def ctx_store(it, b):
                plain_wait(sp, sem("dve_split"), it * 2 + b + 1)
                plain_wait(sp, sem("pool_split"), (it * 2 + b + 1) * 3)
                sp.dma_start(stream[bass.ds(it * 2 + b, 1)].rearrange("o p g w -> p (o g) w"),
                             sbuf2[:, b]).then_inc(stream_out[b], 16)
            ctx_load(0, 0)
            ctx_load(1, 1)
            load_xw(sp, 0)
            load_aw(sp, 0)
            for d, s in consts[EARLY:]:
                sp.dma_start(d, s).then_inc(const_landed, 16)
            for e in range(RING):
                load_ring(sp, 0, e)
            with sp.Fori(0, ITERS - 1) as it:
                for b in range(2):
                    ctx_store(it, b)
                    ctx_load(it * 2 + (2 + b), b)
            for b in range(2):
                ctx_store(ITERS - 1, b)
            for b in range(2):
                sp.wait_ge(stream_out[b], 16 * ITERS)

            for L in range(layers):
                for s in range(SWEEPS[L]):
                    n = SWEEP0[L] + s

                    def max_loads(it):
                        for b in range(2):
                            g = it * 2 + b
                            plain_wait(sp, sem("max_scores_ready"), it * BODY + (TILES * n + G * (b - 1)))
                            sp.dma_start(sbuf1[:, b], stream[bass.ds(g, 1), :, :, 0:S_P1].rearrange(
                                "o p g w -> p (o g) w")).then_inc(p1_landed[b], 16)

                    def pv_loads(it):
                        for b in range(2):
                            g = it * 2 + b
                            if isinstance(it, int) and it == 0 and s == 0 and L > 0:
                                sp.wait_ge(sem("attn_done"), L)
                            plain_wait(sp, sem("pv_done"), it * BODY + (TILES * n + G * (b - 1)))
                            sp.dma_start(sbuf2[:, b], stream[bass.ds(g, 1)].rearrange(
                                "o p g w -> p (o g) w")).then_inc(p2_landed[b], 16)
                    sweep_loop(sp, max_loads, n == 0, False)
                    sweep_loop(sp, pv_loads, s == 0, False)
                if L + 1 < layers:
                    sp.wait_ge(sem("xattn_done"), L + 1)
                    load_xw(sp, L + 1)
                if L == 3 and has(1, L):
                    sp.wait_ge(sem("xattn_done"), L + 1)
                    for d, s in rel_loads:
                        sp.dma_start(d, s).then_inc(sem("rel_landed"), 16)
                if has(1, L) and L + 1 < layers:
                    sp.wait_ge(sem("attn_done"), L + 1)
                    load_aw(sp, L + 1)
                if has(2, L):
                    if L == 2:
                        load_ring2_loop(sp)
                        load_ring(sp, 2, 64)
                    else:
                        for e in range(RING, NE[L]):
                            load_ring(sp, L, e)
                    if L + 1 < LAYERS and has(2, L + 1):
                        for e in range(RING):
                            load_ring(sp, L + 1, e)
            sp.wait_ge(sem("x_final"), 1)
            sp.dma_start(out, x[:]).then_inc(sem("out_written"), 16)
            sp.wait_ge(sem("out_written"), 16)

        @block.gpsimd
        def _(pool):
            g = nc.gpsimd
            chain = [0]

            def link(ins):
                chain[0] += 1
                ins.then_inc(sem("pool_chain"), 1)
                pool.wait_ge(sem("pool_chain"), chain[0])
            link(g.memset(ident[:], 0.0))
            link(g.affine_select(out=ident[:], in_=ident[:], compare_op=ALU.not_equal, fill=1.0, base=0,
                                 pattern=[[-1, P]], channel_multiplier=1))
            link(g.memset(ones[:], 1.0))
            link(g.memset(zrow[:], 0.0))
            link(g.memset(sbuf2[CB:P, :, :, S_D:S_D + P], 0.0))
            link(g.memset(sbuf2[BIAS_HI:BIAS_HI + 1, :, :, S_D:S_D + P], 1.0))
            link(g.memset(sbuf2[BIAS_LO:BIAS_LO + 1, :, :, S_D:S_D + P], 1.0))
            g.memset(sbuf2[:, :, :, S_ONE:S_ONE + 2], 1.0).then_inc(sem("consts_made"), 1)
            pool.wait_ge(sem("consts_made"), 1)

            pool.wait_ge(sem("keep_ready"), 1)
            link(g.partition_all_reduce(alive[:], any_keep[:], P, RMAX))
            g.memset(nan1[:], 0.0).then_inc(sem("alive_ready"), 1)
            pool.wait_ge(sem("alive_ready"), 1)

            def rows(it):
                for b in range(2):
                    n = it * 2 + b
                    plain_wait(pool, in_landed[b], (it + 1) * 16)
                    plain_wait(pool, stream_out[b], it * 16)
                    g.tensor_copy(sbuf2[:, b, :, S_R:S_R + C], ctx_in[:, b]).then_inc(sem("pool_split"), 1)
                    pool.wait_ge(sem("pool_split"), n * 3 + 1)
                    g.tensor_tensor(sbuf2[:, b, :, S_L:S_L + C], ctx_in[:, b], sbuf2[:, b, :, S_R:S_R + C],
                                    ALU.subtract).then_inc(sem("pool_split"), 1)
                    plain_wait(pool, sem("act_split"), (n + 1) * 2)
                    g.tensor_copy(sbuf2[0:CB, b, :, S_D:S_D + P], sbuf2[0:CB, b, :, S_B:S_B + P]
                                  ).then_inc(sem("pool_split"), 1)
            sweep_loop(pool, rows, True, False)

            H2 = P // 2
            for w in windows:
                link(g.memset(w[:], 0.0))
            for w in (win_causal, win_band):
                link(g.affine_select(out=w[:], in_=w[:], compare_op=ALU.is_ge, fill=NEG_ATTN, base=0,
                                     pattern=[[-1, P]], channel_multiplier=1))
            link(g.memset(win_block[0:H2, H2:P], NEG_ATTN))
            link(g.memset(win_block[H2:P, 0:H2], NEG_ATTN))
            link(g.memset(win_causal[H2:P, 0:H2], NEG_ATTN))
            g.affine_select(out=win_band[:], in_=win_band[:], compare_op=ALU.is_ge, fill=NEG_ATTN, base=H2 - 1,
                            pattern=[[1, P]], channel_multiplier=-1).then_inc(sem("windows_ready"), 1)
            pool.wait_ge(sem("windows_ready"), 1)

            for L in range(layers):
                for s in range(SWEEPS[L]):
                    n = SWEEP0[L] + s
                    pool.wait_ge(sem("max_merged"), n + 1)
                    g.partition_all_reduce(maxall[:], runmax[:, 0, :], P, RMAX).then_inc(sem("max_ready"), 1)
                    if L == 1 and s == 0:
                        pool.wait_ge(sem("max_ready"), n + 1)
                        pool.wait_ge(sem("attn_done"), 1)
                        link(g.memset(win_block[:], 0.0))
                        g.affine_select(out=win_block[:], in_=win_block[:], compare_op=ALU.not_equal, fill=1.0,
                                        base=1 - P, pattern=[[1, P]], channel_multiplier=1
                                        ).then_inc(sem("reversal_ready"), 1)
                        pool.wait_ge(sem("reversal_ready"), 1)
                    if L == 2:
                        pool.wait_ge(sem("max_ready"), n + 1)
                        base = TILES * s

                        def shift(it):
                            for k in range(BODY):
                                pool.wait_ge(sem("clipped"), it * BODY + (base + k + 1))
                                g.tensor_tensor(clip[:, k % 2], clip[:, k % 2], maxall[:],
                                                ALU.subtract).then_inc(sem("shifted"), 1)
                        sweep_loop(pool, shift, False, False)
                if L == 2:
                    pool.wait_ge(sem("nan_local"), 1)
                    g.partition_all_reduce(nana[:], nan1[:], P, RMAX).then_inc(sem("nan_ready"), 1)

        @block.tensor
        def _(pe):
            t = nc.tensor

            def turn_x(s):
                pe.wait_ge(sem("xn_ready"), s + 1)
                for c in range(DC):
                    m = t.transpose(bank(0)[:, c * P:(c + 1) * P], xn[:, c * P:(c + 1) * P], ident[:])
                m.then_inc(sem("xnT_psum"), 1)
                pe.wait_ge(sem("xnT_ready"), s + 1)

            pe.wait_ge(sem("consts_made"), 1)
            t.matmul(bank(4)[:, 0:C], zrow[:, 0:P], zrow[:, 0:C], start=True, stop=False, skip_group_check=True)

            def turn_ctx(it):
                for b in range(2):
                    n = it * 2 + b
                    pe.wait_ge(in_landed[b], (it + 1) * 16)
                    wait_count(pe, sem("dve_split"), n)
                    for k in range(G):
                        t.transpose(bank(0, 2)[:, k * P:(k + 1) * P], ctx_in[:, b, k, 0:P], ident[:])
                    for k in range(G):
                        t.transpose(bank(2, 2)[0:CB, k * P:(k + 1) * P], ctx_in[:, b, k, P:C], ident[:])
                    for k in range(G):
                        m = t.matmul(bank(4)[:, 0:C], ones[:], ctx_in[:, b, k, :], start=False,
                                     stop=False, skip_group_check=True)
                    m.then_inc(sem("ctxT_psum"), 1)
            sweep_loop(pe, turn_ctx, True, False)
            pe.wait_ge(sem("ctx_mean_ready"), 1)

            def xattn(L):
                h_n, d = XH[L], XD[L]
                s_at = 3 * L
                turn_x(s_at)
                pe.wait_ge(xw_landed, xw_at[L])
                quads = h_n // 4
                for q in range(quads):
                    for j in range(4):
                        h = 4 * q + j
                        for c in range(DC):
                            m = t.matmul(bank(q)[0:d, j * P:(j + 1) * P], xwq[:, c, h * d:(h + 1) * d],
                                         xnT[:, c, :], start=(c == 0), stop=(c == DC - 1))
                    m.then_inc(sem("qT_psum"), 1)
                for s in range(SWEEPS[L]):
                    n = SWEEP0[L] + s
                    pe.wait_ge(sem("qT_ready"), sum(XH[:L]) // 4 + quads)
                    for j in range(HG):
                        h = HG * s + j
                        t.matmul(bank(4, 2)[:, j * P:(j + 1) * P], xwk[0:d, h, 0:P], qT[0:d, h, :],
                                 start=True, stop=True)
                    for j in range(HG):
                        h = HG * s + j
                        m = t.matmul(bank(6, 2)[0:CB + 1, j * P:(j + 1) * P], xwk[0:d, h, P:C + 1],
                                     qT[0:d, h, :], start=True, stop=True)
                    m.then_inc(sem("qk_psum"), 1)
                    pe.wait_ge(sem("q_hi_ready"), n + 1)
                    base = TILES * n

                    def max_tiles(it):
                        for k in range(BODY):
                            b = k // G
                            if k % G == 0:
                                pe.wait_ge(p1_landed[b], it * 16 + 16 * (ITERS * n + 1))
                            wait_count(pe, sem("max_taken"), it * BODY + (base + k - 1))
                            sc = bank(4 + 2 * (k % 2), 2)
                            for c, rhs in enumerate((qh_a, q_d1)):
                                for m2 in range(2):
                                    m = t.matmul(sc[:, m2 * BANK:(m2 + 1) * BANK],
                                                 sbuf1[:, b, k % G, c * P:(c + 1) * P],
                                                 rhs[:, m2 * BANK:(m2 + 1) * BANK], start=(c == 0), stop=(c == 1))
                            m.then_inc(sem("max_scores_ready"), 1)
                    sweep_loop(pe, max_tiles, n == 0, False)

                    pe.wait_ge(sem("q_all_ready"), n + 1)
                    for b in range(4):
                        t.matmul(bank(b), zrow[:, 0:P], zrow[:], start=True, stop=False, skip_group_check=True)
                    freed = sem("clipped") if L == 2 else sem("p32_ready")
                    fbase = TILES * s if L == 2 else TILES * n - (TILES * SWEEPS[2] if L > 2 else 0)
                    fbase = TILES * s if L == 2 else TILES * n

                    def scores(it, k):
                        b = k // G
                        if k % G == 0:
                            pe.wait_ge(p2_landed[b], it * 16 + 16 * (ITERS * n + 1))
                        wait_count(pe, freed, it * BODY + (fbase + k - 1))
                        sc = bank(4 + 2 * (k % 2), 2)
                        v = sbuf2[:, b, k % G, :]
                        steps = [(S_A, qh_a), (S_A, ql_a), (S_C, qh_a), (S_B, q_bb), (S_D, q_d2)]
                        for i, (o, rhs) in enumerate(steps):
                            for m2 in range(2):
                                m = t.matmul(sc[:, m2 * BANK:(m2 + 1) * BANK], v[:, o:o + P],
                                             rhs[:, m2 * BANK:(m2 + 1) * BANK],
                                             start=(i == 0), stop=(i == len(steps) - 1))
                        m.then_inc(sem("scores_ready"), 1)

                    def pv(it, k):
                        b = k // G
                        pe.wait_ge(sem("p_ready"), it * BODY + (base + k + 1))
                        v = sbuf2[:, b, k % G, :]
                        for j in range(HG):
                            o = psf[:, j * 256:j * 256 + C + 1]
                            a = j * P
                            t.matmul(o, phi[:, k % 2, a:a + P], v[:, S_R:S_R + C + 1], start=False, stop=False,
                                     skip_group_check=True)
                            t.matmul(o[:, 0:C], phi[:, k % 2, a:a + P], v[:, S_L:S_L + C], start=False,
                                     stop=False, skip_group_check=True)
                            m = t.matmul(o, plo[:, k % 2, a:a + P], v[:, S_R:S_R + C + 1], start=False,
                                         stop=False, skip_group_check=True)
                        m.then_inc(sem("pv_done"), 1)

                    def pv_tiles(it):
                        last = isinstance(it, int) and it == ITERS - 1
                        for k in range(BODY):
                            if k < BODY - 1:
                                scores(it, k + 1)
                            elif not last:
                                scores(it + 1, 0)
                            pv(it, k)
                    scores(0, 0)
                    sweep_loop(pe, pv_tiles, n == 0 or (L == 2 and s == 0), True)
                    pe.wait_ge(sem("o_rows_ready"), n + 1)
                if L == 2:
                    pe.wait_ge(sem("guard_done"), 1)
                pe.wait_ge(xw_landed, xw_at[L])
                q0 = sum(XH[:L]) // 4

                def turn_o(q):
                    if q >= 2:
                        pe.wait_ge(sem("oTa_ready"), q0 + q - 1)
                        pe.wait_ge(sem("oTb_ready"), q0 + q - 1)
                    for j in range(4):
                        t.transpose(bank(4 + q % 2)[:, j * P:(j + 1) * P], o_rows[:, 4 * q + j, 0:P], ident[:])
                    for j in range(4):
                        m = t.transpose(bank(6 + q % 2)[0:CB, j * P:(j + 1) * P], o_rows[:, 4 * q + j, P:C],
                                        ident[:])
                    m.then_inc(sem("oT_psum"), 1)

                def values(q):
                    pe.wait_ge(sem("oTa_ready"), q0 + q + 1)
                    pe.wait_ge(sem("oTb_ready"), q0 + q + 1)
                    if q >= 2:
                        pe.wait_ge(sem("avT_ready"), q0 + q - 1)
                    for j in range(4):
                        h = 4 * q + j
                        o = bank(q % 2)[0:d, j * P:(j + 1) * P]
                        t.matmul(o, xwva[:, h * d:(h + 1) * d], oT_a[:, q % 2, j * P:(j + 1) * P],
                                 start=True, stop=False)
                        m = t.matmul(o, xwvb[:, h * d:(h + 1) * d], oT_b[:, q % 2, j * P:(j + 1) * P],
                                     start=False, stop=True)
                    m.then_inc(sem("avT_psum"), 1)

                def project(q):
                    pe.wait_ge(sem("avT_ready"), q0 + q + 1)
                    for j in range(4):
                        h = 4 * q + j
                        m = t.matmul(bank(2)[:, 0:D], avT[0:d, q % 2, j * P:(j + 1) * P], xwo[0:d, h, :],
                                     start=(h == 0), stop=(h == h_n - 1))
                    m.then_inc(sem("wo_used"), 1)
                turn_o(0)
                for q in range(quads):
                    if q + 1 < quads:
                        turn_o(q + 1)
                    values(q)
                    project(q)
                pe.wait_ge(sem("xattn_done"), L + 1)

            def attn(L):
                parts, d, heads = AH[L], AD[L], AS[L]
                turn_x(3 * L + 1)
                pe.wait_ge(aw_landed, aw_at[L])
                kv_in = xnT
                if L == 3:
                    pe.wait_ge(sem("reversal_ready"), 1)
                    for c in range(DC):
                        m = t.matmul(bank(1)[:, c * P:(c + 1) * P], xn[:, c * P:(c + 1) * P], win_block[:],
                                     start=True, stop=True)
                    m.then_inc(sem("xnT_rev_psum"), 1)
                    pe.wait_ge(sem("xnT_rev_ready"), 1)
                    kv_in = xnT_rev
                for w, first_bank in ((0, 0), (1, 4)):
                    for h in range(parts):
                        for c in range(DC):
                            m = t.matmul(bank(first_bank, 4)[0:d, h * P:(h + 1) * P],
                                         aw[:, c, w * D + h * d:w * D + (h + 1) * d], (kv_in if w else xnT)[:, c, :],
                                         start=(c == 0), stop=(c == DC - 1))
                    m.then_inc(sem("attn_qk_psum"), 1)
                pe.wait_ge(sem("attn_k_ready"), L + 1)
                for c in range(DC):
                    m = t.matmul(bank(7)[:, 0:D], kv_in[:, c, :], aw[:, c, 2 * D:3 * D], start=(c == 0),
                                 stop=(c == DC - 1))
                m.then_inc(sem("attn_v_psum"), 1)
                pe.wait_ge(sem("attn_q_ready"), L + 1)
                per = parts // heads
                for h in range(heads):
                    for c in range(per):
                        g = h * per + c
                        m = t.matmul(bank(0, 4)[:, h * P:(h + 1) * P], a_q[0:d, g * P:(g + 1) * P],
                                     a_k[0:d, g * P:(g + 1) * P], start=(c == 0), stop=(c == per - 1))
                m.then_inc(sem("attn_scores"), 1)
                pe.wait_ge(sem("attn_probs"), L + 1)
                for h in range(heads):
                    m = t.transpose(bank(0, 4)[:, h * P:(h + 1) * P], a_S[:, h * P:(h + 1) * P], ident[:])
                m.then_inc(sem("attn_pT_psum"), 1)
                pe.wait_ge(sem("attn_pT_ready"), L + 1)
                pe.wait_ge(sem("attn_v_ready"), L + 1)
                w = D // heads
                for h in range(heads):
                    m = t.matmul(bank(4)[:, h * w:(h + 1) * w], a_T[:, h * P:(h + 1) * P],
                                 a_v[:, h * w:(h + 1) * w], start=True, stop=True)
                m.then_inc(sem("attn_o_psum"), 1)
                pe.wait_ge(sem("attn_o_ready"), L + 1)
                for c in range(DC):
                    m = t.transpose(bank(5)[:, c * P:(c + 1) * P], a_o[:, c * P:(c + 1) * P], ident[:])
                m.then_inc(sem("attn_oT_psum"), 1)
                pe.wait_ge(sem("attn_oT_ready"), L + 1)
                for c in range(DC):
                    m = t.matmul(bank(6)[:, 0:D], a_oT[:, c, :], aw[:, c, 3 * D:4 * D], start=(c == 0),
                                 stop=(c == DC - 1))
                m.then_inc(sem("attn_out_psum"), 1)
                pe.wait_ge(sem("attn_done"), L + 1)

            def route(L, e):
                turn_x(3 * L + 2)
                if L == 0:
                    pe.wait_ge(const_landed, CONSTS_ALL - 16 * EARLY)
                for c in range(DC):
                    m = t.matmul(bank(1)[:, 0:e], xnT[:, c, :], rw[:, L, c, 0:e], start=(c == 0), stop=(c == DC - 1))
                m.then_inc(sem("logits_psum"), 1)

            def glu_experts(L, base):
                f = FW[L]
                fc = f // 2
                t.matmul(bank(2)[:, 0:D], zrow[:, 0:P], zrow[:, 0:D], start=True, stop=False,
                         skip_group_check=True)

                def gate_up(slot, landed, count, par, free):
                    pe.wait_ge(ring_landed[slot], landed)
                    wait_count(pe, sem("h_ready"), free)
                    v = gu_view(slot, f)
                    for half in range(2):
                        for c in range(DC):
                            m = t.matmul(bank(4 + 2 * par + half)[:, 0:f], xnT[:, c, :],
                                         v[:, c, half * f:(half + 1) * f], start=(c == 0), stop=(c == DC - 1))
                    m.then_inc(sem("gu_psum"), 1)

                def down(slot, par, h_at):
                    pe.wait_ge(sem("h_ready"), h_at)
                    for c in range(2):
                        m = t.transpose(bank(par)[0:fc, c * P:(c + 1) * P], h_s[:, par, c * fc:(c + 1) * fc],
                                        ident[:])
                    m.then_inc(sem("hT_psum"), 1)
                    pe.wait_ge(sem("hT_ready"), h_at)
                    dn = dn_view(slot, f)
                    for c in range(2):
                        m = t.matmul(bank(2)[:, 0:D], hT[0:fc, par, c * P:(c + 1) * P], dn[:, c, :],
                                     start=False, stop=False, skip_group_check=True)
                    m.then_inc(sem("ring_used"), 1)
                return gate_up, down

            GLU0 = [0, 0, NE[0], 0]

            def ffn_glu(L):
                route(L, 8 if L == 0 else 64)
                gate_up, down = glu_experts(L, GLU0[L])
                b0 = GLU0[L]
                n_e = NE[L]

                def slot_of(e):
                    return (NE0[L] + e) % RING
                if L == 0:
                    gate_up(slot_of(0), landed_at(L, 0), 0, 0, b0 - 1)
                    for e in range(n_e):
                        if e + 1 < n_e:
                            gate_up(slot_of(e + 1), landed_at(L, e + 1), 0, (e + 1) % 2, b0 + e)
                        down(slot_of(e), e % 2, b0 + e + 1)
                else:
                    step = 16 * RING_DMAS[L]
                    gate_up(slot_of(0), landed_at(L, 0), 0, 0, b0 - 1)
                    with pe.Fori(0, 16) as it:
                        for j in range(RING):
                            gate_up(slot_of(j + 1), it * step + landed_at(L, j + 1), 0, (j + 1) % 2,
                                    it * RING + (b0 + j))
                            down(slot_of(j), j % 2, it * RING + (b0 + j + 1))
                    down(slot_of(64), 0, b0 + 65)
                pe.wait_ge(sem("ffn_done"), L + 1)

            def ffn1():
                route(1, 32)
                for e in range(NE[1]):
                    pe.wait_ge(ring_landed[(NE0[1] + e) % RING], landed_at(1, e))
                    if e >= 2:
                        pe.wait_ge(sem("l1_step"), 2 * (e - 1))
                    v = gu_view((NE0[1] + e) % RING, 256)
                    for c in range(DC):
                        m = t.matmul(bank(4 + e % 2), xnT[:, c, :], v[:, c, :], start=(c == 0), stop=(c == DC - 1))
                    m.then_inc(sem("ring_used"), 1)
                pe.wait_ge(sem("ffn_done"), 2)

            def ffn3():
                pe.wait_ge(sem("csq_ready"), 1)
                for c in range(DC):
                    m = t.matmul(bank(3)[:, 0:8], ones[:], csq[:, c, :], start=(c == 0), stop=(c == DC - 1))
                m.then_inc(sem("cnorm_psum"), 1)
                route(3, 16)
                pe.wait_ge(sem("comb_ready"), 1)
                t.transpose(bank(2)[0:8, 0:P], comb[:, 0:8], ident[:]).then_inc(sem("gT_psum"), 1)
                pe.wait_ge(sem("gT_ready"), 1)
                t.matmul(bank(3)[:, 0:D], gT, b2r[:], start=True, stop=True).then_inc(sem("b2_psum"), 1)

                def up(e):
                    slot = (NE0[3] + e) % RING
                    pe.wait_ge(ring_landed[slot], landed_at(3, e))
                    if e >= 2:
                        pe.wait_ge(sem("gelu_ready"), e - 1)
                    w1 = ring[:, slot, 0:DC * P].rearrange("p (c n) -> p c n", c=DC)
                    for c in range(DC):
                        m = t.matmul(bank(4 + e % 2)[:, 0:P], w1[:, c, :], xnT[:, c, :], start=(c == 0),
                                     stop=(c == DC - 1))
                    m.then_inc(sem("w1_psum"), 1)

                def down(e):
                    slot = (NE0[3] + e) % RING
                    pe.wait_ge(sem("gelu_ready"), e + 1)
                    if e >= 2:
                        pe.wait_ge(sem("l3_taken"), e - 1)
                    t.matmul(bank(6 + e % 2)[:, 0:D], hT[:, e % 2, 0:P], ring[:, slot, 1024:1024 + D],
                             start=True, stop=True).then_inc(sem("ring_used"), 1)
                up(0)
                for e in range(8):
                    if e < 7:
                        up(e + 1)
                    down(e)

            for s in range(stages):
                L = s // 3
                if s % 3 == 0:
                    xattn(L)
                elif s % 3 == 1:
                    attn(L)
                elif L in (0, 2):
                    ffn_glu(L)
                elif L == 1:
                    ffn1()
                else:
                    ffn3()

        @block.scalar
        def _(act):
            a = nc.scalar

            def std(s):
                act.wait_ge(sem("var_ready"), s + 1)
                a.activation(rstd[:], rstd[:], ACT.Sqrt).then_inc(sem("std_ready"), 1)

            def split_ctx(it):
                for b in range(2):
                    n = it * 2 + b
                    act.wait_ge(sem("ctxT_psum"), n + 1)
                    wait_count(act, stream_out[b], it * 16)
                    a.activation(sbuf2[:, b, :, S_A:S_A + P],
                                 bank(0, 2)[:, 0:G * P].rearrange("p (g k) -> p g k", g=G), ACT.Copy
                                 ).then_inc(sem("act_split"), 1)
                    a.activation(sbuf2[0:CB, b, :, S_B:S_B + P],
                                 bank(2, 2)[0:CB, 0:G * P].rearrange("p (g k) -> p g k", g=G), ACT.Copy
                                 ).then_inc(sem("act_split"), 1)
            sweep_loop(act, split_ctx, True, False)

            def xattn(L):
                h_n, d = XH[L], XD[L]
                for s in range(SWEEPS[L]):
                    n = SWEEP0[L] + s
                    act.wait_ge(sem("qk_psum"), n + 1)
                    sc = d ** -0.5
                    if L == 0:
                        act.wait_ge(sem("qscale_ready"), 1)
                    a.activation(qf_a[:], bank(4, 2), ACT.Copy if L else ACT.Identity,
                                 scale=sc if L else qscale0[:, 0:1]).then_inc(sem("qf_ready"), 1)
                    a.activation(qf_b[0:CB + 1, :], bank(6, 2)[0:CB + 1, :], ACT.Copy if L else ACT.Identity,
                                 scale=sc if L else qscale0[0:CB + 1, 0:1]).then_inc(sem("qf_ready"), 1)
                    base = TILES * n

                    def exps(it):
                        for k in range(BODY):
                            if L == 2:
                                act.wait_ge(sem("shifted"), it * BODY + (TILES * s + k + 1))
                                src = clip[:, k % 2]
                            else:
                                act.wait_ge(sem("scores_ready"), it * BODY + (base + k + 1))
                                src = bank(4 + 2 * (k % 2), 2)
                            wait_count(act, sem("p_ready"), it * BODY + (base + k - 1))
                            bias = maskneg[:, bass.ds(it * BODY + k, 1)] if L == 0 else 0.0
                            a.activation(p32[:, k % 2], src, ACT.Exp, bias=bias).then_inc(sem("p32_ready"), 1)
                    sweep_loop(act, exps, n == 0, False)
                q0 = sum(XH[:L]) // 4
                for q in range(h_n // 4):
                    act.wait_ge(sem("oT_psum"), q0 + q + 1)
                    if q >= 2:
                        act.wait_ge(sem("avT_psum"), q0 + q - 1)
                    a.activation(oT_b[:, q % 2, :], bank(6 + q % 2)[0:CB, :], ACT.Copy).then_inc(sem("oTb_ready"), 1)

            def attn(L):
                n = AS[L] * P
                if L == 2:
                    act.wait_ge(sem("l2_scaled"), 1)
                    a.activation(a_T, a_S, ACT.Sigmoid).then_inc(sem("l2_act"), 1)
                    act.wait_ge(sem("l2_act"), 1)
                    a.activation(a_T, a_T, ACT.Square).then_inc(sem("l2_act"), 1)
                    act.wait_ge(sem("l2_centred"), 1)
                    a.activation(a_U, a_U, ACT.Abs).then_inc(sem("l2_act"), 1)
                act.wait_ge(sem("attn_shifted"), L + 1)
                a.activation(a_S[:, 0:n], a_S[:, 0:n], ACT.Exp).then_inc(sem("attn_probs"), 1)
                act.wait_ge(sem("attn_pT_psum"), L + 1)
                a.activation(a_T[:, 0:n], bank(0, 4)[:, 0:n], ACT.Copy).then_inc(sem("attn_pT_ready"), 1)

            def ffn_glu(L):
                f = FW[L]
                act.wait_ge(sem("route_shifted"), L + 1)
                a.activation(prob[:, 0:8 if L == 0 else 64], logit[:, 0:8 if L == 0 else 64], ACT.Exp
                             ).then_inc(sem("route_exp"), 1)
                b0 = 0 if L == 0 else NE[0]

                def one(par, at):
                    act.wait_ge(sem("gu_psum"), at)
                    wait_count(act, sem("h_ready"), at - 2)
                    a.activation(g_s[:, par, 0:f], bank(4 + 2 * par)[:, 0:f], ACT.Silu).then_inc(sem("silu"), 1)
                if L == 0:
                    for e in range(NE[0]):
                        one(e % 2, e + 1)
                else:
                    with act.Fori(0, 16) as it:
                        for j in range(RING):
                            one(j % 2, it * RING + (b0 + j + 1))
                    one(0, b0 + 65)

            def ffn1():
                act.wait_ge(sem("route_shifted"), 2)
                a.activation(prob[:, 0:32], logit[:, 0:32], ACT.Exp).then_inc(sem("route_exp"), 1)

            def ffn3():
                act.wait_ge(sem("cnorm_psum"), 1)
                a.activation(cnorm[:], bank(3)[:, 0:8], ACT.Sqrt).then_inc(sem("norms_ready"), 1)
                act.wait_ge(sem("xsq_ready"), 1)
                a.activation(rsum[:], rsum[:], ACT.Sqrt).then_inc(sem("norms_ready"), 1)
                act.wait_ge(sem("route_shifted"), 4)
                a.activation(prob[:, 0:8], logit[:, 0:8], ACT.Exp).then_inc(sem("route_exp"), 1)
                for e in range(8):
                    act.wait_ge(sem("w1_psum"), e + 1)
                    if e >= 2:
                        act.wait_ge(sem("ring_used"), NE0[3] + e - 1)
                    a.activation(hT[:, e % 2, 0:P], bank(4 + e % 2)[:, 0:P], ACT.Gelu, bias=b1T[:, e:e + 1]
                                 ).then_inc(sem("gelu_ready"), 1)

            for s in range(stages):
                L = s // 3
                std(s)
                if s % 3 == 0:
                    xattn(L)
                elif s % 3 == 1:
                    attn(L)
                elif L in (0, 2):
                    ffn_glu(L)
                elif L == 1:
                    ffn1()
                else:
                    ffn3()

        @block.vector
        def _(dve):
            v = nc.vector
            chain = [0]

            def link(ins):
                chain[0] += 1
                ins.then_inc(sem("dve_chain"), 1)
                dve.wait_ge(sem("dve_chain"), chain[0])

            def norm(s):
                link(v.bn_stats(stats[:], x[:]))
                link(v.bn_aggr(mv[:], stats[:]))
                v.tensor_scalar(rstd[:], mv[:, 1:2], EPS, None, ALU.add).then_inc(sem("var_ready"), 1)
                dve.wait_ge(sem("std_ready"), s + 1)
                link(v.reciprocal(rstd[:], rstd[:]))
                v.tensor_scalar(xn[:], x[:], mv[:, 0:1], rstd[:, 0:1], ALU.subtract, ALU.mult
                                ).then_inc(sem("xn_ready"), 1)
                dve.wait_ge(sem("xnT_psum"), s + 1)
                v.tensor_copy(xnT[:].rearrange("p c n -> p (c n)"), bank(0)[:, 0:D]).then_inc(sem("xnT_ready"), 1)
                dve.wait_ge(sem("xnT_ready"), s + 1)

            link(v.memset(q_d1[:], 0.0))
            link(v.memset(q_d2[:], 0.0))
            dve.wait_ge(sem("early_landed"), 16 * EARLY)
            link(v.tensor_copy(keep[:], keep_u8[:]))
            link(v.tensor_scalar(keep[:], keep[:], 0.0, None, ALU.is_gt))
            v.tensor_reduce(any_keep[:], keep[:], AX_X, ALU.max).then_inc(sem("keep_ready"), 1)
            dve.wait_ge(sem("alive_ready"), 1)
            v.tensor_scalar(qscale0[:], alive[:], XD[0] ** -0.5, None, ALU.mult).then_inc(sem("qscale_ready"), 1)
            link(v.tensor_scalar(maskneg[:], keep[:], -NEG, NEG, ALU.mult, ALU.add))
            link(v.tensor_scalar(maskneg[:], maskneg[:], alive[:, 0:1], None, ALU.mult))

            def split_ctx(it):
                for b in range(2):
                    n = it * 2 + b
                    dve.wait_ge(sem("act_split"), n * 2 + 1)
                    v.tensor_tensor(sbuf2[:, b, :, S_C:S_C + P],
                                    bank(0, 2)[:, 0:G * P].rearrange("p (g k) -> p g k", g=G),
                                    sbuf2[:, b, :, S_A:S_A + P], ALU.subtract)
                    dve.wait_ge(sem("act_split"), n * 2 + 2)
                    v.tensor_tensor(sbuf2[CB:P, b, :, S_B:S_B + P],
                                    bank(2, 2)[0:CB, 0:G * P].rearrange("p (g k) -> p g k", g=G),
                                    sbuf2[0:CB, b, :, S_B:S_B + P], ALU.subtract).then_inc(sem("dve_split"), 1)
            sweep_loop(dve, split_ctx, False, False)
            dve.wait_ge(sem("ctxT_psum"), GROUPS)
            v.tensor_scalar(ctx_mean[:], bank(4)[:, 0:C], 1.0 / KEYS, None, ALU.mult
                            ).then_inc(sem("ctx_mean_ready"), 1)
            dve.wait_ge(const_landed, CONSTS_ALL - 16 * EARLY)

            def xattn(L):
                h_n, d = XH[L], XD[L]
                quads = h_n // 4
                q0 = sum(XH[:L]) // 4
                norm(3 * L)
                for q in range(quads):
                    dve.wait_ge(sem("qT_psum"), q0 + q + 1)
                    o = qT[0:d, 4 * q:4 * q + 4, :]
                    i = bank(q)[0:d, :].rearrange("p (h n) -> p h n", h=4)
                    if L < 2:
                        v.tensor_copy(o, i).then_inc(sem("qT_ready"), 1)
                    else:
                        v.tensor_tensor(o, i, xbq[0:d, L - 2, 4 * q:4 * q + 4].unsqueeze(2).to_broadcast([d, 4, P]),
                                        ALU.add).then_inc(sem("qT_ready"), 1)
                for s in range(SWEEPS[L]):
                    n = SWEEP0[L] + s
                    base = TILES * n
                    dve.wait_ge(sem("qf_ready"), 2 * n + 1)
                    link(v.tensor_copy(qh_a[:], qf_a[:]))
                    v.tensor_tensor(ql_a[:], qf_a[:], qh_a[:], ALU.subtract)
                    dve.wait_ge(sem("qf_ready"), 2 * n + 2)
                    v.tensor_copy(q_bb[0:CB, :], qf_b[0:CB, :])
                    v.tensor_copy(q_bb[CB:P, :], qf_b[0:CB, :])
                    link(v.tensor_copy(q_d1[0:CB + 1, :], qf_b[0:CB + 1, :]))
                    v.tensor_tensor(q_d2[0:CB, :], qf_b[0:CB, :], q_d1[0:CB, :], ALU.subtract)
                    v.tensor_tensor(q_d1[BIAS_LO:BIAS_LO + 1, :], qf_b[BIAS_HI:BIAS_HI + 1, :],
                                    q_d1[BIAS_HI:BIAS_HI + 1, :], ALU.subtract).then_inc(sem("q_hi_ready"), 1)
                    link(v.memset(runmax[:], NEG))

                    def take_max(it):
                        for k in range(BODY):
                            dve.wait_ge(sem("max_scores_ready"), it * BODY + (base + k + 1))
                            wait_count(dve, sem("max_taken"), it * BODY + (base + k - 1))
                            if L == 0:
                                v.scalar_tensor_tensor(runmax[:, k % 2], bank(4 + 2 * (k % 2), 2),
                                                       maskneg[:, bass.ds(it * BODY + k, 1)], runmax[:, k % 2],
                                                       ALU.add, ALU.max).then_inc(sem("max_taken"), 1)
                            else:
                                v.tensor_tensor(runmax[:, k % 2], bank(4 + 2 * (k % 2), 2), runmax[:, k % 2],
                                                ALU.max).then_inc(sem("max_taken"), 1)
                    sweep_loop(dve, take_max, n == 0, False)
                    dve.wait_ge(sem("max_taken"), base + TILES)
                    if L == 2:
                        link(v.tensor_tensor(runmax[:, 0], runmax[:, 0], runmax[:, 1], ALU.max))
                        v.tensor_scalar(runmax[:, 0], runmax[:, 0], CLAMP, -CLAMP, ALU.min, ALU.max
                                        ).then_inc(sem("max_merged"), 1)
                        link(v.tensor_copy(q_d2[BIAS_HI:BIAS_HI + 1, :], q_d1[BIAS_HI:BIAS_HI + 1, :]))
                        v.tensor_copy(q_d2[BIAS_LO:BIAS_LO + 1, :], q_d1[BIAS_LO:BIAS_LO + 1, :]
                                      ).then_inc(sem("q_all_ready"), 1)
                    else:
                        v.tensor_tensor(runmax[:, 0], runmax[:, 0], runmax[:, 1], ALU.max
                                        ).then_inc(sem("max_merged"), 1)
                        dve.wait_ge(sem("max_ready"), n + 1)
                        hi = slice(BIAS_HI, BIAS_HI + 1)
                        link(v.tensor_tensor(qf_b[hi, :], qf_b[hi, :], maxall[hi, :], ALU.subtract))
                        link(v.tensor_copy(q_d2[hi, :], qf_b[hi, :]))
                        v.tensor_tensor(q_d2[BIAS_LO:BIAS_LO + 1, :], qf_b[hi, :], q_d2[hi, :],
                                        ALU.subtract).then_inc(sem("q_all_ready"), 1)

                    def split_p(it, k):
                        dve.wait_ge(sem("p32_ready"), it * BODY + (base + k + 1))
                        wait_count(dve, sem("pv_done"), it * BODY + (base + k - 1))
                        v.tensor_copy(phi[:, k % 2], p32[:, k % 2]).then_inc(sem("phi_ready"), 1)
                        dve.wait_ge(sem("phi_ready"), it * BODY + (base + k + 1))
                        v.tensor_tensor(plo[:, k % 2], p32[:, k % 2], phi[:, k % 2], ALU.subtract
                                        ).then_inc(sem("p_ready"), 1)

                    def clamp(it, k):
                        dve.wait_ge(sem("scores_ready"), it * BODY + (base + k + 1))
                        wait_count(dve, sem("p32_ready"), it * BODY + (base + k - 1))
                        v.tensor_scalar(clip[:, k % 2], bank(4 + 2 * (k % 2), 2), CLAMP, -CLAMP, ALU.min,
                                        ALU.max).then_inc(sem("clipped"), 1)

                    def p_tiles(it):
                        last = isinstance(it, int) and it == ITERS - 1
                        for k in range(BODY):
                            if L == 2 and k < BODY - 1:
                                clamp(it, k + 1)
                            elif L == 2 and not last:
                                clamp(it + 1, 0)
                            split_p(it, k)
                    if L == 2:
                        clamp(0, 0)
                    sweep_loop(dve, p_tiles, n == 0, L == 2)
                    dve.wait_ge(sem("pv_done"), base + TILES)
                    acc = bank(0, 4).rearrange("p (h n) -> p h n", h=HG)
                    dn = den[:, HG * s:HG * s + HG]
                    rd = rden[:, HG * s:HG * s + HG]
                    link(v.tensor_copy(dn, acc[:, :, C]))
                    link(v.reciprocal(rd, dn))
                    v.tensor_tensor(o_rows[:, HG * s:HG * s + HG, :], acc[:, :, 0:C],
                                    rd.unsqueeze(2).to_broadcast([P, HG, C]), ALU.mult
                                    ).then_inc(sem("o_rows_ready"), 1)
                if L == 2:
                    dve.wait_ge(sem("o_rows_ready"), SWEEP0[2] + 2)
                    link(v.tensor_tensor(nanf[:], den[:], den[:], ALU.not_equal))
                    v.tensor_reduce(nan1[:], nanf[:], AX_X, ALU.max).then_inc(sem("nan_local"), 1)
                    dve.wait_ge(sem("nan_ready"), 1)
                    for h in range(16):
                        g = v.copy_predicated(o_rows[:, h, :], nana[:, 0:1].bitcast(U32).to_broadcast([P, C]),
                                              ctx_mean[:])
                    g.then_inc(sem("guard_done"), 1)
                for q in range(quads):
                    dve.wait_ge(sem("oT_psum"), q0 + q + 1)
                    if q >= 2:
                        dve.wait_ge(sem("avT_psum"), q0 + q - 1)
                    v.tensor_copy(oT_a[:, q % 2, :], bank(4 + q % 2)).then_inc(sem("oTa_ready"), 1)
                    dve.wait_ge(sem("avT_psum"), q0 + q + 1)
                    if q >= 2:
                        dve.wait_ge(sem("wo_used"), q0 + q - 1)
                    if L < 2:
                        v.tensor_copy(avT[0:d, q % 2, :], bank(q % 2)[0:d, :]).then_inc(sem("avT_ready"), 1)
                    else:
                        v.tensor_tensor(avT[0:d, q % 2, :].rearrange("p (h n) -> p h n", h=4),
                                        bank(q % 2)[0:d, :].rearrange("p (h n) -> p h n", h=4),
                                        xbv[0:d, L - 2, 4 * q:4 * q + 4].unsqueeze(2).to_broadcast([d, 4, P]),
                                        ALU.add).then_inc(sem("avT_ready"), 1)
                link(v.tensor_tensor(x[:], x[:], bo_all[:, L, :], ALU.add))
                dve.wait_ge(sem("wo_used"), q0 + quads)
                v.tensor_tensor(x[:], bank(2)[:, 0:D], x[:], ALU.add).then_inc(sem("xattn_done"), 1)
                dve.wait_ge(sem("xattn_done"), L + 1)

            def attn(L):
                parts, d, heads = AH[L], AD[L], AS[L]
                n = heads * P
                norm(3 * L + 1)
                if L == 3:
                    dve.wait_ge(sem("xnT_rev_psum"), 1)
                    v.tensor_copy(xnT_rev.rearrange("p c n -> p (c n)"), bank(1)[:, 0:D]
                                  ).then_inc(sem("xnT_rev_ready"), 1)
                for w, (dst, bias, name) in enumerate(((a_q, abq, "attn_q_ready"), (a_k, abk, "attn_k_ready"))):
                    dve.wait_ge(sem("attn_qk_psum"), 2 * L + w + 1)
                    o = dst[0:d, 0:parts * P].rearrange("p (h n) -> p h n", h=parts)
                    i = bank(4 * w, 4)[0:d, 0:parts * P].rearrange("p (h n) -> p h n", h=parts)
                    if L == 2:
                        v.tensor_copy(o, i).then_inc(sem(name), 1)
                    else:
                        v.tensor_tensor(o, i, bias[0:d, L, 0:parts].unsqueeze(2).to_broadcast([d, parts, P]),
                                        ALU.add).then_inc(sem(name), 1)
                dve.wait_ge(sem("attn_v_psum"), L + 1)
                if L == 2:
                    v.tensor_copy(a_v, bank(7)[:, 0:D]).then_inc(sem("attn_v_ready"), 1)
                else:
                    v.tensor_tensor(a_v, bank(7)[:, 0:D], abv[:, L, :], ALU.add).then_inc(sem("attn_v_ready"), 1)
                dve.wait_ge(sem("attn_scores"), L + 1)
                S3 = a_S[:, 0:n].rearrange("p (h n) -> p h n", h=heads)
                U3 = a_U[:, 0:n].rearrange("p (h n) -> p h n", h=heads)
                B3 = bank(0, 4)[:, 0:n].rearrange("p (h n) -> p h n", h=heads)

                def per_head(t2):
                    return t2[:, 0:heads].unsqueeze(2).to_broadcast([P, heads, P])
                if L < 3:
                    dve.wait_ge(sem("windows_ready"), 1)
                    win = windows[L][:].unsqueeze(1).to_broadcast([P, heads, P])
                if L < 2:
                    link(v.scalar_tensor_tensor(S3, B3, ASCALE[L], win, ALU.mult, ALU.add))
                elif L == 3:
                    dve.wait_ge(sem("rel_landed"), 16 * len(rel_loads))
                    link(v.scalar_tensor_tensor(S3, B3, ASCALE[L], rel, ALU.mult, ALU.add))
                else:
                    v.tensor_scalar(a_S, bank(0, 4), ASCALE[2], None, ALU.mult).then_inc(sem("l2_scaled"), 1)
                    dve.wait_ge(sem("l2_scaled"), 1)
                    link(v.tensor_reduce(a_m[:, 0:heads], S3, AX_X, ALU.add))
                    link(v.tensor_scalar(a_m[:, 0:heads], a_m[:, 0:heads], 1.0 / P, None, ALU.mult))
                    v.tensor_tensor(U3, S3, per_head(a_m), ALU.subtract).then_inc(sem("l2_centred"), 1)
                    link(v.tensor_scalar(ngates[:], gates[:], -1.0, None, ALU.mult))
                    dve.wait_ge(sem("l2_act"), 2)
                    link(v.scalar_tensor_tensor(a_T, a_T, ngates[:, 0:1], a_S, ALU.mult, ALU.add))
                    link(v.scalar_tensor_tensor(a_T, a_S, gates[:, 1:2], a_T, ALU.mult, ALU.add))
                    dve.wait_ge(sem("l2_act"), 3)
                    link(v.scalar_tensor_tensor(a_S, a_U, ngates[:, 2:3], a_T, ALU.mult, ALU.add))
                    link(v.tensor_tensor(S3, S3, win, ALU.add))
                link(v.tensor_reduce(a_m[:, 0:heads], S3, AX_X, ALU.max))
                v.tensor_tensor(S3, S3, per_head(a_m), ALU.subtract).then_inc(sem("attn_shifted"), 1)
                dve.wait_ge(sem("attn_probs"), L + 1)
                link(v.tensor_reduce(a_s[:, 0:heads], S3, AX_X, ALU.add))
                link(v.reciprocal(a_s[:, 0:heads], a_s[:, 0:heads]))
                dve.wait_ge(sem("attn_o_psum"), L + 1)
                w = D // heads
                v.tensor_tensor(a_o.rearrange("p (h n) -> p h n", h=heads),
                                bank(4)[:, 0:D].rearrange("p (h n) -> p h n", h=heads),
                                a_s[:, 0:heads].unsqueeze(2).to_broadcast([P, heads, w]), ALU.mult
                                ).then_inc(sem("attn_o_ready"), 1)
                dve.wait_ge(sem("attn_oT_psum"), L + 1)
                v.tensor_copy(a_oT.rearrange("p c n -> p (c n)"), bank(5)[:, 0:D]).then_inc(sem("attn_oT_ready"), 1)
                if L != 2:
                    link(v.tensor_tensor(x[:], x[:], bo_all[:, 4 + L, :], ALU.add))
                if L == 1:
                    link(v.tensor_tensor(x[:], x[:], xn[:], ALU.add))
                dve.wait_ge(sem("attn_out_psum"), L + 1)
                v.tensor_tensor(x[:], bank(6)[:, 0:D], x[:], ALU.add).then_inc(sem("attn_done"), 1)
                dve.wait_ge(sem("attn_done"), L + 1)

            def softmax_route(L, e):
                dve.wait_ge(sem("logits_psum"), L + 1)
                link(v.tensor_reduce(rmax[:], bank(1)[:, 0:e], AX_X, ALU.max))
                v.tensor_scalar(logit[:, 0:e], bank(1)[:, 0:e], rmax[:, 0:1], None, ALU.subtract
                                ).then_inc(sem("route_shifted"), 1)
                dve.wait_ge(sem("route_exp"), L + 1)
                link(v.tensor_reduce(rsum[:], prob[:, 0:e], AX_X, ALU.add))
                link(v.reciprocal(rinv[:], rsum[:]))
                link(v.tensor_scalar(prob[:, 0:e], prob[:, 0:e], rinv[:, 0:1], None, ALU.mult))

            def pick_top(e, k):
                link(v.memset(prob[:, e:e + 8], -1.0))
                link(v.max(top8[:], prob[:, 0:e]))
                if k < 8:
                    link(v.memset(top8[:, k:8], -1.0))
                link(v.match_replace(probr[:, 0:e + 8], top8[:], prob[:, 0:e + 8], -2.0))
                link(v.scalar_tensor_tensor(comb[:, 0:e], probr[:, 0:e], -2.0, prob[:, 0:e], ALU.is_equal, ALU.mult))

            def finish(L, value):
                v.tensor_tensor(x[:], value, x[:], ALU.add).then_inc(sem("ffn_done"), 1)
                dve.wait_ge(sem("ffn_done"), L + 1)

            def ffn_glu(L):
                f = FW[L]
                fc = f // 2
                e_n = 8 if L == 0 else 64
                norm(3 * L + 2)
                softmax_route(L, e_n)
                if L == 0:
                    pick_top(8, 2)
                    link(v.memset(comb[:, 8:10], 1.0))
                else:
                    pick_top(64, 8)
                    link(v.tensor_reduce(rsum[:], top8[:], AX_X, ALU.add))
                    link(v.reciprocal(rinv[:], rsum[:]))
                    link(v.tensor_scalar(comb[:, 0:64], comb[:, 0:64], rinv[:, 0:1], None, ALU.mult))
                    link(v.memset(comb[:, 64:65], 1.0))
                b0 = 0 if L == 0 else NE[0]

                def hidden(e, par, at):
                    dve.wait_ge(sem("silu"), at)
                    wait_count(dve, sem("hT_psum"), at - 2)
                    v.scalar_tensor_tensor(h_s[:, par, 0:f], g_s[:, par, 0:f], comb[:, bass.ds(e, 1)],
                                           bank(5 + 2 * par)[:, 0:f], ALU.mult, ALU.mult
                                           ).then_inc(sem("h_ready"), 1)

                def turned(par, at):
                    dve.wait_ge(sem("hT_psum"), at)
                    v.tensor_copy(hT[0:fc, par, :], bank(par)[0:fc, 0:2 * P]).then_inc(sem("hT_ready"), 1)
                hidden(0, 0, b0 + 1)
                if L == 0:
                    for e in range(NE[0]):
                        if e + 1 < NE[0]:
                            hidden(e + 1, (e + 1) % 2, e + 2)
                        turned(e % 2, e + 1)
                else:
                    with dve.Fori(0, 16) as it:
                        for j in range(RING):
                            hidden(it * RING + (j + 1), (j + 1) % 2, it * RING + (b0 + j + 2))
                            turned(j % 2, it * RING + (b0 + j + 1))
                    turned(0, b0 + 65)
                dve.wait_ge(sem("ring_used"), NE0[L + 1])
                finish(L, bank(2)[:, 0:D])

            def ffn1():
                norm(5)
                softmax_route(1, 32)
                pick_top(32, 2)
                link(v.memset(y_acc, 0.0))
                for e in range(NE[1]):
                    dve.wait_ge(sem("ring_used"), NE0[1] + e + 1)
                    for j in range(2):
                        if e >= 1:
                            dve.wait_ge(sem("l1_step"), 2 * (e - 1) + j + 1)
                        g = v.scalar_tensor_tensor(y_acc[:, j, :], bank(4 + e % 2)[:, j * D:(j + 1) * D],
                                                   comb[:, 2 * e + j:2 * e + j + 1], y_acc[:, j, :],
                                                   ALU.mult, ALU.add)
                        g.then_inc(sem("l1_step"), 1)
                dve.wait_ge(sem("l1_step"), 2 * NE[1])
                link(v.tensor_tensor(y_acc[:, 0, :], y_acc[:, 0, :], y_acc[:, 1, :], ALU.add))
                finish(1, y_acc[:, 0, :])

            def ffn3():
                v.tensor_tensor(csq[:], rw[:, 3, :, 0:8], rw[:, 3, :, 0:8], ALU.mult).then_inc(sem("csq_ready"), 1)
                norm(11)
                link(v.tensor_tensor(xsq, xn[:], xn[:], ALU.mult))
                v.tensor_reduce(rsum[:], xsq, AX_X, ALU.add).then_inc(sem("xsq_ready"), 1)
                dve.wait_ge(sem("norms_ready"), 2)
                link(v.tensor_scalar(rsum[:], rsum[:], 1e-12, None, ALU.max))
                link(v.reciprocal(rinv[:], rsum[:]))
                link(v.tensor_scalar(cnorm[:], cnorm[:], 1e-12, None, ALU.max))
                link(v.reciprocal(cnorm[:], cnorm[:]))
                dve.wait_ge(sem("logits_psum"), 4)
                link(v.scalar_tensor_tensor(logit[:, 0:8], bank(1)[:, 0:8], rinv[:, 0:1], cnorm[:], ALU.mult, ALU.mult))
                link(v.tensor_tensor(logit[:, 0:8], bank(1)[:, 8:16], logit[:, 0:8], ALU.add))
                link(v.max(top8[:], logit[:, 0:8]))
                link(v.tensor_scalar(comb[:, 0:8], logit[:, 0:8], top8[:, 1:2], None, ALU.is_ge))
                v.tensor_scalar(logit[:, 0:8], logit[:, 0:8], top8[:, 0:1], None, ALU.subtract
                                ).then_inc(sem("route_shifted"), 1)
                dve.wait_ge(sem("route_exp"), 4)
                link(v.tensor_tensor(comb[:, 0:8], prob[:, 0:8], comb[:, 0:8], ALU.mult))
                link(v.tensor_reduce(rsum[:], comb[:, 0:8], AX_X, ALU.add))
                link(v.reciprocal(rinv[:], rsum[:]))
                v.tensor_scalar(comb[:, 0:8], comb[:, 0:8], rinv[:, 0:1], None, ALU.mult).then_inc(sem("comb_ready"), 1)
                dve.wait_ge(sem("comb_ready"), 1)
                dve.wait_ge(sem("gT_psum"), 1)
                v.tensor_copy(gT, bank(2)[0:8, 0:P]).then_inc(sem("gT_ready"), 1)
                dve.wait_ge(sem("b2_psum"), 1)
                link(v.tensor_copy(y_acc[:, 0, :], bank(3)[:, 0:D]))
                for e in range(8):
                    dve.wait_ge(sem("ring_used"), NE0[3] + e + 1)
                    if e:
                        dve.wait_ge(sem("l3_taken"), e)
                    v.scalar_tensor_tensor(y_acc[:, 0, :], bank(6 + e % 2)[:, 0:D], comb[:, e:e + 1],
                                           y_acc[:, 0, :], ALU.mult, ALU.add).then_inc(sem("l3_taken"), 1)
                dve.wait_ge(sem("l3_taken"), 8)
                finish(3, y_acc[:, 0, :])

            for s in range(stages):
                L = s // 3
                if s % 3 == 0:
                    xattn(L)
                elif s % 3 == 1:
                    attn(L)
                elif L in (0, 2):
                    ffn_glu(L)
                elif L == 1:
                    ffn1()
                else:
                    ffn3()
            v.tensor_scalar(x[:], x[:], 1.0, None, ALU.mult).then_inc(sem("x_final"), 1)


STAGES = 12


def kernel(**inputs):
    import numpy as np
    import concourse.bacc as bacc
    from concourse.bass_utils import run_bass_kernel_spmd

    nc = bacc.Bacc("TRN2", target_bir_lowering=False, num_devices=1)
    a = {n: np.asarray(v) for n, v in inputs.items()}
    lay = {"x": a["x"][0], "ctx": a["ctx_768"][0], "mask": a["mask_BxS2_bk0"][0]}
    xn = [("L0_xattn_W_q", "L0_xattn_W_k", "L0_xattn_W_v", "L0_xattn_W_o"),
          ("L1_xattn_w_q", None, None, "L1_xattn_w_out"),
          ("L2_xattn_Wq", "L2_xattn_Wk", "L2_xattn_Wv", "L2_xattn_Wo"),
          ("L3_xattn_wq", "L3_xattn_wk", "L3_xattn_wv", "L3_xattn_wo")]
    for L, (q, k, v, o) in enumerate(xn):
        inner = XH[L] * XD[L]
        kv = a["L1_xattn_w_kv"]
        lay[f"x{L}_wq"] = a[q]
        bk = a[f"L{L}_xattn_bk"] if L >= 2 else np.zeros(inner, np.float32)
        wk = np.concatenate([(a[k] if k else kv[:, :inner]).T, bk[:, None]], axis=1)
        lay[f"x{L}_wkT"] = wk.reshape(XH[L], XD[L], C + 1).transpose(1, 0, 2)
        lay[f"x{L}_wv"] = a[v] if v else kv[:, inner:]
        lay[f"x{L}_wo"] = a[o]
    for n in "qkvo":
        lay[f"a0_w{n}"] = a[f"L0_attn_W{n}"]
        lay[f"a1_w{n}"] = a[f"L1_attn_W{n}"].T
        lay[f"a2_w{n}"] = a[f"L2_attn_W{n}"].T
    for i, n in enumerate("qkv"):
        lay[f"a3_w{n}"] = a["L3_attn_W_qkv"][:, i * D:(i + 1) * D]
    lay["a3_wo"] = a["L3_attn_W_out"]
    for n in ["L0_xattn_b_o", "L1_xattn_b_out", "L2_xattn_bo", "L3_xattn_bo", "L0_attn_bo", "L1_attn_bo",
              "L3_attn_b_out", "L0_ffn_router_w", "L0_ffn_gate_w", "L0_ffn_up_w",
              "L0_ffn_down_w", "L0_ffn_shared_gate_w", "L0_ffn_shared_up_w", "L0_ffn_shared_down_w",
              "L1_ffn_expert_weights", "L2_ffn_w_gate", "L2_ffn_w_up", "L2_ffn_w_down", "L2_ffn_ws_gate_up",
              "L2_ffn_ws_down", "L3_ffn_w1", "L3_ffn_w2", "L3_ffn_b2"]:
        lay[n] = a[n]
    for n in ["sep", "align", "coh"]:
        lay[f"L2_attn_{n}_gate"] = a[f"L2_attn_{n}_gate"].reshape(1)
    for n in ["L1_ffn_router_w", "L2_ffn_router_w", "L3_ffn_centroids", "L3_ffn_w_route"]:
        lay[n + "T"] = a[n].T
    for n in ["L2_xattn_bq", "L2_xattn_bv", "L3_xattn_bq", "L3_xattn_bv"]:
        lay[n + "T"] = a[n].reshape(16, 16).T
    b3 = a["L3_attn_b_qkv"]
    for i, (q, k, v) in {0: (a["L0_attn_bq"], a["L0_attn_bk"], a["L0_attn_bv"]),
                         1: (a["L1_attn_bq"], a["L1_attn_bk"], a["L1_attn_bv"]),
                         3: (b3[0:D], b3[D:2 * D], b3[2 * D:3 * D])}.items():
        lay[f"a{i}_bqT"] = q.reshape(AH[i], AD[i]).T
        lay[f"a{i}_bkT"] = k.reshape(AH[i], AD[i]).T
        lay[f"a{i}_bv"] = v
    lay["L3_ffn_b1T"] = a["L3_ffn_b1"].T
    lay["L3_attn_rel_biasT"] = a["L3_attn_rel_bias"].T
    arrays, io = {}, {}
    for n, v in lay.items():
        v = np.ascontiguousarray(v)
        arrays[f"in_{n}"] = v
        io[n] = nc.dram_tensor(f"in_{n}", v.shape, mybir.dt.from_np(v.dtype), kind="ExternalInput").ap()
    out = nc.dram_tensor("out_x", (1, P, D), F32, kind="ExternalOutput").ap()
    build(nc, io, out.rearrange("a p d -> (a p) d"), STAGES)
    r = run_bass_kernel_spmd(nc, [arrays], core_ids=[0])
    return r.results[0]["out_x"]
```

```python
from contextlib import ExitStack

import concourse.bass as bass
from concourse import mybir

ALU = mybir.AluOpType
ACT = mybir.ActivationFunctionType
AX_X = mybir.AxisListType.X
F32 = mybir.dt.float32
BF16 = mybir.dt.bfloat16
U8 = mybir.dt.uint8
U32 = mybir.dt.uint32
RMAX = bass.bass_isa.ReduceOp.max

P = 128
D = 256
DC = D // P
C = 192
CB = C - P
KEYS = 12544
TILES = KEYS // P
G = 7
GROUPS = TILES // G
BODY = 2 * G
ITERS = GROUPS // 2
HG = 8
QC = HG * P
BANK = 512
GK = G * P

S_A, S_D, S_B, S_C, S_R, S_ONE, S_L = 0, 128, 256, 384, 512, 704, 706
S_W = S_L + C
S_P1 = 256
BIAS_HI, BIAS_LO = 64, 96

NEG = -1.7e38
NEG_ATTN = -1e30
CLAMP = 10000.0
MAX_REL = 256
EPS = 1e-5
RING = 4

XH = [8, 16, 16, 16]
XD = [64, 64, 16, 16]
SWEEPS = [1, 2]
SWEEP0 = [0, 1]
WH = 16
WP = WH // 2
VW = 2 * WH + 2
UNITS = 2 * TILES
UBODY = 2 * BODY
LEAD = 3
SLOTS = 4
PROJ = 15
AH = [8, 2, 16, 16]
AD = [32, 128, 16, 16]
AS = [8, 1, 16, 16]
ASCALE = [32 ** -0.5, 0.25, 0.25, 0.25]
NE = [10, 16, 65, 8]
NE0 = [sum(NE[:i]) for i in range(5)]
FW = [256, 0, 192, 0]
LAYERS = 4


def sweep_loop(eng, body, peel_first, peel_last):
    lo, hi = int(peel_first), ITERS - int(peel_last)
    for it in range(lo):
        body(it)
    with eng.Fori(lo, hi) as it:
        body(it)
    for it in range(hi, ITERS):
        body(it)


def wait_count(eng, sem, count):
    if isinstance(count, int) and count <= 0:
        return
    eng.wait_ge(sem, count)


def build(nc, io, out, stages=12):
    with ExitStack() as ctx:
        def sb(name, shape, dt=F32):
            return ctx.enter_context(nc.sbuf_tensor(name, shape, dt))

        named = {}

        def sem(name):
            if name not in named:
                named[name] = ctx.enter_context(nc.semaphore(name))
            return named[name]

        ps = ctx.enter_context(nc.psum_tensor("ps", [P, 8, BANK], F32))
        psf = ps[:].rearrange("p b n -> p (b n)")

        def bank(b, n=1):
            return psf[:, b * BANK:(b + n) * BANK]

        kst = nc.dram_tensor("keys_T", [2, 2, GROUPS, D, GK], BF16, kind="Internal").ap()
        vst = nc.dram_tensor("values", [2, GROUPS, P, G * WH * VW], BF16, kind="Internal").ap()
        stream = nc.dram_tensor("ctx_stream", [GROUPS, P, G, S_W], BF16, kind="Internal").ap()

        ident = sb("ident", [P, P])
        ones = sb("ones", [P, P])
        onesb = sb("ones_bf16", [P, P], BF16)
        zrow = sb("zrow", [P, BANK], BF16)
        win_block = sb("win_block", [P, P])
        win_causal = sb("win_causal", [P, P])
        win_band = sb("win_band", [P, P])
        windows = [win_block, win_causal, win_band]
        x = sb("x_res", [P, D])
        xn = sb("xn", [P, D])
        xnT = sb("xnT", [P, DC, P])
        stats = sb("stats", [P, 6])
        mv = sb("mv", [P, 2])
        rstd = sb("rstd", [P, 1])
        o_rows = sb("o_rows", [P, 16, C])
        ctx_in = o_rows[:].rearrange("p h c -> p (h c)")[:, 0:2 * G * C].rearrange("p (b g c) -> p b g c", b=2, g=G)
        sregion = sb("stream_region", [P, 2 * G * (S_W + S_P1)], BF16)
        sbuf2 = sregion[:, 0:2 * G * S_W].rearrange("p (b g w) -> p b g w", b=2, g=G)
        sbuf1 = sregion[:, 2 * G * S_W:].rearrange("p (b g w) -> p b g w", b=2, g=G)
        kbuf = sregion[:, 0:2 * WP * GK].rearrange("p (b j n) -> p b j n", b=2, j=WP)
        keep_u8 = sb("keep_u8", [P, TILES], U8)
        keep = sb("keep", [P, TILES])
        maskneg = sb("maskneg", [P, TILES])
        any_keep = sb("any_keep", [P, 1])
        alive = sb("alive", [P, 1])
        qscale0 = sb("qscale0", [P, 1])
        xwq = sb("xwq", [P, DC, 1024])
        WKW = 16 * (C + 1)
        xwkv = sb("xwkv", [P, WKW + 2048])
        xwk = xwkv[0:64, 0:WKW].rearrange("p (h c) -> p h c", h=16)
        xwva = xwkv[:, WKW:WKW + 1024]
        xwvb = xwkv[0:CB, WKW + 1024:WKW + 2048]
        vbuf = xwkv[:].bitcast(BF16)[:, 0:2 * G * WH * VW].rearrange("p (b g h w) -> p b g h w", b=2, g=G, h=WH)
        xwo = sb("xwo", [P, 16, D])
        xwo2 = xwo[:, 0:DC, :]
        xbq4 = sb("xbq4", [P, 2, WP])
        half_a = sb("half_a", [P, 1])
        half_b = sb("half_b", [P, 1])
        vsum = o_rows[:].rearrange("p h c -> p (h c)")[:, 0:WH * VW].rearrange("p (h w) -> p h w", h=WH)
        bo_all = sb("bo_all", [P, 8, D])
        qT = sb("qT", [P, 16, P])
        qf_a = sb("qf_a", [P, QC])
        qf_b = sb("qf_b", [P, QC])
        vmean = qf_b[:, 0:D]
        qh_a = sb("qh_a", [P, QC], BF16)
        ql_a = sb("ql_a", [P, QC], BF16)
        q_bb = sb("q_bb", [P, QC], BF16)
        q_d1 = sb("q_d1", [P, QC], BF16)
        q_d2 = sb("q_d2", [P, QC], BF16)
        maxall = sb("maxall", [P, QC])
        p32 = sb("p32", [P, SLOTS, QC])
        runmax = p32[:, 0:2]
        parts = sb("p_parts", [P, 2, SLOTS, QC], BF16)
        phi, plo = parts[:, 0], parts[:, 1]
        kstage = p32[:].rearrange("p s n -> p (s n)").bitcast(BF16)[:, 0:8 * GK].rearrange(
            "p (m h n) -> p m h n", m=4, h=2)
        vstage = parts[:].rearrange("p a s n -> p (a s n)")[:, 0:2 * G * WH * VW].rearrange(
            "p (l g h w) -> p l g h w", l=2, g=G, h=WH)
        mq = maxall[:].bitcast(BF16)
        maxl = qT[:].rearrange("p h n -> p (h n)")
        den = sb("den", [P, 16])
        rden = sb("rden", [P, 16])
        nanf = sb("nanf", [P, 16])
        nan1 = sb("nan1", [P, 1])
        nana = sb("nana", [P, 1])
        oT_a = qf_a[:].rearrange("p (b n) -> p b n", b=2)
        oT_b = qf_b[0:CB, :].rearrange("p (b n) -> p b n", b=2)
        avT = maxall[0:64, :].rearrange("p (b n) -> p b n", b=2)
        aw = sb("aw", [P, DC, 4 * D])
        abq = sb("abq", [P, 4, 16])
        abk = sb("abk", [P, 4, 16])
        abv = sb("abv", [P, 4, D])
        gates = sb("gates", [P, 3])
        ngates = sb("ngates", [P, 3])
        rel = o_rows[:].rearrange("p h c -> p (h c)")[:, 0:16 * P].rearrange("p (h n) -> p h n", h=16)
        a_m = sb("a_m", [P, 16])
        a_s = sb("a_s", [P, 16])
        a_v = qh_a[:].bitcast(F32)[:, 0:D]
        a_o = ql_a[:].bitcast(F32)[:, 0:D]
        a_oT = q_bb[:].bitcast(F32)[:, 0:D].rearrange("p (c n) -> p c n", c=DC)
        xnT_rev = q_bb[:].bitcast(F32)[:, D:2 * D].rearrange("p (c n) -> p c n", c=DC)
        qk_buf = sregion[:].bitcast(F32)
        a_q = qk_buf[:, 0:2048]
        a_k = qk_buf[:, 2048:4096]
        a_S = p32[:, 0:2].rearrange("p a n -> p (a n)")
        a_U = p32[:, 2:4].rearrange("p a n -> p (a n)")
        a_T = phi.bitcast(F32).rearrange("p a n -> p (a n)")
        ring = sb("ring", [P, RING, 1536])
        rw = sb("rw", [P, LAYERS, DC, 64])
        logit = sb("logit", [P, 64])
        prob = sb("prob", [P, 72])
        probr = sb("probr", [P, 72])
        top8 = sb("top8", [P, 8])
        rmax = sb("rmax", [P, 1])
        rsum = sb("rsum", [P, 1])
        rinv = sb("rinv", [P, 1])
        comb = sb("comb", [P, 66])
        g_s = phi[:, 0].bitcast(F32).rearrange("p (b n) -> p b n", b=2)
        h_s = phi[:, 1].bitcast(F32).rearrange("p (b n) -> p b n", b=2)
        hT = plo[:, 0].bitcast(F32).rearrange("p (b n) -> p b n", b=2)
        y_acc = plo[:, 1].bitcast(F32).rearrange("p (b n) -> p b n", b=2)
        xsq = g_s[:, 0, :]
        b1T = sb("b1T", [P, 8])
        b2r = sb("b2r", [8, D])
        csq = sb("csq", [P, DC, 8])
        cnorm = sb("cnorm", [P, 8])
        gT = qT[0:8, 0, :]

        PIECES = [(qh_a, S_A), (ql_a, S_A), (qh_a, S_C), (q_bb, S_B), (q_d2, S_D)]
        in_landed = [sem("ctx_in_landed0"), sem("ctx_in_landed1")]
        stream_out = [sem("stream_written0"), sem("stream_written1")]
        p1_landed = [sem("max_stream_landed0"), sem("max_stream_landed1")]
        p2_landed = [sem("stream_landed0"), sem("stream_landed1")]
        k_landed = [sem("keys_landed0"), sem("keys_landed1")]
        v_landed = [sem("values_landed0"), sem("values_landed1")]
        ring_landed = [sem(f"ring_landed{i}") for i in range(RING)]
        xw_landed = sem("xattn_weights_landed")
        aw_landed = sem("attn_weights_landed")
        const_landed = sem("consts_landed")
        XW_DMAS = [5, 5, 2, 2]
        AW_DMAS = [4, 4, 4, 4]
        xw_at = [16 * sum(XW_DMAS[:i + 1]) for i in range(4)]
        aw_at = [16 * sum(AW_DMAS[:i + 1]) for i in range(4)]
        const_count = [0]

        block = ctx.enter_context(nc.Block())

        def plain_wait(eng, s, count):
            if isinstance(count, int):
                if count > 0:
                    eng.wait_ge(s, count)
                return
            count = eng.snap(count)
            eng.wait_ge(s, count)
            eng.sem_inc(sem("waits_passed"), 1)
        ctx_rows = io["ctx"].rearrange("(p t) c -> p t c", t=TILES)
        layers = (stages + 2) // 3

        def has(kind, layer):
            return 3 * layer + kind < stages

        consts = [
            (x[:], io["x"]),
            (keep_u8[:], io["mask"].rearrange("(p t) -> p t", t=TILES)),
        ]
        for i, n in enumerate(["L0_xattn_b_o", "L1_xattn_b_out", "L2_xattn_bo", "L3_xattn_bo"]):
            consts.append((bo_all[:, i, :], io[n].partition_broadcast(P)))
        for i, n in enumerate(["L0_attn_bo", "L1_attn_bo", None, "L3_attn_b_out"]):
            if n:
                consts.append((bo_all[:, 4 + i, :], io[n].partition_broadcast(P)))
        for i, n in enumerate(["L2_xattn", "L3_xattn"]):
            for j in range(4):
                consts.append((xbq4[32 * j:32 * j + 32, i, :], io[n + "_bqT"]))
        for i in (0, 1, 3):
            consts.append((abq[0:AD[i], i, 0:AH[i]], io[f"a{i}_bqT"]))
            consts.append((abk[0:AD[i], i, 0:AH[i]], io[f"a{i}_bkT"]))
            consts.append((abv[:, i, :], io[f"a{i}_bv"].partition_broadcast(P)))
        for i, n in enumerate(["sep", "align", "coh"]):
            consts.append((gates[:, i:i + 1], io[f"L2_attn_{n}_gate"].partition_broadcast(P)))
        for i, (n, e) in enumerate([("L0_ffn_router_w", 8), ("L1_ffn_router_wT", 32), ("L2_ffn_router_wT", 64)]):
            consts.append((rw[:, i, :, 0:e], io[n].rearrange("(c p) e -> p c e", p=P)))
        consts.append((rw[:, 3, :, 0:8], io["L3_ffn_centroidsT"].rearrange("(c p) e -> p c e", p=P)))
        consts.append((rw[:, 3, :, 8:16], io["L3_ffn_w_routeT"].rearrange("(c p) e -> p c e", p=P)))
        consts.append((b1T[:], io["L3_ffn_b1T"]))
        consts.append((b2r[:], io["L3_ffn_b2"]))
        relT = io["L3_attn_rel_biasT"]
        rel_loads = [(rel, bass.AP(relT.tensor, MAX_REL - P + 1, [[1, P], [2 * MAX_REL + 1, 16], [1, P]]))]
        CONSTS_ALL = 16 * len(consts)
        EARLY = 2

        def load_xw(sp, L):
            h, d = XH[L], XD[L]
            inner = h * d if L < 2 else WP * P
            sp.dma_start(xwq[:, :, 0:inner], io[f"x{L}_wq"].rearrange("(c p) n -> p c n", p=P)).then_inc(xw_landed, 16)
            if L >= 2:
                sp.dma_start(xwo2, io[f"x{L}_wo"].rearrange("(c p) n -> p c n", p=P)).then_inc(xw_landed, 16)
                return
            sp.dma_start(xwk[0:d, 0:h, :], io[f"x{L}_wkT"]).then_inc(xw_landed, 16)
            sp.dma_start(xwva[:, 0:inner], io[f"x{L}_wv"][0:P, :]).then_inc(xw_landed, 16)
            sp.dma_start(xwvb[:, 0:inner], io[f"x{L}_wv"][P:C, :]).then_inc(xw_landed, 16)
            sp.dma_start(xwo[0:d, 0:h, :], io[f"x{L}_wo"].rearrange("(h d) n -> d h n", d=d)).then_inc(xw_landed, 16)

        def load_aw(sp, L):
            for j, n in enumerate("qkvo"):
                sp.dma_start(aw[:, :, j * D:(j + 1) * D],
                             io[f"a{L}_w{n}"].rearrange("(c p) n -> p c n", p=P)).then_inc(aw_landed, 16)

        def ring_parts(L, e):
            if L == 0:
                f = FW[0]
                if e < 8:
                    g, u, d = io["L0_ffn_gate_w"][e], io["L0_ffn_up_w"][e], io["L0_ffn_down_w"][e]
                else:
                    o = (e - 8) * f
                    g, u = io["L0_ffn_shared_gate_w"][:, o:o + f], io["L0_ffn_shared_up_w"][:, o:o + f]
                    d = io["L0_ffn_shared_down_w"][o:o + f, :]
                return g, u, d
            if L == 2:
                return (io["L2_ffn_w_gate"][e], io["L2_ffn_w_up"][e], io["L2_ffn_w_down"][e])

        def gu_view(slot, f):
            return ring[:, slot, 0:2 * DC * f].rearrange("p (c n) -> p c n", c=DC)

        def dn_view(slot, f):
            return ring[0:f // 2, slot, 1024:1024 + 2 * D].rearrange("p (c n) -> p c n", c=2)

        RING_DMAS = [3, 2, 3, 2]

        def ring_slot_at(L, e):
            return (NE0[L] + e) % RING

        def landed_before(slot, L):
            n = 0
            for l in range(L):
                n += 16 * RING_DMAS[l] * len([e for e in range(NE[l]) if (NE0[l] + e) % RING == slot])
            return n

        def landed_at(L, e):
            slot = (NE0[L] + e) % RING
            k = len([i for i in range(e + 1) if (NE0[L] + i) % RING == slot])
            return landed_before(slot, L) + 16 * RING_DMAS[L] * k

        def load_ring(sp, L, e):
            n = NE0[L] + e
            slot = n % RING
            wait_count(sp, sem("ring_used"), n - RING + 1)
            s = ring_landed[slot]
            if L in (0, 2):
                f = FW[L]
                if L == 2 and e == 64:
                    gu = io["L2_ffn_ws_gate_up"]
                    g, u, d = gu[:, 0:f], gu[:, f:2 * f], io["L2_ffn_ws_down"]
                else:
                    g, u, d = ring_parts(L, e)
                v = gu_view(slot, f)
                sp.dma_start(v[:, :, 0:f], g.rearrange("(c p) n -> p c n", p=P)).then_inc(s, 16)
                sp.dma_start(v[:, :, f:2 * f], u.rearrange("(c p) n -> p c n", p=P)).then_inc(s, 16)
                sp.dma_start(dn_view(slot, f), d.rearrange("(c p) n -> p c n", p=f // 2)).then_inc(s, 16)
            elif L == 1:
                v = gu_view(slot, 256)
                for j in range(2):
                    sp.dma_start(v[:, :, j * D:(j + 1) * D],
                                 io["L1_ffn_expert_weights"][2 * e + j].rearrange("(c p) n -> p c n", p=P)
                                 ).then_inc(s, 16)
            else:
                sp.dma_start(ring[:, slot, 0:DC * P].rearrange("p (c n) -> p c n", c=DC),
                             io["L3_ffn_w1"][e].rearrange("(c p) n -> p c n", p=P)).then_inc(s, 16)
                sp.dma_start(ring[:, slot, 1024:1024 + D], io["L3_ffn_w2"][e]).then_inc(s, 16)

        def load_ring2_loop(sp):
            with sp.Fori(1, 16) as it:
                for j in range(RING):
                    slot = (NE0[2] + j) % RING
                    s = ring_landed[slot]
                    f = FW[2]
                    plain_wait(sp, sem("ring_used"), it * RING + (NE0[2] + j - RING + 1))
                    v = gu_view(slot, f)
                    e = it * RING + j
                    sp.dma_start(v[:, :, 0:f], io["L2_ffn_w_gate"][bass.ds(e, 1)].rearrange(
                        "o (c p) n -> p (o c) n", p=P)).then_inc(s, 16)
                    sp.dma_start(v[:, :, f:2 * f], io["L2_ffn_w_up"][bass.ds(e, 1)].rearrange(
                        "o (c p) n -> p (o c) n", p=P)).then_inc(s, 16)
                    sp.dma_start(dn_view(slot, f), io["L2_ffn_w_down"][bass.ds(e, 1)].rearrange(
                        "o (c p) n -> p (o c) n", p=f // 2)).then_inc(s, 16)

        @block.sync
        def _(sp):
            for d, s in consts[:EARLY]:
                sp.dma_start(d, s).then_inc(sem("early_landed"), 16)

            def ctx_load(g, b):
                sp.dma_start(ctx_in[:, b], ctx_rows[:, bass.ds(g * G, G), :]).then_inc(in_landed[b], 16)

            def ctx_store(it, b):
                plain_wait(sp, sem("dve_split"), it * 2 + b + 1)
                plain_wait(sp, sem("pool_split"), it * 2 + (b + 1))
                sp.dma_start(stream[bass.ds(it * 2 + b, 1)].rearrange("o p g w -> p (o g) w"),
                             sbuf2[:, b]).then_inc(stream_out[b], 16)
            ctx_load(0, 0)
            ctx_load(1, 1)
            sp.dma_start(qf_a[:], io["kv23"][0:P, :]).then_inc(sem("kv_weights_landed"), 16)
            sp.dma_start(qf_b[0:CB + 1, :], io["kv23"][P:C + 1, :]).then_inc(sem("kv_weights_landed"), 16)
            load_xw(sp, 0)
            load_aw(sp, 0)
            for d, s in consts[EARLY:]:
                sp.dma_start(d, s).then_inc(const_landed, 16)
            for e in range(RING):
                load_ring(sp, 0, e)

            def kv_store(it, b):
                g = it * 2 + b
                plain_wait(sp, sem("proj_lo"), g * PROJ + 8)
                for l in range(2):
                    for hl in range(2):
                        sp.dma_start(kst[l, hl, bass.ds(g, 1)].rearrange("o (m p) n -> p (o m) n", p=P),
                                     kstage[:, 2 * l:2 * l + 2, hl, :]).then_inc(sem("keys_written"), 16)
                plain_wait(sp, sem("proj_lo"), g * PROJ + PROJ)
                for l in range(2):
                    sp.dma_start(vst[l, bass.ds(g, 1)].rearrange("o p n -> p (o n)"),
                                 vstage[:, l].rearrange("p g h w -> p (g h w)")
                                 ).then_inc(sem("values_written"), 16)
            with sp.Fori(0, ITERS - 1) as it:
                for b in range(2):
                    ctx_store(it, b)
                    ctx_load(it * 2 + (2 + b), b)
                    kv_store(it, b)
            for b in range(2):
                ctx_store(ITERS - 1, b)
                kv_store(ITERS - 1, b)
            for b in range(2):
                sp.wait_ge(stream_out[b], 16 * ITERS)
            sp.wait_ge(sem("keys_written"), 64 * GROUPS)
            sp.wait_ge(sem("values_written"), 32 * GROUPS)

            for L in range(layers):
                if L >= 2:
                    l = L - 2

                    def k_load(g, b):
                        for j, hl in enumerate((0, 1, 0)):
                            sp.dma_start(kbuf[32 * j:32 * j + 32, b],
                                         kst[l, hl, bass.ds(g, 1)].rearrange("o (j r) n -> r (o j) n", r=32)
                                         ).then_inc(k_landed[b], 16)

                    def max_k_loads(it):
                        for b in range(2):
                            if isinstance(it, int):
                                sp.wait_ge(sem("attn_done"), L)
                            else:
                                plain_wait(sp, sem("low_max_scores"), it * UBODY + (UNITS * l + 2 * G * (b - 1)))
                            k_load(it * 2 + b, b)

                    def kv_loads(it):
                        for b in range(2):
                            if isinstance(it, int):
                                sp.wait_ge(sem("low_max_scores"), UNITS * (l + 1) - 2 * G * (1 - b))
                            else:
                                plain_wait(sp, sem("low_pv_done"), it * UBODY + (UNITS * l + 2 * G * (b - 1)))
                            k_load(it * 2 + b, b)
                            sp.dma_start(vbuf[:, b].rearrange("p g h w -> p (g h w)"),
                                         vst[l, bass.ds(it * 2 + b, 1)].rearrange("o p n -> p (o n)")
                                         ).then_inc(v_landed[b], 16)
                    sweep_loop(sp, max_k_loads, True, False)
                    sweep_loop(sp, kv_loads, True, False)
                for s in range(SWEEPS[L] if L < 2 else 0):
                    n = SWEEP0[L] + s

                    def max_loads(it):
                        for b in range(2):
                            g = it * 2 + b
                            plain_wait(sp, sem("max_scores_ready"), it * BODY + (TILES * n + G * (b - 1)))
                            sp.dma_start(sbuf1[:, b], stream[bass.ds(g, 1), :, :, 0:S_P1].rearrange(
                                "o p g w -> p (o g) w")).then_inc(p1_landed[b], 16)

                    def pv_loads(it):
                        for b in range(2):
                            g = it * 2 + b
                            if isinstance(it, int) and it == 0 and s == 0 and L > 0:
                                sp.wait_ge(sem("attn_done"), L)
                            plain_wait(sp, sem("pv_done"), it * BODY + (TILES * n + G * (b - 1)))
                            sp.dma_start(sbuf2[:, b], stream[bass.ds(g, 1)].rearrange(
                                "o p g w -> p (o g) w")).then_inc(p2_landed[b], 16)
                    sweep_loop(sp, max_loads, n == 0, False)
                    sweep_loop(sp, pv_loads, s == 0, False)
                if L + 1 < layers:
                    sp.wait_ge(sem("xattn_done"), L + 1)
                    load_xw(sp, L + 1)
                if L == 3 and has(1, L):
                    sp.wait_ge(sem("xattn_done"), L + 1)
                    for d, s in rel_loads:
                        sp.dma_start(d, s).then_inc(sem("rel_landed"), 16)
                if has(1, L) and L + 1 < layers:
                    sp.wait_ge(sem("attn_done"), L + 1)
                    load_aw(sp, L + 1)
                if has(2, L):
                    if L == 2:
                        load_ring2_loop(sp)
                        load_ring(sp, 2, 64)
                    else:
                        for e in range(RING, NE[L]):
                            load_ring(sp, L, e)
                    if L + 1 < LAYERS and has(2, L + 1):
                        for e in range(RING):
                            load_ring(sp, L + 1, e)
            sp.wait_ge(sem("x_final"), 1)
            sp.dma_start(out, x[:]).then_inc(sem("out_written"), 16)
            sp.wait_ge(sem("out_written"), 16)

        @block.gpsimd
        def _(pool):
            g = nc.gpsimd
            chain = [0]

            def link(ins):
                chain[0] += 1
                ins.then_inc(sem("pool_chain"), 1)
                pool.wait_ge(sem("pool_chain"), chain[0])
            link(g.memset(ident[:], 0.0))
            link(g.affine_select(out=ident[:], in_=ident[:], compare_op=ALU.not_equal, fill=1.0, base=0,
                                 pattern=[[-1, P]], channel_multiplier=1))
            link(g.memset(ones[:], 1.0))
            link(g.memset(zrow[:], 0.0))
            link(g.memset(onesb[:], 1.0))
            link(g.memset(vstage, 1.0))
            link(g.memset(sbuf2[CB:P, :, :, S_D:S_D + P], 0.0))
            link(g.memset(sbuf2[BIAS_HI:BIAS_HI + 1, :, :, S_D:S_D + P], 1.0))
            link(g.memset(sbuf2[BIAS_LO:BIAS_LO + 1, :, :, S_D:S_D + P], 1.0))
            g.memset(sbuf2[:, :, :, S_ONE:S_ONE + 2], 1.0).then_inc(sem("consts_made"), 1)
            pool.wait_ge(sem("consts_made"), 1)

            pool.wait_ge(sem("keep_ready"), 1)
            link(g.partition_all_reduce(alive[:], any_keep[:], P, RMAX))
            g.memset(nan1[:], 0.0).then_inc(sem("alive_ready"), 1)
            pool.wait_ge(sem("alive_ready"), 1)

            def rows(it):
                for b in range(2):
                    n = it * 2 + b
                    pool.wait_ge(sem("act_rows"), n + 1)
                    g.tensor_tensor(sbuf2[:, b, :, S_L:S_L + C], ctx_in[:, b], sbuf2[:, b, :, S_R:S_R + C],
                                    ALU.subtract).then_inc(sem("pool_split"), 1)
            sweep_loop(pool, rows, True, False)

            H2 = P // 2
            for w in windows:
                link(g.memset(w[:], 0.0))
            for w in (win_causal, win_band):
                link(g.affine_select(out=w[:], in_=w[:], compare_op=ALU.is_ge, fill=NEG_ATTN, base=0,
                                     pattern=[[-1, P]], channel_multiplier=1))
            link(g.memset(win_block[0:H2, H2:P], NEG_ATTN))
            link(g.memset(win_block[H2:P, 0:H2], NEG_ATTN))
            link(g.memset(win_causal[H2:P, 0:H2], NEG_ATTN))
            g.affine_select(out=win_band[:], in_=win_band[:], compare_op=ALU.is_ge, fill=NEG_ATTN, base=H2 - 1,
                            pattern=[[1, P]], channel_multiplier=-1).then_inc(sem("windows_ready"), 1)
            pool.wait_ge(sem("windows_ready"), 1)

            def low_pool(L):
                l = L - 2
                pool.wait_ge(sem("attn_done"), L)
                g.memset(kbuf[96:P], 1.0).then_inc(sem("key_ones"), 1)
                pool.wait_ge(sem("key_ones"), l + 1)
                if L == 2:
                    pool.wait_ge(sem("low_max_merged"), 1)
                else:
                    pool.wait_ge(sem("low_max_taken"), UNITS * (l + 1))
                g.partition_all_reduce(maxl, p32[:, 0:2].rearrange("p a n -> p (a n)"), P, RMAX
                                       ).then_inc(sem("low_max_ready"), 1)
                pool.wait_ge(sem("low_max_ready"), l + 1)
                base = UNITS * l

                def units(it):
                    for u in range(UBODY):
                        at = it * UBODY + (base + u)
                        pool.wait_ge(sem("low_hi_ready"), at + 1)
                        g.tensor_tensor(plo[:, u % SLOTS], p32[:, u % SLOTS], phi[:, u % SLOTS], ALU.subtract
                                        ).then_inc(sem("low_lo_ready"), 1)
                if L == 2:
                    sweep_loop(pool, units, False, False)
                    pool.wait_ge(sem("nan_local"), 1)
                    g.partition_all_reduce(nana[:], nan1[:], P, RMAX).then_inc(sem("nan_ready"), 1)

            for L in range(layers):
                for s in range(SWEEPS[L] if L < 2 else 0):
                    n = SWEEP0[L] + s
                    pool.wait_ge(sem("max_merged"), n + 1)
                    g.partition_all_reduce(maxall[:], runmax[:, 0, :], P, RMAX).then_inc(sem("max_ready"), 1)
                    if L == 1 and s == 0:
                        pool.wait_ge(sem("max_ready"), n + 1)
                        pool.wait_ge(sem("attn_done"), 1)
                        link(g.memset(win_block[:], 0.0))
                        g.affine_select(out=win_block[:], in_=win_block[:], compare_op=ALU.not_equal, fill=1.0,
                                        base=1 - P, pattern=[[1, P]], channel_multiplier=1
                                        ).then_inc(sem("reversal_ready"), 1)
                        pool.wait_ge(sem("reversal_ready"), 1)
                if L >= 2:
                    low_pool(L)

        @block.tensor
        def _(pe):
            t = nc.tensor

            def turn_x(s):
                pe.wait_ge(sem("xn_ready"), s + 1)
                for c in range(DC):
                    m = t.transpose(bank(0)[:, c * P:(c + 1) * P], xn[:, c * P:(c + 1) * P], ident[:])
                m.then_inc(sem("xnT_psum"), 1)
                pe.wait_ge(sem("xnT_ready"), s + 1)

            pe.wait_ge(sem("consts_made"), 1)
            def turn_ctx(g, b):
                pe.wait_ge(in_landed[b], (g - b) * 8 + 16)
                wait_count(pe, sem("dve_split"), g)
                wait_count(pe, sem("act_split"), g * 3)
                for k in range(G):
                    t.transpose(bank(0, 2)[:, k * P:(k + 1) * P], ctx_in[:, b, k, 0:P], ident[:])
                for k in range(G):
                    m = t.transpose(bank(2, 2)[0:CB, k * P:(k + 1) * P], ctx_in[:, b, k, P:C], ident[:])
                m.then_inc(sem("ctxT_psum"), 1)

            def project_ctx(g, b):
                pe.wait_ge(sem("dve_split"), g + 1)
                pe.wait_ge(sem("act_split"), g * 3 + 3)
                u = 0
                for mt in range(4):
                    for lo, hi in ((0, 4), (4, G)):
                        wait_count(pe, sem("proj_lo"), g * PROJ + (u - 2))
                        o = bank(5 + u % 3)[:, 0:(hi - lo) * P]
                        for i, (w, c) in enumerate(PIECES):
                            m = t.matmul(o, w[:, mt * P:(mt + 1) * P], sbuf2[:, b, lo:hi, c:c + P],
                                         start=(i == 0), stop=(i == len(PIECES) - 1))
                        m.then_inc(sem("proj_psum"), 1)
                        u += 1
                for k in range(G):
                    wait_count(pe, sem("proj_lo"), g * PROJ + (u - 2))
                    for i, (w, c) in enumerate(PIECES):
                        m = t.matmul(bank(5 + u % 3), sbuf2[:, b, k, c:c + P], w[:, 512:1024],
                                     start=(i == 0), stop=(i == len(PIECES) - 1))
                    m.then_inc(sem("proj_psum"), 1)
                    u += 1

            pe.wait_ge(sem("kv_pieces_ready"), 1)
            turn_ctx(0, 0)

            def prepare(it):
                last = isinstance(it, int) and it == ITERS - 1
                for b in range(2):
                    if not (last and b == 1):
                        turn_ctx(it * 2 + (b + 1), 1 - b)
                    project_ctx(it * 2 + b, b)
            sweep_loop(pe, prepare, True, True)

            def xattn(L):
                h_n, d = XH[L], XD[L]
                s_at = 3 * L
                turn_x(s_at)
                pe.wait_ge(xw_landed, xw_at[L])
                quads = h_n // 4
                for q in range(quads):
                    for j in range(4):
                        h = 4 * q + j
                        for c in range(DC):
                            m = t.matmul(bank(q)[0:d, j * P:(j + 1) * P], xwq[:, c, h * d:(h + 1) * d],
                                         xnT[:, c, :], start=(c == 0), stop=(c == DC - 1))
                    m.then_inc(sem("qT_psum"), 1)
                for s in range(SWEEPS[L]):
                    n = SWEEP0[L] + s
                    pe.wait_ge(sem("qT_ready"), sum(XH[:L]) // 4 + quads)
                    for j in range(HG):
                        h = HG * s + j
                        t.matmul(bank(4, 2)[:, j * P:(j + 1) * P], xwk[0:d, h, 0:P], qT[0:d, h, :],
                                 start=True, stop=True)
                    for j in range(HG):
                        h = HG * s + j
                        m = t.matmul(bank(6, 2)[0:CB + 1, j * P:(j + 1) * P], xwk[0:d, h, P:C + 1],
                                     qT[0:d, h, :], start=True, stop=True)
                    m.then_inc(sem("qk_psum"), 1)
                    pe.wait_ge(sem("q_hi_ready"), n + 1)
                    base = TILES * n

                    def max_tiles(it):
                        for k in range(BODY):
                            b = k // G
                            if k % G == 0:
                                pe.wait_ge(p1_landed[b], it * 16 + 16 * (ITERS * n + 1))
                            wait_count(pe, sem("max_taken"), it * BODY + (base + k - 1))
                            sc = bank(4 + 2 * (k % 2), 2)
                            for c, rhs in enumerate((qh_a, q_d1)):
                                for m2 in range(2):
                                    m = t.matmul(sc[:, m2 * BANK:(m2 + 1) * BANK],
                                                 sbuf1[:, b, k % G, c * P:(c + 1) * P],
                                                 rhs[:, m2 * BANK:(m2 + 1) * BANK], start=(c == 0), stop=(c == 1))
                            m.then_inc(sem("max_scores_ready"), 1)
                    sweep_loop(pe, max_tiles, n == 0, False)

                    pe.wait_ge(sem("q_all_ready"), n + 1)
                    for b in range(4):
                        t.matmul(bank(b), zrow[:, 0:P], zrow[:], start=True, stop=False, skip_group_check=True)

                    def scores(it, k):
                        b = k // G
                        if k % G == 0:
                            pe.wait_ge(p2_landed[b], it * 16 + 16 * (ITERS * n + 1))
                        wait_count(pe, sem("p32_ready"), it * BODY + (base + k - 1))
                        sc = bank(4 + 2 * (k % 2), 2)
                        v = sbuf2[:, b, k % G, :]
                        steps = [(S_A, qh_a), (S_A, ql_a), (S_C, qh_a), (S_B, q_bb), (S_D, q_d2)]
                        for i, (o, rhs) in enumerate(steps):
                            for m2 in range(2):
                                m = t.matmul(sc[:, m2 * BANK:(m2 + 1) * BANK], v[:, o:o + P],
                                             rhs[:, m2 * BANK:(m2 + 1) * BANK],
                                             start=(i == 0), stop=(i == len(steps) - 1))
                        m.then_inc(sem("scores_ready"), 1)

                    def pv(it, k):
                        b = k // G
                        pe.wait_ge(sem("p_ready"), it * BODY + (base + k + 1))
                        v = sbuf2[:, b, k % G, :]
                        for j in range(HG):
                            o = psf[:, j * 256:j * 256 + C + 1]
                            a = j * P
                            t.matmul(o, phi[:, k % 2, a:a + P], v[:, S_R:S_R + C + 1], start=False, stop=False,
                                     skip_group_check=True)
                            t.matmul(o[:, 0:C], phi[:, k % 2, a:a + P], v[:, S_L:S_L + C], start=False,
                                     stop=False, skip_group_check=True)
                            m = t.matmul(o, plo[:, k % 2, a:a + P], v[:, S_R:S_R + C + 1], start=False,
                                         stop=False, skip_group_check=True)
                        m.then_inc(sem("pv_done"), 1)

                    def pv_tiles(it):
                        last = isinstance(it, int) and it == ITERS - 1
                        for k in range(BODY):
                            if k < BODY - 1:
                                scores(it, k + 1)
                            elif not last:
                                scores(it + 1, 0)
                            pv(it, k)
                    scores(0, 0)
                    sweep_loop(pe, pv_tiles, n == 0, True)
                    pe.wait_ge(sem("o_rows_ready"), n + 1)
                q0 = sum(XH[:L]) // 4

                def turn_o(q):
                    if q >= 2:
                        pe.wait_ge(sem("oTa_ready"), q0 + q - 1)
                        pe.wait_ge(sem("oTb_ready"), q0 + q - 1)
                    for j in range(4):
                        t.transpose(bank(4 + q % 2)[:, j * P:(j + 1) * P], o_rows[:, 4 * q + j, 0:P], ident[:])
                    for j in range(4):
                        m = t.transpose(bank(6 + q % 2)[0:CB, j * P:(j + 1) * P], o_rows[:, 4 * q + j, P:C],
                                        ident[:])
                    m.then_inc(sem("oT_psum"), 1)

                def values(q):
                    pe.wait_ge(sem("oTa_ready"), q0 + q + 1)
                    pe.wait_ge(sem("oTb_ready"), q0 + q + 1)
                    if q >= 2:
                        pe.wait_ge(sem("avT_ready"), q0 + q - 1)
                    for j in range(4):
                        h = 4 * q + j
                        o = bank(q % 2)[0:d, j * P:(j + 1) * P]
                        t.matmul(o, xwva[:, h * d:(h + 1) * d], oT_a[:, q % 2, j * P:(j + 1) * P],
                                 start=True, stop=False)
                        m = t.matmul(o, xwvb[:, h * d:(h + 1) * d], oT_b[:, q % 2, j * P:(j + 1) * P],
                                     start=False, stop=True)
                    m.then_inc(sem("avT_psum"), 1)

                def project(q):
                    pe.wait_ge(sem("avT_ready"), q0 + q + 1)
                    for j in range(4):
                        h = 4 * q + j
                        m = t.matmul(bank(2)[:, 0:D], avT[0:d, q % 2, j * P:(j + 1) * P], xwo[0:d, h, :],
                                     start=(h == 0), stop=(h == h_n - 1))
                    m.then_inc(sem("wo_used"), 1)
                turn_o(0)
                for q in range(quads):
                    if q + 1 < quads:
                        turn_o(q + 1)
                    values(q)
                    project(q)
                pe.wait_ge(sem("xattn_done"), L + 1)

            def xattn_low(L):
                l = L - 2
                turn_x(3 * L)
                pe.wait_ge(xw_landed, xw_at[L])
                for j in range(WP):
                    for c in range(DC):
                        m = t.matmul(bank(4, 2)[:, j * P:(j + 1) * P],
                                     xwq[:, c, j * P:(j + 1) * P],
                                     xnT[:, c, :], start=(c == 0), stop=(c == DC - 1))
                m.then_inc(sem("low_q_psum"), 1)
                pe.wait_ge(sem("low_q_ready"), l + 1)
                pe.wait_ge(sem("key_ones"), l + 1)
                base = UNITS * l

                def pair_scores(b, k, half):
                    sc = bank(4 + 2 * half, 2)
                    for j in range(4):
                        m = t.matmul(sc[:, j * 256:(j + 1) * 256],
                                     kbuf[:, b, 4 * half + j, k * P:(k + 1) * P],
                                     mq[:, (4 * half + j) * 256:(4 * half + j + 1) * 256], start=True, stop=True)
                    return m

                def max_units(it):
                    for u in range(UBODY):
                        b, k, half = u // (2 * G), u // 2 % G, u % 2
                        if u % (2 * G) == 0:
                            pe.wait_ge(k_landed[b], it * 48 + 48 * (2 * ITERS * l + 1))
                        wait_count(pe, sem("low_max_taken"), it * UBODY + (base + u - 1))
                        pair_scores(b, k, half).then_inc(sem("low_max_scores"), 1)
                sweep_loop(pe, max_units, l == 0, False)

                pe.wait_ge(sem("low_max_taken"), base + UNITS)
                if L == 3:
                    pe.wait_ge(sem("low_q_shifted"), 1)
                for b in range(4 if L == 2 else 2):
                    t.matmul(bank(b), zrow[:, 0:P], zrow[:], start=True, stop=False, skip_group_check=True)
                freed = sem("low_clipped") if L == 2 else sem("low_exp_ready")

                def scores(it, u):
                    b, k, half = u // (2 * G), u // 2 % G, u % 2
                    if u % (2 * G) == 0:
                        pe.wait_ge(k_landed[b], it * 48 + 48 * (2 * ITERS * l + ITERS + 1))
                    wait_count(pe, freed, it * UBODY + ((0 if L == 2 else base) + u - 1))
                    pair_scores(b, k, half).then_inc(sem("low_scores"), 1)

                def pv(it, u):
                    b, k, half = u // (2 * G), u // 2 % G, u % 2
                    if u % (2 * G) == 0:
                        pe.wait_ge(v_landed[b], it * 16 + 16 * (ITERS * l + 1))
                    pe.wait_ge(sem("low_lo_ready"), it * UBODY + (base + u + 1))
                    if L == 2 and half == 0:
                        for q in range(2):
                            t.matmul(bank(2 + q)[:, 0:8 * VW], onesb[:],
                                     vbuf[:, b, k, 8 * q:8 * q + 8, :].rearrange("p h w -> p (h w)"),
                                     start=False, stop=False, skip_group_check=True)
                    for j in range(HG):
                        o = bank(half)[:, j * 64:j * 64 + VW - 1]
                        v = vbuf[:, b, k, HG * half + j, :]
                        t.matmul(o, phi[:, u % SLOTS, j * P:(j + 1) * P], v[:, 0:VW - 1], start=False,
                                 stop=False, skip_group_check=True)
                        m = t.matmul(o[:, 0:WH + 1], plo[:, u % SLOTS, j * P:(j + 1) * P], v[:, 0:WH + 1],
                                     start=False, stop=False, skip_group_check=True)
                    m.then_inc(sem("low_pv_done"), 1)

                def units(it):
                    last = isinstance(it, int) and it == ITERS - 1
                    for u in range(UBODY):
                        if u + LEAD < UBODY:
                            scores(it, u + LEAD)
                        elif not last:
                            scores(it + 1, u + LEAD - UBODY)
                        pv(it, u)
                for u in range(LEAD):
                    scores(0, u)
                sweep_loop(pe, units, True, True)
                pe.wait_ge(sem("low_o_ready"), l + 1)
                for c in range(DC):
                    m = t.transpose(bank(5)[:, c * P:(c + 1) * P], a_o[:, c * P:(c + 1) * P], ident[:])
                m.then_inc(sem("low_oT_psum"), 1)
                pe.wait_ge(sem("low_oT_ready"), l + 1)
                for c in range(DC):
                    m = t.matmul(bank(6)[:, 0:D], a_oT[:, c, :], xwo2[:, c, :], start=(c == 0), stop=(c == DC - 1))
                m.then_inc(sem("low_out_psum"), 1)
                pe.wait_ge(sem("xattn_done"), L + 1)

            def attn(L):
                parts, d, heads = AH[L], AD[L], AS[L]
                turn_x(3 * L + 1)
                pe.wait_ge(aw_landed, aw_at[L])
                kv_in = xnT
                if L == 3:
                    pe.wait_ge(sem("reversal_ready"), 1)
                    for c in range(DC):
                        m = t.matmul(bank(1)[:, c * P:(c + 1) * P], xn[:, c * P:(c + 1) * P], win_block[:],
                                     start=True, stop=True)
                    m.then_inc(sem("xnT_rev_psum"), 1)
                    pe.wait_ge(sem("xnT_rev_ready"), 1)
                    kv_in = xnT_rev
                for w, first_bank in ((0, 0), (1, 4)):
                    for h in range(parts):
                        for c in range(DC):
                            m = t.matmul(bank(first_bank, 4)[0:d, h * P:(h + 1) * P],
                                         aw[:, c, w * D + h * d:w * D + (h + 1) * d], (kv_in if w else xnT)[:, c, :],
                                         start=(c == 0), stop=(c == DC - 1))
                    m.then_inc(sem("attn_qk_psum"), 1)
                pe.wait_ge(sem("attn_k_ready"), L + 1)
                for c in range(DC):
                    m = t.matmul(bank(7)[:, 0:D], kv_in[:, c, :], aw[:, c, 2 * D:3 * D], start=(c == 0),
                                 stop=(c == DC - 1))
                m.then_inc(sem("attn_v_psum"), 1)
                pe.wait_ge(sem("attn_q_ready"), L + 1)
                per = parts // heads
                for h in range(heads):
                    for c in range(per):
                        g = h * per + c
                        m = t.matmul(bank(0, 4)[:, h * P:(h + 1) * P], a_q[0:d, g * P:(g + 1) * P],
                                     a_k[0:d, g * P:(g + 1) * P], start=(c == 0), stop=(c == per - 1))
                m.then_inc(sem("attn_scores"), 1)
                pe.wait_ge(sem("attn_probs"), L + 1)
                for h in range(heads):
                    m = t.transpose(bank(0, 4)[:, h * P:(h + 1) * P], a_S[:, h * P:(h + 1) * P], ident[:])
                m.then_inc(sem("attn_pT_psum"), 1)
                pe.wait_ge(sem("attn_pT_ready"), L + 1)
                pe.wait_ge(sem("attn_v_ready"), L + 1)
                w = D // heads
                for h in range(heads):
                    m = t.matmul(bank(4)[:, h * w:(h + 1) * w], a_T[:, h * P:(h + 1) * P],
                                 a_v[:, h * w:(h + 1) * w], start=True, stop=True)
                m.then_inc(sem("attn_o_psum"), 1)
                pe.wait_ge(sem("attn_o_ready"), L + 1)
                for c in range(DC):
                    m = t.transpose(bank(5)[:, c * P:(c + 1) * P], a_o[:, c * P:(c + 1) * P], ident[:])
                m.then_inc(sem("attn_oT_psum"), 1)
                pe.wait_ge(sem("attn_oT_ready"), L + 1)
                for c in range(DC):
                    m = t.matmul(bank(6)[:, 0:D], a_oT[:, c, :], aw[:, c, 3 * D:4 * D], start=(c == 0),
                                 stop=(c == DC - 1))
                m.then_inc(sem("attn_out_psum"), 1)
                pe.wait_ge(sem("attn_done"), L + 1)

            def route(L, e):
                turn_x(3 * L + 2)
                if L == 0:
                    pe.wait_ge(const_landed, CONSTS_ALL - 16 * EARLY)
                for c in range(DC):
                    m = t.matmul(bank(1)[:, 0:e], xnT[:, c, :], rw[:, L, c, 0:e], start=(c == 0), stop=(c == DC - 1))
                m.then_inc(sem("logits_psum"), 1)

            def glu_experts(L, base):
                f = FW[L]
                fc = f // 2
                t.matmul(bank(2)[:, 0:D], zrow[:, 0:P], zrow[:, 0:D], start=True, stop=False,
                         skip_group_check=True)

                def gate_up(slot, landed, count, par, free):
                    pe.wait_ge(ring_landed[slot], landed)
                    wait_count(pe, sem("h_ready"), free)
                    v = gu_view(slot, f)
                    for half in range(2):
                        for c in range(DC):
                            m = t.matmul(bank(4 + 2 * par + half)[:, 0:f], xnT[:, c, :],
                                         v[:, c, half * f:(half + 1) * f], start=(c == 0), stop=(c == DC - 1))
                    m.then_inc(sem("gu_psum"), 1)

                def down(slot, par, h_at):
                    pe.wait_ge(sem("h_ready"), h_at)
                    for c in range(2):
                        m = t.transpose(bank(par)[0:fc, c * P:(c + 1) * P], h_s[:, par, c * fc:(c + 1) * fc],
                                        ident[:])
                    m.then_inc(sem("hT_psum"), 1)
                    pe.wait_ge(sem("hT_ready"), h_at)
                    dn = dn_view(slot, f)
                    for c in range(2):
                        m = t.matmul(bank(2)[:, 0:D], hT[0:fc, par, c * P:(c + 1) * P], dn[:, c, :],
                                     start=False, stop=False, skip_group_check=True)
                    m.then_inc(sem("ring_used"), 1)
                return gate_up, down

            GLU0 = [0, 0, NE[0], 0]

            def ffn_glu(L):
                route(L, 8 if L == 0 else 64)
                gate_up, down = glu_experts(L, GLU0[L])
                b0 = GLU0[L]
                n_e = NE[L]

                def slot_of(e):
                    return (NE0[L] + e) % RING
                if L == 0:
                    gate_up(slot_of(0), landed_at(L, 0), 0, 0, b0 - 1)
                    for e in range(n_e):
                        if e + 1 < n_e:
                            gate_up(slot_of(e + 1), landed_at(L, e + 1), 0, (e + 1) % 2, b0 + e)
                        down(slot_of(e), e % 2, b0 + e + 1)
                else:
                    step = 16 * RING_DMAS[L]
                    gate_up(slot_of(0), landed_at(L, 0), 0, 0, b0 - 1)
                    with pe.Fori(0, 16) as it:
                        for j in range(RING):
                            gate_up(slot_of(j + 1), it * step + landed_at(L, j + 1), 0, (j + 1) % 2,
                                    it * RING + (b0 + j))
                            down(slot_of(j), j % 2, it * RING + (b0 + j + 1))
                    down(slot_of(64), 0, b0 + 65)
                pe.wait_ge(sem("ffn_done"), L + 1)

            def ffn1():
                route(1, 32)
                for e in range(NE[1]):
                    pe.wait_ge(ring_landed[(NE0[1] + e) % RING], landed_at(1, e))
                    if e >= 2:
                        pe.wait_ge(sem("l1_step"), 2 * (e - 1))
                    v = gu_view((NE0[1] + e) % RING, 256)
                    for c in range(DC):
                        m = t.matmul(bank(4 + e % 2), xnT[:, c, :], v[:, c, :], start=(c == 0), stop=(c == DC - 1))
                    m.then_inc(sem("ring_used"), 1)
                pe.wait_ge(sem("ffn_done"), 2)

            def ffn3():
                pe.wait_ge(sem("csq_ready"), 1)
                for c in range(DC):
                    m = t.matmul(bank(3)[:, 0:8], ones[:], csq[:, c, :], start=(c == 0), stop=(c == DC - 1))
                m.then_inc(sem("cnorm_psum"), 1)
                route(3, 16)
                pe.wait_ge(sem("comb_ready"), 1)
                t.transpose(bank(2)[0:8, 0:P], comb[:, 0:8], ident[:]).then_inc(sem("gT_psum"), 1)
                pe.wait_ge(sem("gT_ready"), 1)
                t.matmul(bank(3)[:, 0:D], gT, b2r[:], start=True, stop=True).then_inc(sem("b2_psum"), 1)

                def up(e):
                    slot = (NE0[3] + e) % RING
                    pe.wait_ge(ring_landed[slot], landed_at(3, e))
                    if e >= 2:
                        pe.wait_ge(sem("gelu_ready"), e - 1)
                    w1 = ring[:, slot, 0:DC * P].rearrange("p (c n) -> p c n", c=DC)
                    for c in range(DC):
                        m = t.matmul(bank(4 + e % 2)[:, 0:P], w1[:, c, :], xnT[:, c, :], start=(c == 0),
                                     stop=(c == DC - 1))
                    m.then_inc(sem("w1_psum"), 1)

                def down(e):
                    slot = (NE0[3] + e) % RING
                    pe.wait_ge(sem("gelu_ready"), e + 1)
                    if e >= 2:
                        pe.wait_ge(sem("l3_taken"), e - 1)
                    t.matmul(bank(6 + e % 2)[:, 0:D], hT[:, e % 2, 0:P], ring[:, slot, 1024:1024 + D],
                             start=True, stop=True).then_inc(sem("ring_used"), 1)
                up(0)
                for e in range(8):
                    if e < 7:
                        up(e + 1)
                    down(e)

            for s in range(stages):
                L = s // 3
                if s % 3 == 0:
                    (xattn if L < 2 else xattn_low)(L)
                elif s % 3 == 1:
                    attn(L)
                elif L in (0, 2):
                    ffn_glu(L)
                elif L == 1:
                    ffn1()
                else:
                    ffn3()

        @block.scalar
        def _(act):
            a = nc.scalar

            def std(s):
                act.wait_ge(sem("var_ready"), s + 1)
                a.activation(rstd[:], rstd[:], ACT.Sqrt).then_inc(sem("std_ready"), 1)

            def split_ctx(g, b):
                act.wait_ge(sem("ctxT_psum"), g + 1)
                wait_count(act, stream_out[b], (g - b) * 8)
                a.activation(sbuf2[:, b, :, S_A:S_A + P],
                             bank(0, 2)[:, 0:GK].rearrange("p (g k) -> p g k", g=G), ACT.Copy
                             ).then_inc(sem("act_split"), 1)
                a.activation(sbuf2[0:CB, b, :, S_B:S_B + P],
                             bank(2, 2)[0:CB, 0:GK].rearrange("p (g k) -> p g k", g=G), ACT.Copy
                             ).then_inc(sem("act_split"), 1)
                a.activation(sbuf2[0:CB, b, :, S_D:S_D + P],
                             bank(2, 2)[0:CB, 0:GK].rearrange("p (g k) -> p g k", g=G), ACT.Copy
                             ).then_inc(sem("act_split"), 1)
                a.activation(sbuf2[:, b, :, S_R:S_R + C], ctx_in[:, b], ACT.Copy).then_inc(sem("act_rows"), 1)

            def proj_high(g):
                u = 0
                wait_count(act, sem("keys_written"), g * 64)
                for mt in range(4):
                    for lo, hi in ((0, 4), (4, G)):
                        act.wait_ge(sem("proj_psum"), g * PROJ + (u + 1))
                        a.activation(kstage[:, mt, 0, lo * P:hi * P], bank(5 + u % 3)[:, 0:(hi - lo) * P], ACT.Copy
                                     ).then_inc(sem("proj_hi"), 1)
                        u += 1
                wait_count(act, sem("values_written"), g * 32)
                for k in range(G):
                    act.wait_ge(sem("proj_psum"), g * PROJ + (u + 1))
                    a.activation(vstage[:, :, k, :, 0:WH],
                                 bank(5 + u % 3).rearrange("p (l h w) -> p l h w", l=2, h=WH), ACT.Copy
                                 ).then_inc(sem("proj_hi"), 1)
                    u += 1
            split_ctx(0, 0)

            def prepare(it):
                last = isinstance(it, int) and it == ITERS - 1
                for b in range(2):
                    if not (last and b == 1):
                        split_ctx(it * 2 + (b + 1), 1 - b)
                    proj_high(it * 2 + b)
            sweep_loop(act, prepare, True, True)

            def xattn_low(L):
                l = L - 2
                base = UNITS * l

                def units(it):
                    for u in range(UBODY):
                        at = it * UBODY + (base + u)
                        sl = p32[:, u % SLOTS]
                        if L == 2:
                            act.wait_ge(sem("low_shifted"), at + 1)
                            a.activation(sl, sl, ACT.Exp).then_inc(sem("low_exp_ready"), 1)
                            act.wait_ge(sem("low_exp_ready"), at + 1)
                            wait_count(act, sem("low_pv_done"), at + (1 - SLOTS))
                            a.activation(phi[:, u % SLOTS], sl, ACT.Copy).then_inc(sem("low_hi_ready"), 1)
                        else:
                            act.wait_ge(sem("low_scores"), at + 1)
                            act.wait_ge(sem("low_lo_ready"), at + (1 - SLOTS))
                            a.activation(sl, bank(4 + 2 * (u % 2), 2), ACT.Exp).then_inc(sem("low_exp_ready"), 1)
                sweep_loop(act, units, L == 2, False)

            def xattn(L):
                h_n, d = XH[L], XD[L]
                for s in range(SWEEPS[L]):
                    n = SWEEP0[L] + s
                    act.wait_ge(sem("qk_psum"), n + 1)
                    sc = d ** -0.5
                    if L == 0:
                        act.wait_ge(sem("qscale_ready"), 1)
                    a.activation(qf_a[:], bank(4, 2), ACT.Copy if L else ACT.Identity,
                                 scale=sc if L else qscale0[:, 0:1]).then_inc(sem("qf_ready"), 1)
                    a.activation(qf_b[0:CB + 1, :], bank(6, 2)[0:CB + 1, :], ACT.Copy if L else ACT.Identity,
                                 scale=sc if L else qscale0[0:CB + 1, 0:1]).then_inc(sem("qf_ready"), 1)
                    base = TILES * n

                    def exps(it):
                        for k in range(BODY):
                            act.wait_ge(sem("scores_ready"), it * BODY + (base + k + 1))
                            src = bank(4 + 2 * (k % 2), 2)
                            wait_count(act, sem("p_ready"), it * BODY + (base + k - 1))
                            bias = maskneg[:, bass.ds(it * BODY + k, 1)] if L == 0 else 0.0
                            a.activation(p32[:, k % 2], src, ACT.Exp, bias=bias).then_inc(sem("p32_ready"), 1)
                    sweep_loop(act, exps, n == 0, False)
                q0 = sum(XH[:L]) // 4
                for q in range(h_n // 4):
                    act.wait_ge(sem("oT_psum"), q0 + q + 1)
                    if q >= 2:
                        act.wait_ge(sem("avT_psum"), q0 + q - 1)
                    a.activation(oT_b[:, q % 2, :], bank(6 + q % 2)[0:CB, :], ACT.Copy).then_inc(sem("oTb_ready"), 1)

            def attn(L):
                n = AS[L] * P
                if L == 2:
                    act.wait_ge(sem("l2_scaled"), 1)
                    a.activation(a_T, a_S, ACT.Sigmoid).then_inc(sem("l2_act"), 1)
                    act.wait_ge(sem("l2_act"), 1)
                    a.activation(a_T, a_T, ACT.Square).then_inc(sem("l2_act"), 1)
                    act.wait_ge(sem("l2_centred"), 1)
                    a.activation(a_U, a_U, ACT.Abs).then_inc(sem("l2_act"), 1)
                act.wait_ge(sem("attn_shifted"), L + 1)
                a.activation(a_S[:, 0:n], a_S[:, 0:n], ACT.Exp).then_inc(sem("attn_probs"), 1)
                act.wait_ge(sem("attn_pT_psum"), L + 1)
                a.activation(a_T[:, 0:n], bank(0, 4)[:, 0:n], ACT.Copy).then_inc(sem("attn_pT_ready"), 1)

            def ffn_glu(L):
                f = FW[L]
                act.wait_ge(sem("route_shifted"), L + 1)
                a.activation(prob[:, 0:8 if L == 0 else 64], logit[:, 0:8 if L == 0 else 64], ACT.Exp
                             ).then_inc(sem("route_exp"), 1)
                b0 = 0 if L == 0 else NE[0]

                def one(par, at):
                    act.wait_ge(sem("gu_psum"), at)
                    wait_count(act, sem("h_ready"), at - 2)
                    a.activation(g_s[:, par, 0:f], bank(4 + 2 * par)[:, 0:f], ACT.Silu).then_inc(sem("silu"), 1)
                if L == 0:
                    for e in range(NE[0]):
                        one(e % 2, e + 1)
                else:
                    with act.Fori(0, 16) as it:
                        for j in range(RING):
                            one(j % 2, it * RING + (b0 + j + 1))
                    one(0, b0 + 65)

            def ffn1():
                act.wait_ge(sem("route_shifted"), 2)
                a.activation(prob[:, 0:32], logit[:, 0:32], ACT.Exp).then_inc(sem("route_exp"), 1)

            def ffn3():
                act.wait_ge(sem("cnorm_psum"), 1)
                a.activation(cnorm[:], bank(3)[:, 0:8], ACT.Sqrt).then_inc(sem("norms_ready"), 1)
                act.wait_ge(sem("xsq_ready"), 1)
                a.activation(rsum[:], rsum[:], ACT.Sqrt).then_inc(sem("norms_ready"), 1)
                act.wait_ge(sem("route_shifted"), 4)
                a.activation(prob[:, 0:8], logit[:, 0:8], ACT.Exp).then_inc(sem("route_exp"), 1)
                for e in range(8):
                    act.wait_ge(sem("w1_psum"), e + 1)
                    if e >= 2:
                        act.wait_ge(sem("ring_used"), NE0[3] + e - 1)
                    a.activation(hT[:, e % 2, 0:P], bank(4 + e % 2)[:, 0:P], ACT.Gelu, bias=b1T[:, e:e + 1]
                                 ).then_inc(sem("gelu_ready"), 1)

            for s in range(stages):
                L = s // 3
                std(s)
                if s % 3 == 0:
                    (xattn if L < 2 else xattn_low)(L)
                elif s % 3 == 1:
                    attn(L)
                elif L in (0, 2):
                    ffn_glu(L)
                elif L == 1:
                    ffn1()
                else:
                    ffn3()

        @block.vector
        def _(dve):
            v = nc.vector
            chain = [0]

            def link(ins):
                chain[0] += 1
                ins.then_inc(sem("dve_chain"), 1)
                dve.wait_ge(sem("dve_chain"), chain[0])

            def norm(s):
                link(v.bn_stats(stats[:], x[:]))
                link(v.bn_aggr(mv[:], stats[:]))
                v.tensor_scalar(rstd[:], mv[:, 1:2], EPS, None, ALU.add).then_inc(sem("var_ready"), 1)
                dve.wait_ge(sem("std_ready"), s + 1)
                link(v.reciprocal(rstd[:], rstd[:]))
                v.tensor_scalar(xn[:], x[:], mv[:, 0:1], rstd[:, 0:1], ALU.subtract, ALU.mult
                                ).then_inc(sem("xn_ready"), 1)
                dve.wait_ge(sem("xnT_psum"), s + 1)
                v.tensor_copy(xnT[:].rearrange("p c n -> p (c n)"), bank(0)[:, 0:D]).then_inc(sem("xnT_ready"), 1)
                dve.wait_ge(sem("xnT_ready"), s + 1)

            link(v.memset(q_d1[:], 0.0))
            link(v.memset(q_d2[:], 0.0))
            dve.wait_ge(sem("early_landed"), 16 * EARLY)
            link(v.tensor_copy(keep[:], keep_u8[:]))
            link(v.tensor_scalar(keep[:], keep[:], 0.0, None, ALU.is_gt))
            v.tensor_reduce(any_keep[:], keep[:], AX_X, ALU.max).then_inc(sem("keep_ready"), 1)
            dve.wait_ge(sem("alive_ready"), 1)
            v.tensor_scalar(qscale0[:], alive[:], XD[0] ** -0.5, None, ALU.mult).then_inc(sem("qscale_ready"), 1)
            link(v.tensor_scalar(maskneg[:], keep[:], -NEG, NEG, ALU.mult, ALU.add))
            link(v.tensor_scalar(maskneg[:], maskneg[:], alive[:, 0:1], None, ALU.mult))

            def split_weights():
                link(v.tensor_copy(qh_a[:], qf_a[:]))
                v.tensor_tensor(ql_a[:], qf_a[:], qh_a[:], ALU.subtract)
                v.tensor_copy(q_bb[0:CB, :], qf_b[0:CB, :])
                v.tensor_copy(q_bb[CB:P, :], qf_b[0:CB, :])
                link(v.tensor_copy(q_d1[0:CB + 1, :], qf_b[0:CB + 1, :]))
                v.tensor_tensor(q_d2[0:CB, :], qf_b[0:CB, :], q_d1[0:CB, :], ALU.subtract)
                v.tensor_copy(q_d2[BIAS_HI:BIAS_HI + 1, :], q_d1[BIAS_HI:BIAS_HI + 1, :])
                v.tensor_tensor(q_d2[BIAS_LO:BIAS_LO + 1, :], qf_b[BIAS_HI:BIAS_HI + 1, :],
                                q_d1[BIAS_HI:BIAS_HI + 1, :], ALU.subtract).then_inc(sem("kv_pieces_ready"), 1)
            dve.wait_ge(sem("kv_weights_landed"), 32)
            split_weights()
            dve.wait_ge(sem("consts_made"), 1)
            by_half = ident[:].rearrange("p (a b c) -> p b a c", a=4, b=2)
            v.tensor_reduce(half_a[:], by_half[:, 0], mybir.AxisListType.XY, ALU.add)
            v.tensor_reduce(half_b[:], by_half[:, 1], mybir.AxisListType.XY, ALU.add)

            def split_ctx(g, b):
                dve.wait_ge(sem("act_split"), g * 3 + 1)
                v.tensor_tensor(sbuf2[:, b, :, S_C:S_C + P],
                                bank(0, 2)[:, 0:GK].rearrange("p (g k) -> p g k", g=G),
                                sbuf2[:, b, :, S_A:S_A + P], ALU.subtract)
                dve.wait_ge(sem("act_split"), g * 3 + 3)
                v.tensor_tensor(sbuf2[CB:P, b, :, S_B:S_B + P],
                                bank(2, 2)[0:CB, 0:GK].rearrange("p (g k) -> p g k", g=G),
                                sbuf2[0:CB, b, :, S_B:S_B + P], ALU.subtract).then_inc(sem("dve_split"), 1)

            def proj_low(g):
                u = 0
                for mt in range(4):
                    for lo, hi in ((0, 4), (4, G)):
                        dve.wait_ge(sem("proj_hi"), g * PROJ + (u + 1))
                        v.tensor_tensor(kstage[:, mt, 1, lo * P:hi * P], bank(5 + u % 3)[:, 0:(hi - lo) * P],
                                        kstage[:, mt, 0, lo * P:hi * P], ALU.subtract
                                        ).then_inc(sem("proj_lo"), 1)
                        u += 1
                for k in range(G):
                    dve.wait_ge(sem("proj_hi"), g * PROJ + (u + 1))
                    v.tensor_tensor(vstage[:, :, k, :, WH + 1:2 * WH + 1],
                                    bank(5 + u % 3).rearrange("p (l h w) -> p l h w", l=2, h=WH),
                                    vstage[:, :, k, :, 0:WH], ALU.subtract).then_inc(sem("proj_lo"), 1)
                    u += 1
            split_ctx(0, 0)

            def prepare(it):
                last = isinstance(it, int) and it == ITERS - 1
                for b in range(2):
                    if not (last and b == 1):
                        split_ctx(it * 2 + (b + 1), 1 - b)
                    proj_low(it * 2 + b)
            sweep_loop(dve, prepare, True, True)
            dve.wait_ge(sem("keys_written"), 64 * GROUPS)
            dve.wait_ge(sem("values_written"), 32 * GROUPS)
            dve.wait_ge(const_landed, CONSTS_ALL - 16 * EARLY)

            def xattn(L):
                h_n, d = XH[L], XD[L]
                quads = h_n // 4
                q0 = sum(XH[:L]) // 4
                norm(3 * L)
                for q in range(quads):
                    dve.wait_ge(sem("qT_psum"), q0 + q + 1)
                    o = qT[0:d, 4 * q:4 * q + 4, :]
                    i = bank(q)[0:d, :].rearrange("p (h n) -> p h n", h=4)
                    v.tensor_copy(o, i).then_inc(sem("qT_ready"), 1)
                for s in range(SWEEPS[L]):
                    n = SWEEP0[L] + s
                    base = TILES * n
                    dve.wait_ge(sem("qf_ready"), 2 * n + 1)
                    link(v.tensor_copy(qh_a[:], qf_a[:]))
                    v.tensor_tensor(ql_a[:], qf_a[:], qh_a[:], ALU.subtract)
                    dve.wait_ge(sem("qf_ready"), 2 * n + 2)
                    v.tensor_copy(q_bb[0:CB, :], qf_b[0:CB, :])
                    v.tensor_copy(q_bb[CB:P, :], qf_b[0:CB, :])
                    link(v.tensor_copy(q_d1[0:CB + 1, :], qf_b[0:CB + 1, :]))
                    v.tensor_tensor(q_d2[0:CB, :], qf_b[0:CB, :], q_d1[0:CB, :], ALU.subtract)
                    v.tensor_tensor(q_d1[BIAS_LO:BIAS_LO + 1, :], qf_b[BIAS_HI:BIAS_HI + 1, :],
                                    q_d1[BIAS_HI:BIAS_HI + 1, :], ALU.subtract).then_inc(sem("q_hi_ready"), 1)
                    link(v.memset(runmax[:], NEG))

                    def take_max(it):
                        for k in range(BODY):
                            dve.wait_ge(sem("max_scores_ready"), it * BODY + (base + k + 1))
                            wait_count(dve, sem("max_taken"), it * BODY + (base + k - 1))
                            if L == 0:
                                v.scalar_tensor_tensor(runmax[:, k % 2], bank(4 + 2 * (k % 2), 2),
                                                       maskneg[:, bass.ds(it * BODY + k, 1)], runmax[:, k % 2],
                                                       ALU.add, ALU.max).then_inc(sem("max_taken"), 1)
                            else:
                                v.tensor_tensor(runmax[:, k % 2], bank(4 + 2 * (k % 2), 2), runmax[:, k % 2],
                                                ALU.max).then_inc(sem("max_taken"), 1)
                    sweep_loop(dve, take_max, n == 0, False)
                    dve.wait_ge(sem("max_taken"), base + TILES)
                    v.tensor_tensor(runmax[:, 0], runmax[:, 0], runmax[:, 1], ALU.max
                                    ).then_inc(sem("max_merged"), 1)
                    dve.wait_ge(sem("max_ready"), n + 1)
                    hi = slice(BIAS_HI, BIAS_HI + 1)
                    link(v.tensor_tensor(qf_b[hi, :], qf_b[hi, :], maxall[hi, :], ALU.subtract))
                    link(v.tensor_copy(q_d2[hi, :], qf_b[hi, :]))
                    v.tensor_tensor(q_d2[BIAS_LO:BIAS_LO + 1, :], qf_b[hi, :], q_d2[hi, :],
                                    ALU.subtract).then_inc(sem("q_all_ready"), 1)

                    def split_p(it, k):
                        dve.wait_ge(sem("p32_ready"), it * BODY + (base + k + 1))
                        wait_count(dve, sem("pv_done"), it * BODY + (base + k - 1))
                        v.tensor_copy(phi[:, k % 2], p32[:, k % 2]).then_inc(sem("phi_ready"), 1)
                        dve.wait_ge(sem("phi_ready"), it * BODY + (base + k + 1))
                        v.tensor_tensor(plo[:, k % 2], p32[:, k % 2], phi[:, k % 2], ALU.subtract
                                        ).then_inc(sem("p_ready"), 1)

                    def p_tiles(it):
                        for k in range(BODY):
                            split_p(it, k)
                    sweep_loop(dve, p_tiles, n == 0, False)
                    dve.wait_ge(sem("pv_done"), base + TILES)
                    acc = bank(0, 4).rearrange("p (h n) -> p h n", h=HG)
                    dn = den[:, HG * s:HG * s + HG]
                    rd = rden[:, HG * s:HG * s + HG]
                    link(v.tensor_copy(dn, acc[:, :, C]))
                    link(v.reciprocal(rd, dn))
                    v.tensor_tensor(o_rows[:, HG * s:HG * s + HG, :], acc[:, :, 0:C],
                                    rd.unsqueeze(2).to_broadcast([P, HG, C]), ALU.mult
                                    ).then_inc(sem("o_rows_ready"), 1)
                for q in range(quads):
                    dve.wait_ge(sem("oT_psum"), q0 + q + 1)
                    if q >= 2:
                        dve.wait_ge(sem("avT_psum"), q0 + q - 1)
                    v.tensor_copy(oT_a[:, q % 2, :], bank(4 + q % 2)).then_inc(sem("oTa_ready"), 1)
                    dve.wait_ge(sem("avT_psum"), q0 + q + 1)
                    if q >= 2:
                        dve.wait_ge(sem("wo_used"), q0 + q - 1)
                    v.tensor_copy(avT[0:d, q % 2, :], bank(q % 2)[0:d, :]).then_inc(sem("avT_ready"), 1)
                link(v.tensor_tensor(x[:], x[:], bo_all[:, L, :], ALU.add))
                dve.wait_ge(sem("wo_used"), q0 + quads)
                v.tensor_tensor(x[:], bank(2)[:, 0:D], x[:], ALU.add).then_inc(sem("xattn_done"), 1)
                dve.wait_ge(sem("xattn_done"), L + 1)

            def xattn_low(L):
                l = L - 2
                base = UNITS * l
                norm(3 * L)
                q3 = qf_a[:].rearrange("p (j n) -> p j n", j=WP)
                mq4 = mq.rearrange("p (j b n) -> p j b n", j=WP, b=2)
                dve.wait_ge(sem("low_q_psum"), l + 1)
                link(v.tensor_tensor(q3, bank(4, 2).rearrange("p (j n) -> p j n", j=WP),
                                     xbq4[:, l, :].unsqueeze(2).to_broadcast([P, WP, P]), ALU.add))
                link(v.tensor_scalar(qf_a[:], qf_a[:], WH ** -0.5, None, ALU.mult))
                link(v.tensor_copy(qh_a[:], qf_a[:]))
                link(v.tensor_tensor(ql_a[:], qf_a[:], qh_a[:], ALU.subtract))
                for half, mine in ((0, half_a), (1, half_b)):
                    v.tensor_scalar(mq4[0:64, :, half, :], qh_a[0:64, :].rearrange("p (j n) -> p j n", j=WP),
                                    mine[0:64, 0:1], None, ALU.mult)
                    v.tensor_scalar(mq4[64:96, :, half, :], ql_a[64:96, :].rearrange("p (j n) -> p j n", j=WP),
                                    mine[64:96, 0:1], None, ALU.mult)
                v.memset(mq[96:P, :], 0.0).then_inc(sem("low_q_ready"), 1)
                link(v.memset(runmax, NEG))

                def take_max(it):
                    for u in range(UBODY):
                        dve.wait_ge(sem("low_max_scores"), it * UBODY + (base + u + 1))
                        wait_count(dve, sem("low_max_taken"), it * UBODY + (base + u - 1))
                        v.tensor_tensor(runmax[:, u % 2], bank(4 + 2 * (u % 2), 2), runmax[:, u % 2],
                                        ALU.max).then_inc(sem("low_max_taken"), 1)
                sweep_loop(dve, take_max, l == 0, False)
                dve.wait_ge(sem("low_max_taken"), base + UNITS)
                if L == 2:
                    v.tensor_scalar(runmax, runmax, CLAMP, -CLAMP, ALU.min, ALU.max
                                    ).then_inc(sem("low_max_merged"), 1)
                    dve.wait_ge(sem("low_max_ready"), 1)
                else:
                    dve.wait_ge(sem("low_max_ready"), 2)
                    r = slice(96, P)
                    th = qf_a[:].bitcast(BF16)[r, :]
                    tl = qf_b[:].bitcast(BF16)[r, :]
                    link(v.tensor_scalar(th, maxl[r, :], -1.0, None, ALU.mult))
                    link(v.scalar_tensor_tensor(tl, maxl[r, :], -1.0, th, ALU.mult, ALU.subtract))
                    link(v.tensor_scalar(mq[r, :], tl, ident[r, 97:98], None, ALU.mult))
                    v.scalar_tensor_tensor(mq[r, :], th, ident[r, 96:97], mq[r, :], ALU.mult, ALU.add
                                           ).then_inc(sem("low_q_shifted"), 1)
                    dve.wait_ge(sem("low_q_shifted"), 1)

                def units(it):
                    for u in range(UBODY):
                        at = it * UBODY + (base + u)
                        if L == 2:
                            dve.wait_ge(sem("low_scores"), at + 1)
                            wait_count(dve, sem("low_lo_ready"), at + (1 - SLOTS))
                            v.tensor_scalar(p32[:, u % SLOTS], bank(4 + 2 * (u % 2), 2), CLAMP, -CLAMP, ALU.min,
                                            ALU.max).then_inc(sem("low_clipped"), 1)
                            dve.wait_ge(sem("low_clipped"), at + 1)
                            v.tensor_tensor(p32[:, u % SLOTS], p32[:, u % SLOTS],
                                            maxl[:, (u % 2) * QC:(u % 2 + 1) * QC], ALU.subtract
                                            ).then_inc(sem("low_shifted"), 1)
                        else:
                            dve.wait_ge(sem("low_exp_ready"), at + 1)
                            dve.wait_ge(sem("low_pv_done"), at + (1 - SLOTS))
                            v.tensor_copy(phi[:, u % SLOTS], p32[:, u % SLOTS]).then_inc(sem("low_hi_ready"), 1)
                            dve.wait_ge(sem("low_hi_ready"), at + 1)
                            v.tensor_tensor(plo[:, u % SLOTS], p32[:, u % SLOTS], phi[:, u % SLOTS], ALU.subtract
                                            ).then_inc(sem("low_lo_ready"), 1)
                sweep_loop(dve, units, L == 2, False)
                dve.wait_ge(sem("low_pv_done"), base + UNITS)

                def joined(acc, dst):
                    d3 = dst.rearrange("p (h n) -> p h n", h=WH)
                    link(v.tensor_copy(d3, acc[:, :, WH + 1:2 * WH + 1]))
                    link(v.tensor_tensor(d3, acc[:, :, 0:WH], d3, ALU.add))
                    link(v.tensor_copy(den[:], acc[:, :, WH]))
                    link(v.reciprocal(rden[:], den[:]))
                    return v.tensor_tensor(d3, d3, rden[:].unsqueeze(2).to_broadcast([P, WH, WH]), ALU.mult)
                if L == 2:
                    for q in range(2):
                        sums = bank(2 + q)[:, 0:8 * VW].rearrange("p (h w) -> p h w", h=8)
                        v.tensor_copy(vsum[:, 8 * q:8 * q + 8, :], sums)
                    link(v.memset(a_m[:], 0.0))
                    link(joined(vsum, vmean))
                acc = bank(0, 2).rearrange("p (h w) -> p h w", h=WH)
                done = joined(acc, a_o)
                if L == 2:
                    link(done)
                    link(v.tensor_tensor(nanf[:], den[:], den[:], ALU.not_equal))
                    v.tensor_reduce(nan1[:], nanf[:], AX_X, ALU.max).then_inc(sem("nan_local"), 1)
                    dve.wait_ge(sem("nan_ready"), 1)
                    done = v.copy_predicated(a_o, nana[:, 0:1].bitcast(U32).to_broadcast([P, D]), vmean)
                done.then_inc(sem("low_o_ready"), 1)
                dve.wait_ge(sem("low_oT_psum"), l + 1)
                v.tensor_copy(a_oT.rearrange("p c n -> p (c n)"), bank(5)[:, 0:D]).then_inc(sem("low_oT_ready"), 1)
                link(v.tensor_tensor(x[:], x[:], bo_all[:, L, :], ALU.add))
                dve.wait_ge(sem("low_out_psum"), l + 1)
                v.tensor_tensor(x[:], bank(6)[:, 0:D], x[:], ALU.add).then_inc(sem("xattn_done"), 1)
                dve.wait_ge(sem("xattn_done"), L + 1)

            def attn(L):
                parts, d, heads = AH[L], AD[L], AS[L]
                n = heads * P
                norm(3 * L + 1)
                if L == 3:
                    dve.wait_ge(sem("xnT_rev_psum"), 1)
                    v.tensor_copy(xnT_rev.rearrange("p c n -> p (c n)"), bank(1)[:, 0:D]
                                  ).then_inc(sem("xnT_rev_ready"), 1)
                for w, (dst, bias, name) in enumerate(((a_q, abq, "attn_q_ready"), (a_k, abk, "attn_k_ready"))):
                    dve.wait_ge(sem("attn_qk_psum"), 2 * L + w + 1)
                    o = dst[0:d, 0:parts * P].rearrange("p (h n) -> p h n", h=parts)
                    i = bank(4 * w, 4)[0:d, 0:parts * P].rearrange("p (h n) -> p h n", h=parts)
                    if L == 2:
                        v.tensor_copy(o, i).then_inc(sem(name), 1)
                    else:
                        v.tensor_tensor(o, i, bias[0:d, L, 0:parts].unsqueeze(2).to_broadcast([d, parts, P]),
                                        ALU.add).then_inc(sem(name), 1)
                dve.wait_ge(sem("attn_v_psum"), L + 1)
                if L == 2:
                    v.tensor_copy(a_v, bank(7)[:, 0:D]).then_inc(sem("attn_v_ready"), 1)
                else:
                    v.tensor_tensor(a_v, bank(7)[:, 0:D], abv[:, L, :], ALU.add).then_inc(sem("attn_v_ready"), 1)
                dve.wait_ge(sem("attn_scores"), L + 1)
                S3 = a_S[:, 0:n].rearrange("p (h n) -> p h n", h=heads)
                U3 = a_U[:, 0:n].rearrange("p (h n) -> p h n", h=heads)
                B3 = bank(0, 4)[:, 0:n].rearrange("p (h n) -> p h n", h=heads)

                def per_head(t2):
                    return t2[:, 0:heads].unsqueeze(2).to_broadcast([P, heads, P])
                if L < 3:
                    dve.wait_ge(sem("windows_ready"), 1)
                    win = windows[L][:].unsqueeze(1).to_broadcast([P, heads, P])
                if L < 2:
                    link(v.scalar_tensor_tensor(S3, B3, ASCALE[L], win, ALU.mult, ALU.add))
                elif L == 3:
                    dve.wait_ge(sem("rel_landed"), 16 * len(rel_loads))
                    link(v.scalar_tensor_tensor(S3, B3, ASCALE[L], rel, ALU.mult, ALU.add))
                else:
                    v.tensor_scalar(a_S, bank(0, 4), ASCALE[2], None, ALU.mult).then_inc(sem("l2_scaled"), 1)
                    dve.wait_ge(sem("l2_scaled"), 1)
                    link(v.tensor_reduce(a_m[:, 0:heads], S3, AX_X, ALU.add))
                    link(v.tensor_scalar(a_m[:, 0:heads], a_m[:, 0:heads], 1.0 / P, None, ALU.mult))
                    v.tensor_tensor(U3, S3, per_head(a_m), ALU.subtract).then_inc(sem("l2_centred"), 1)
                    link(v.tensor_scalar(ngates[:], gates[:], -1.0, None, ALU.mult))
                    dve.wait_ge(sem("l2_act"), 2)
                    link(v.scalar_tensor_tensor(a_T, a_T, ngates[:, 0:1], a_S, ALU.mult, ALU.add))
                    link(v.scalar_tensor_tensor(a_T, a_S, gates[:, 1:2], a_T, ALU.mult, ALU.add))
                    dve.wait_ge(sem("l2_act"), 3)
                    link(v.scalar_tensor_tensor(a_S, a_U, ngates[:, 2:3], a_T, ALU.mult, ALU.add))
                    link(v.tensor_tensor(S3, S3, win, ALU.add))
                link(v.tensor_reduce(a_m[:, 0:heads], S3, AX_X, ALU.max))
                v.tensor_tensor(S3, S3, per_head(a_m), ALU.subtract).then_inc(sem("attn_shifted"), 1)
                dve.wait_ge(sem("attn_probs"), L + 1)
                link(v.tensor_reduce(a_s[:, 0:heads], S3, AX_X, ALU.add))
                link(v.reciprocal(a_s[:, 0:heads], a_s[:, 0:heads]))
                dve.wait_ge(sem("attn_o_psum"), L + 1)
                w = D // heads
                v.tensor_tensor(a_o.rearrange("p (h n) -> p h n", h=heads),
                                bank(4)[:, 0:D].rearrange("p (h n) -> p h n", h=heads),
                                a_s[:, 0:heads].unsqueeze(2).to_broadcast([P, heads, w]), ALU.mult
                                ).then_inc(sem("attn_o_ready"), 1)
                dve.wait_ge(sem("attn_oT_psum"), L + 1)
                v.tensor_copy(a_oT.rearrange("p c n -> p (c n)"), bank(5)[:, 0:D]).then_inc(sem("attn_oT_ready"), 1)
                if L != 2:
                    link(v.tensor_tensor(x[:], x[:], bo_all[:, 4 + L, :], ALU.add))
                if L == 1:
                    link(v.tensor_tensor(x[:], x[:], xn[:], ALU.add))
                dve.wait_ge(sem("attn_out_psum"), L + 1)
                v.tensor_tensor(x[:], bank(6)[:, 0:D], x[:], ALU.add).then_inc(sem("attn_done"), 1)
                dve.wait_ge(sem("attn_done"), L + 1)

            def softmax_route(L, e):
                dve.wait_ge(sem("logits_psum"), L + 1)
                link(v.tensor_reduce(rmax[:], bank(1)[:, 0:e], AX_X, ALU.max))
                v.tensor_scalar(logit[:, 0:e], bank(1)[:, 0:e], rmax[:, 0:1], None, ALU.subtract
                                ).then_inc(sem("route_shifted"), 1)
                dve.wait_ge(sem("route_exp"), L + 1)
                link(v.tensor_reduce(rsum[:], prob[:, 0:e], AX_X, ALU.add))
                link(v.reciprocal(rinv[:], rsum[:]))
                link(v.tensor_scalar(prob[:, 0:e], prob[:, 0:e], rinv[:, 0:1], None, ALU.mult))

            def pick_top(e, k):
                link(v.memset(prob[:, e:e + 8], -1.0))
                link(v.max(top8[:], prob[:, 0:e]))
                if k < 8:
                    link(v.memset(top8[:, k:8], -1.0))
                link(v.match_replace(probr[:, 0:e + 8], top8[:], prob[:, 0:e + 8], -2.0))
                link(v.scalar_tensor_tensor(comb[:, 0:e], probr[:, 0:e], -2.0, prob[:, 0:e], ALU.is_equal, ALU.mult))

            def finish(L, value):
                v.tensor_tensor(x[:], value, x[:], ALU.add).then_inc(sem("ffn_done"), 1)
                dve.wait_ge(sem("ffn_done"), L + 1)

            def ffn_glu(L):
                f = FW[L]
                fc = f // 2
                e_n = 8 if L == 0 else 64
                norm(3 * L + 2)
                softmax_route(L, e_n)
                if L == 0:
                    pick_top(8, 2)
                    link(v.memset(comb[:, 8:10], 1.0))
                else:
                    pick_top(64, 8)
                    link(v.tensor_reduce(rsum[:], top8[:], AX_X, ALU.add))
                    link(v.reciprocal(rinv[:], rsum[:]))
                    link(v.tensor_scalar(comb[:, 0:64], comb[:, 0:64], rinv[:, 0:1], None, ALU.mult))
                    link(v.memset(comb[:, 64:65], 1.0))
                b0 = 0 if L == 0 else NE[0]

                def hidden(e, par, at):
                    dve.wait_ge(sem("silu"), at)
                    wait_count(dve, sem("hT_psum"), at - 2)
                    v.scalar_tensor_tensor(h_s[:, par, 0:f], g_s[:, par, 0:f], comb[:, bass.ds(e, 1)],
                                           bank(5 + 2 * par)[:, 0:f], ALU.mult, ALU.mult
                                           ).then_inc(sem("h_ready"), 1)

                def turned(par, at):
                    dve.wait_ge(sem("hT_psum"), at)
                    v.tensor_copy(hT[0:fc, par, :], bank(par)[0:fc, 0:2 * P]).then_inc(sem("hT_ready"), 1)
                hidden(0, 0, b0 + 1)
                if L == 0:
                    for e in range(NE[0]):
                        if e + 1 < NE[0]:
                            hidden(e + 1, (e + 1) % 2, e + 2)
                        turned(e % 2, e + 1)
                else:
                    with dve.Fori(0, 16) as it:
                        for j in range(RING):
                            hidden(it * RING + (j + 1), (j + 1) % 2, it * RING + (b0 + j + 2))
                            turned(j % 2, it * RING + (b0 + j + 1))
                    turned(0, b0 + 65)
                dve.wait_ge(sem("ring_used"), NE0[L + 1])
                finish(L, bank(2)[:, 0:D])

            def ffn1():
                norm(5)
                softmax_route(1, 32)
                pick_top(32, 2)
                link(v.memset(y_acc, 0.0))
                for e in range(NE[1]):
                    dve.wait_ge(sem("ring_used"), NE0[1] + e + 1)
                    for j in range(2):
                        if e >= 1:
                            dve.wait_ge(sem("l1_step"), 2 * (e - 1) + j + 1)
                        g = v.scalar_tensor_tensor(y_acc[:, j, :], bank(4 + e % 2)[:, j * D:(j + 1) * D],
                                                   comb[:, 2 * e + j:2 * e + j + 1], y_acc[:, j, :],
                                                   ALU.mult, ALU.add)
                        g.then_inc(sem("l1_step"), 1)
                dve.wait_ge(sem("l1_step"), 2 * NE[1])
                link(v.tensor_tensor(y_acc[:, 0, :], y_acc[:, 0, :], y_acc[:, 1, :], ALU.add))
                finish(1, y_acc[:, 0, :])

            def ffn3():
                v.tensor_tensor(csq[:], rw[:, 3, :, 0:8], rw[:, 3, :, 0:8], ALU.mult).then_inc(sem("csq_ready"), 1)
                norm(11)
                link(v.tensor_tensor(xsq, xn[:], xn[:], ALU.mult))
                v.tensor_reduce(rsum[:], xsq, AX_X, ALU.add).then_inc(sem("xsq_ready"), 1)
                dve.wait_ge(sem("norms_ready"), 2)
                link(v.tensor_scalar(rsum[:], rsum[:], 1e-12, None, ALU.max))
                link(v.reciprocal(rinv[:], rsum[:]))
                link(v.tensor_scalar(cnorm[:], cnorm[:], 1e-12, None, ALU.max))
                link(v.reciprocal(cnorm[:], cnorm[:]))
                dve.wait_ge(sem("logits_psum"), 4)
                link(v.scalar_tensor_tensor(logit[:, 0:8], bank(1)[:, 0:8], rinv[:, 0:1], cnorm[:], ALU.mult, ALU.mult))
                link(v.tensor_tensor(logit[:, 0:8], bank(1)[:, 8:16], logit[:, 0:8], ALU.add))
                link(v.max(top8[:], logit[:, 0:8]))
                link(v.tensor_scalar(comb[:, 0:8], logit[:, 0:8], top8[:, 1:2], None, ALU.is_ge))
                v.tensor_scalar(logit[:, 0:8], logit[:, 0:8], top8[:, 0:1], None, ALU.subtract
                                ).then_inc(sem("route_shifted"), 1)
                dve.wait_ge(sem("route_exp"), 4)
                link(v.tensor_tensor(comb[:, 0:8], prob[:, 0:8], comb[:, 0:8], ALU.mult))
                link(v.tensor_reduce(rsum[:], comb[:, 0:8], AX_X, ALU.add))
                link(v.reciprocal(rinv[:], rsum[:]))
                v.tensor_scalar(comb[:, 0:8], comb[:, 0:8], rinv[:, 0:1], None, ALU.mult).then_inc(sem("comb_ready"), 1)
                dve.wait_ge(sem("comb_ready"), 1)
                dve.wait_ge(sem("gT_psum"), 1)
                v.tensor_copy(gT, bank(2)[0:8, 0:P]).then_inc(sem("gT_ready"), 1)
                dve.wait_ge(sem("b2_psum"), 1)
                link(v.tensor_copy(y_acc[:, 0, :], bank(3)[:, 0:D]))
                for e in range(8):
                    dve.wait_ge(sem("ring_used"), NE0[3] + e + 1)
                    if e:
                        dve.wait_ge(sem("l3_taken"), e)
                    v.scalar_tensor_tensor(y_acc[:, 0, :], bank(6 + e % 2)[:, 0:D], comb[:, e:e + 1],
                                           y_acc[:, 0, :], ALU.mult, ALU.add).then_inc(sem("l3_taken"), 1)
                dve.wait_ge(sem("l3_taken"), 8)
                finish(3, y_acc[:, 0, :])

            for s in range(stages):
                L = s // 3
                if s % 3 == 0:
                    (xattn if L < 2 else xattn_low)(L)
                elif s % 3 == 1:
                    attn(L)
                elif L in (0, 2):
                    ffn_glu(L)
                elif L == 1:
                    ffn1()
                else:
                    ffn3()
            v.tensor_scalar(x[:], x[:], 1.0, None, ALU.mult).then_inc(sem("x_final"), 1)


STAGES = 12


def kernel(**inputs):
    import numpy as np
    import concourse.bacc as bacc
    from concourse.bass_utils import run_bass_kernel_spmd

    nc = bacc.Bacc("TRN2", target_bir_lowering=False, num_devices=1)
    a = {n: np.asarray(v) for n, v in inputs.items()}
    lay = {"x": a["x"][0], "ctx": a["ctx_768"][0], "mask": a["mask_BxS2_bk0"][0]}
    xn = [("L0_xattn_W_q", "L0_xattn_W_k", "L0_xattn_W_v", "L0_xattn_W_o"),
          ("L1_xattn_w_q", None, None, "L1_xattn_w_out"),
          ("L2_xattn_Wq", "L2_xattn_Wk", "L2_xattn_Wv", "L2_xattn_Wo"),
          ("L3_xattn_wq", "L3_xattn_wk", "L3_xattn_wv", "L3_xattn_wo")]
    lay["kv23"] = np.concatenate([
        np.concatenate([a[f"L{L}_xattn_{'W' if L == 2 else 'w'}{n}"], a[f"L{L}_xattn_b{n}"][None]])
        for n in "kv" for L in (2, 3)], axis=1)
    for L, (q, k, v, o) in enumerate(xn):
        inner = XH[L] * XD[L]
        if L >= 2:
            lay[f"x{L}_wq"] = np.tile(a[q].reshape(D, WP, 1, 32), (1, 1, 4, 1)).reshape(D, WP * P)
            lay[f"x{L}_wo"] = a[o]
            continue
        kv = a["L1_xattn_w_kv"]
        lay[f"x{L}_wq"] = a[q]
        bk = np.zeros(inner, np.float32)
        wk = np.concatenate([(a[k] if k else kv[:, :inner]).T, bk[:, None]], axis=1)
        lay[f"x{L}_wkT"] = wk.reshape(XH[L], XD[L], C + 1).transpose(1, 0, 2)
        lay[f"x{L}_wv"] = a[v] if v else kv[:, inner:]
        lay[f"x{L}_wo"] = a[o]
    for n in "qkvo":
        lay[f"a0_w{n}"] = a[f"L0_attn_W{n}"]
        lay[f"a1_w{n}"] = a[f"L1_attn_W{n}"].T
        lay[f"a2_w{n}"] = a[f"L2_attn_W{n}"].T
    for i, n in enumerate("qkv"):
        lay[f"a3_w{n}"] = a["L3_attn_W_qkv"][:, i * D:(i + 1) * D]
    lay["a3_wo"] = a["L3_attn_W_out"]
    for n in ["L0_xattn_b_o", "L1_xattn_b_out", "L2_xattn_bo", "L3_xattn_bo", "L0_attn_bo", "L1_attn_bo",
              "L3_attn_b_out", "L0_ffn_router_w", "L0_ffn_gate_w", "L0_ffn_up_w",
              "L0_ffn_down_w", "L0_ffn_shared_gate_w", "L0_ffn_shared_up_w", "L0_ffn_shared_down_w",
              "L1_ffn_expert_weights", "L2_ffn_w_gate", "L2_ffn_w_up", "L2_ffn_w_down", "L2_ffn_ws_gate_up",
              "L2_ffn_ws_down", "L3_ffn_w1", "L3_ffn_w2", "L3_ffn_b2"]:
        lay[n] = a[n]
    for n in ["sep", "align", "coh"]:
        lay[f"L2_attn_{n}_gate"] = a[f"L2_attn_{n}_gate"].reshape(1)
    for n in ["L1_ffn_router_w", "L2_ffn_router_w", "L3_ffn_centroids", "L3_ffn_w_route"]:
        lay[n + "T"] = a[n].T
    for n in ["L2_xattn_bq", "L3_xattn_bq"]:
        lay[n + "T"] = a[n].reshape(WP, 32).T
    b3 = a["L3_attn_b_qkv"]
    for i, (q, k, v) in {0: (a["L0_attn_bq"], a["L0_attn_bk"], a["L0_attn_bv"]),
                         1: (a["L1_attn_bq"], a["L1_attn_bk"], a["L1_attn_bv"]),
                         3: (b3[0:D], b3[D:2 * D], b3[2 * D:3 * D])}.items():
        lay[f"a{i}_bqT"] = q.reshape(AH[i], AD[i]).T
        lay[f"a{i}_bkT"] = k.reshape(AH[i], AD[i]).T
        lay[f"a{i}_bv"] = v
    lay["L3_ffn_b1T"] = a["L3_ffn_b1"].T
    lay["L3_attn_rel_biasT"] = a["L3_attn_rel_bias"].T
    arrays, io = {}, {}
    for n, v in lay.items():
        v = np.ascontiguousarray(v)
        arrays[f"in_{n}"] = v
        io[n] = nc.dram_tensor(f"in_{n}", v.shape, mybir.dt.from_np(v.dtype), kind="ExternalInput").ap()
    out = nc.dram_tensor("out_x", (1, P, D), F32, kind="ExternalOutput").ap()
    build(nc, io, out.rearrange("a p d -> (a p) d"), STAGES)
    r = run_bass_kernel_spmd(nc, [arrays], core_ids=[0])
    return r.results[0]["out_x"]
```

```python
from contextlib import ExitStack

import concourse.bass as bass
from concourse import mybir

ALU = mybir.AluOpType
ACT = mybir.ActivationFunctionType
AX_X = mybir.AxisListType.X
F32 = mybir.dt.float32
BF16 = mybir.dt.bfloat16
U8 = mybir.dt.uint8
U32 = mybir.dt.uint32
RMAX = bass.bass_isa.ReduceOp.max

P = 128
D = 256
DC = D // P
C = 192
CB = C - P
KEYS = 12544
TILES = KEYS // P
G = 7
GROUPS = TILES // G
BODY = 2 * G
ITERS = GROUPS // 2
HG = 8
QC = HG * P
BANK = 512
GK = G * P

S_A, S_D, S_B, S_C, S_R, S_ONE, S_L = 0, 128, 256, 384, 512, 704, 706
S_W = S_L + C
S_P1 = 256
BIAS_HI, BIAS_LO = 64, 96

NEG = -1.7e38
NEG_ATTN = -1e30
CLAMP = 10000.0
MAX_REL = 256
EPS = 1e-5
RING = 8
OWN = 4

XH = [8, 16, 16, 16]
XD = [64, 64, 16, 16]
SWEEPS = [1, 2]
SWEEP0 = [0, 1]
WH = 16
WP = WH // 2
VW = 2 * WH + 2
UNITS = 2 * TILES
UBODY = 2 * BODY
LEAD = 5
SLOTS = 4
LOW_SLOTS = 7
LO_SLOTS = 4
POOL_LO = [(1, 2, 4, 5, 7, 9, 10, 12, 13), (1, 4, 8, 11)]
LARGEST = 3.0e38
MARGIN = 2.0 ** -8
MAX_PAIR = [0, 1, 2, 3, 0, 1, 2, 3, 0, 1, 2, 0, 1, 2]
STAGES_IN = 4
PROJ = 15
AH = [8, 2, 16, 16]
AD = [32, 128, 16, 16]
AS = [8, 1, 16, 16]
ASCALE = [32 ** -0.5, 0.25, 0.25, 0.25]
NE = [10, 16, 65, 8]
NE0 = [sum(NE[:i]) for i in range(5)]
FW = [256, 0, 192, 0]
LAYERS = 4


def sweep_loop(eng, body, peel_first, peel_last):
    lo, hi = int(peel_first), ITERS - int(peel_last)
    for it in range(lo):
        body(it)
    with eng.Fori(lo, hi) as it:
        body(it)
    for it in range(hi, ITERS):
        body(it)


def wait_count(eng, sem, count):
    if isinstance(count, int) and count <= 0:
        return
    eng.wait_ge(sem, count)


def pair_before(k):
    return max(i for i in range(-BODY, k) if MAX_PAIR[i % BODY] == MAX_PAIR[k])


def build(nc, io, out, stages=12):
    with ExitStack() as ctx:
        def sb(name, shape, dt=F32):
            return ctx.enter_context(nc.sbuf_tensor(name, shape, dt))

        named = {}

        def sem(name):
            if name not in named:
                named[name] = ctx.enter_context(nc.semaphore(name))
            return named[name]

        ps = ctx.enter_context(nc.psum_tensor("ps", [P, 8, BANK], F32))
        psf = ps[:].rearrange("p b n -> p (b n)")

        def bank(b, n=1):
            return psf[:, b * BANK:(b + n) * BANK]

        kst = nc.dram_tensor("keys_T", [2, 2, GROUPS, D, GK], BF16, kind="Internal").ap()
        vst = nc.dram_tensor("values", [2, GROUPS, P, G * WH * VW], BF16, kind="Internal").ap()
        stream = nc.dram_tensor("ctx_stream", [GROUPS, P, G, S_W], BF16, kind="Internal").ap()

        ident = sb("ident", [P, P])
        ones = sb("ones", [P, P])
        onesb = sb("ones_bf16", [P, P], BF16)
        zrow = sb("zrow", [P, BANK], BF16)
        win_block = sb("win_block", [P, P])
        win_causal = sb("win_causal", [P, P])
        win_band = sb("win_band", [P, P])
        windows = [win_block, win_causal, win_band]
        x = sb("x_res", [P, D])
        xn = sb("xn", [P, D])
        xnT = sb("xnT", [P, DC, P])
        stats = sb("stats", [P, 6])
        mv = sb("mv", [P, 2])
        rstd = sb("rstd", [P, 1])
        o_rows = sb("o_rows", [P, 16, C])
        ctx_in = o_rows[:].rearrange("p h c -> p (h c)")[:, 0:2 * G * C].rearrange("p (b g c) -> p b g c", b=2, g=G)
        sregion = sb("stream_region", [P, 2 * G * (S_W + S_P1)], BF16)
        sbuf2 = sregion[:, 0:2 * G * S_W].rearrange("p (b g w) -> p b g w", b=2, g=G)
        sbuf1 = sregion[:, 2 * G * S_W:].rearrange("p (b g w) -> p b g w", b=2, g=G)
        kbuf = sregion[:, 0:2 * WP * GK].rearrange("p (b j n) -> p b j n", b=2, j=WP)
        keep_u8 = sb("keep_u8", [P, TILES], U8)
        keep = sb("keep", [P, TILES])
        maskneg = sb("maskneg", [P, TILES])
        any_keep = sb("any_keep", [P, 1])
        alive = sb("alive", [P, 1])
        qscale0 = sb("qscale0", [P, 1])
        xwq = sb("xwq", [P, DC, 1024])
        WKW = 16 * (C + 1)
        xwkv = sb("xwkv", [P, WKW + 2048])
        xwk = xwkv[0:64, 0:WKW].rearrange("p (h c) -> p h c", h=16)
        xwva = xwkv[:, WKW:WKW + 1024]
        xwvb = xwkv[0:CB, WKW + 1024:WKW + 2048]
        vbuf = xwkv[:].bitcast(BF16)[:, 0:2 * G * WH * VW].rearrange("p (b g h w) -> p b g h w", b=2, g=G, h=WH)
        xwo = sb("xwo", [P, 16, D])
        xwo2 = xwo[:, 0:DC, :]
        xbq4 = sb("xbq4", [P, 2, WP])
        half_a = sb("half_a", [P, 1])
        half_b = sb("half_b", [P, 1])
        vsum = o_rows[:].rearrange("p h c -> p (h c)")[:, 0:WH * VW].rearrange("p (h w) -> p h w", h=WH)
        bo_all = sb("bo_all", [P, 8, D])
        qT = sb("qT", [P, 16, P])
        qf_a = sb("qf_a", [P, QC])
        qf_b = sb("qf_b", [P, QC])
        vmean = qf_b[:, 0:D]
        qh_a = sb("qh_a", [P, QC], BF16)
        ql_a = sb("ql_a", [P, QC], BF16)
        q_bb = sb("q_bb", [P, QC], BF16)
        q_d1 = sb("q_d1", [P, QC], BF16)
        q_d2 = sb("q_d2", [P, QC], BF16)
        maxall = sb("maxall", [P, QC])
        p32 = sb("p32", [P, SLOTS, QC])
        runmax = p32[:, 0:2]
        parts = sb("p_parts", [P, 2, SLOTS, QC], BF16)
        phi, plo = parts[:, 0], parts[:, 1]
        parts_f32 = parts.rearrange("p a s n -> p (a s n)").bitcast(F32)

        def low_p(u):
            i = u % LOW_SLOTS
            return p32[:, i] if i < SLOTS else parts_f32[:, (i - SLOTS) * QC:(i - SLOTS + 1) * QC]

        def low_hi(u):
            return low_p(u).bitcast(BF16).rearrange("p (n two) -> p n two", two=2)[:, :, 1]

        def low_lo(u):
            i = u % LO_SLOTS
            return (plo[:, 2], plo[:, 3], q_d1[:], q_d2[:])[i]

        def max_copy(i):
            return phi[:, i]
        acc16 = plo[:, 0:2]
        kstage = p32[:].rearrange("p s n -> p (s n)").bitcast(BF16)[:, 0:8 * GK].rearrange(
            "p (m h n) -> p m h n", m=4, h=2)
        vstage = parts[:].rearrange("p a s n -> p (a s n)")[:, 0:2 * G * WH * VW].rearrange(
            "p (l g h w) -> p l g h w", l=2, g=G, h=WH)
        mq = maxall[:].bitcast(BF16)
        maxl = qT[:].rearrange("p h n -> p (h n)")
        den = sb("den", [P, 16])
        rden = sb("rden", [P, 16])
        nanf = sb("nanf", [P, 16])
        nan1 = sb("nan1", [P, 1])
        nana = sb("nana", [P, 1])
        oT_a = qf_a[:].rearrange("p (b n) -> p b n", b=2)
        oT_b = qf_b[0:CB, :].rearrange("p (b n) -> p b n", b=2)
        avT = maxall[0:64, :].rearrange("p (b n) -> p b n", b=2)
        aw = sb("aw", [P, DC, 4 * D])
        abq = sb("abq", [P, 4, 16])
        abk = sb("abk", [P, 4, 16])
        abv = sb("abv", [P, 4, D])
        gates = sb("gates", [P, 3])
        ngates = sb("ngates", [P, 3])
        rel = o_rows[:].rearrange("p h c -> p (h c)")[:, 0:16 * P].rearrange("p (h n) -> p h n", h=16)
        a_m = sb("a_m", [P, 16])
        a_s = sb("a_s", [P, 16])
        a_v = qh_a[:].bitcast(F32)[:, 0:D]
        a_o = ql_a[:].bitcast(F32)[:, 0:D]
        a_oT = q_bb[:].bitcast(F32)[:, 0:D].rearrange("p (c n) -> p c n", c=DC)
        xnT_rev = q_bb[:].bitcast(F32)[:, D:2 * D].rearrange("p (c n) -> p c n", c=DC)
        qk_buf = sregion[:].bitcast(F32)
        a_q = qk_buf[:, 0:2048]
        a_k = qk_buf[:, 2048:4096]
        a_S = p32[:, 0:2].rearrange("p a n -> p (a n)")
        a_U = p32[:, 2:4].rearrange("p a n -> p (a n)")
        a_T = phi.bitcast(F32).rearrange("p a n -> p (a n)")
        ring_own = sb("ring", [P, OWN, 1536])
        ring_shared = sregion[:].bitcast(F32)[:, 0:(RING - OWN) * 1536].rearrange("p (s n) -> p s n", s=RING - OWN)

        def ring(slot):
            return ring_own[:, slot] if slot < OWN else ring_shared[:, slot - OWN]
        rw = sb("rw", [P, LAYERS, DC, 64])
        logit = sb("logit", [P, 64])
        prob = sb("prob", [P, 72])
        probr = sb("probr", [P, 72])
        top8 = sb("top8", [P, 8])
        rmax = sb("rmax", [P, 1])
        rsum = sb("rsum", [P, 1])
        rinv = sb("rinv", [P, 1])
        comb = sb("comb", [P, 66])
        g_s = phi[:, 0].bitcast(F32).rearrange("p (b n) -> p b n", b=2)
        h_s = phi[:, 1].bitcast(F32).rearrange("p (b n) -> p b n", b=2)
        hT = plo[:, 0].bitcast(F32).rearrange("p (b n) -> p b n", b=2)
        y_acc = plo[:, 1].bitcast(F32).rearrange("p (b n) -> p b n", b=2)
        xsq = g_s[:, 0, :]
        b1T = sb("b1T", [P, 8])
        b2r = sb("b2r", [8, D])
        csq = sb("csq", [P, DC, 8])
        cnorm = sb("cnorm", [P, 8])
        gT = qT[0:8, 0, :]

        PIECES = [(qh_a, S_A), (ql_a, S_A), (qh_a, S_C), (q_bb, S_B), (q_d2, S_D)]
        in_landed = [sem("ctx_in_landed0"), sem("ctx_in_landed1")]
        stream_out = [sem("stream_written0"), sem("stream_written1")]
        p1_landed = [sem("max_stream_landed0"), sem("max_stream_landed1")]
        p2_landed = [sem("stream_landed0"), sem("stream_landed1")]
        k_landed = [sem("keys_landed0"), sem("keys_landed1")]
        v_landed = [sem("values_landed0"), sem("values_landed1")]
        ring_landed = [sem(f"ring_landed{i}") for i in range(RING)]
        xw_landed = sem("xattn_weights_landed")
        aw_landed = sem("attn_weights_landed")
        const_landed = sem("consts_landed")
        QUERY_BANK = [6, 0]
        XW_DMAS = [5, 5, 2, 2]
        AW_DMAS = [4, 4, 4, 4]
        xw_at = [16 * sum(XW_DMAS[:i + 1]) for i in range(4)]
        aw_at = [16 * sum(AW_DMAS[:i + 1]) for i in range(4)]
        const_count = [0]

        def lo_maker(l, u):
            return "low_lo_pool" if u % 14 in POOL_LO[l] else "low_lo_dve"

        def lo_made(l, it, u):
            def share(layer, units):
                return len([i for i in range(units) if lo_maker(layer, i) == lo_maker(l, u)])
            return it * share(l, UBODY) + ITERS * sum(share(e, UBODY) for e in range(l)) + share(l, u + 1)

        def low_copies(l, u):
            return 3 * UNITS // 4 * l + 3 * (u // 4) + u % 4

        block = ctx.enter_context(nc.Block())

        def plain_wait(eng, s, count):
            if isinstance(count, int):
                if count > 0:
                    eng.wait_ge(s, count)
                return
            count = eng.snap(count)
            eng.wait_ge(s, count)
            eng.sem_inc(sem("waits_passed"), 1)
        ctx_rows = io["ctx"].rearrange("(p t) c -> p t c", t=TILES)
        layers = (stages + 2) // 3

        def has(kind, layer):
            return 3 * layer + kind < stages

        consts = [
            (x[:], io["x"]),
            (keep_u8[:], io["mask"].rearrange("(p t) -> p t", t=TILES)),
        ]
        for i, n in enumerate(["L0_xattn_b_o", "L1_xattn_b_out", "L2_xattn_bo", "L3_xattn_bo"]):
            consts.append((bo_all[:, i, :], io[n].partition_broadcast(P)))
        for i, n in enumerate(["L0_attn_bo", "L1_attn_bo", None, "L3_attn_b_out"]):
            if n:
                consts.append((bo_all[:, 4 + i, :], io[n].partition_broadcast(P)))
        for i, n in enumerate(["L2_xattn", "L3_xattn"]):
            for j in range(4):
                consts.append((xbq4[32 * j:32 * j + 32, i, :], io[n + "_bqT"]))
        for i in (0, 1, 3):
            consts.append((abq[0:AD[i], i, 0:AH[i]], io[f"a{i}_bqT"]))
            consts.append((abk[0:AD[i], i, 0:AH[i]], io[f"a{i}_bkT"]))
            consts.append((abv[:, i, :], io[f"a{i}_bv"].partition_broadcast(P)))
        for i, n in enumerate(["sep", "align", "coh"]):
            consts.append((gates[:, i:i + 1], io[f"L2_attn_{n}_gate"].partition_broadcast(P)))
        for i, (n, e) in enumerate([("L0_ffn_router_w", 8), ("L1_ffn_router_wT", 32), ("L2_ffn_router_wT", 64)]):
            consts.append((rw[:, i, :, 0:e], io[n].rearrange("(c p) e -> p c e", p=P)))
        consts.append((rw[:, 3, :, 0:8], io["L3_ffn_centroidsT"].rearrange("(c p) e -> p c e", p=P)))
        consts.append((rw[:, 3, :, 8:16], io["L3_ffn_w_routeT"].rearrange("(c p) e -> p c e", p=P)))
        consts.append((b1T[:], io["L3_ffn_b1T"]))
        consts.append((b2r[:], io["L3_ffn_b2"]))
        relT = io["L3_attn_rel_biasT"]
        rel_loads = [(rel, bass.AP(relT.tensor, MAX_REL - P + 1, [[1, P], [2 * MAX_REL + 1, 16], [1, P]]))]
        CONSTS_ALL = 16 * len(consts)
        EARLY = 2

        def load_xw(sp, L):
            h, d = XH[L], XD[L]
            inner = h * d if L < 2 else WP * P
            sp.dma_start(xwq[:, :, 0:inner], io[f"x{L}_wq"].rearrange("(c p) n -> p c n", p=P)).then_inc(xw_landed, 16)
            if L >= 2:
                sp.dma_start(xwo2, io[f"x{L}_wo"].rearrange("(c p) n -> p c n", p=P)).then_inc(xw_landed, 16)
                return
            sp.dma_start(xwk[0:d, 0:h, :], io[f"x{L}_wkT"]).then_inc(xw_landed, 16)
            sp.dma_start(xwva[:, 0:inner], io[f"x{L}_wv"][0:P, :]).then_inc(xw_landed, 16)
            sp.dma_start(xwvb[:, 0:inner], io[f"x{L}_wv"][P:C, :]).then_inc(xw_landed, 16)
            sp.dma_start(xwo[0:d, 0:h, :], io[f"x{L}_wo"].rearrange("(h d) n -> d h n", d=d)).then_inc(xw_landed, 16)

        def load_aw(sp, L):
            for j, n in enumerate("qkvo"):
                sp.dma_start(aw[:, :, j * D:(j + 1) * D],
                             io[f"a{L}_w{n}"].rearrange("(c p) n -> p c n", p=P)).then_inc(aw_landed, 16)

        def ring_parts(L, e):
            if L == 0:
                f = FW[0]
                if e < 8:
                    g, u, d = io["L0_ffn_gate_w"][e], io["L0_ffn_up_w"][e], io["L0_ffn_down_w"][e]
                else:
                    o = (e - 8) * f
                    g, u = io["L0_ffn_shared_gate_w"][:, o:o + f], io["L0_ffn_shared_up_w"][:, o:o + f]
                    d = io["L0_ffn_shared_down_w"][o:o + f, :]
                return g, u, d
            if L == 2:
                return (io["L2_ffn_w_gate"][e], io["L2_ffn_w_up"][e], io["L2_ffn_w_down"][e])

        def gu_view(slot, f):
            return ring(slot)[:, 0:2 * DC * f].rearrange("p (c n) -> p c n", c=DC)

        def dn_view(slot, f):
            return ring(slot)[0:f // 2, 1024:1024 + 2 * D].rearrange("p (c n) -> p c n", c=2)

        RING_DMAS = [3, 2, 3, 2]

        def landed_before(slot, L):
            n = 0
            for l in range(L):
                n += 16 * RING_DMAS[l] * len([e for e in range(NE[l]) if e % RING == slot])
            return n

        def landed_at(L, e):
            return landed_before(e % RING, L) + 16 * RING_DMAS[L] * (e // RING + 1)

        def load_ring(sp, L, e):
            slot = e % RING
            wait_count(sp, sem("ring_used"), NE0[L] + max(e - RING + 1, 0))
            if OWN <= e < RING:
                sp.wait_ge(sem("attn_done"), L + 1)
            s = ring_landed[slot]
            if L in (0, 2):
                f = FW[L]
                if L == 2 and e == 64:
                    gu = io["L2_ffn_ws_gate_up"]
                    g, u, d = gu[:, 0:f], gu[:, f:2 * f], io["L2_ffn_ws_down"]
                else:
                    g, u, d = ring_parts(L, e)
                v = gu_view(slot, f)
                sp.dma_start(v[:, :, 0:f], g.rearrange("(c p) n -> p c n", p=P)).then_inc(s, 16)
                sp.dma_start(v[:, :, f:2 * f], u.rearrange("(c p) n -> p c n", p=P)).then_inc(s, 16)
                sp.dma_start(dn_view(slot, f), d.rearrange("(c p) n -> p c n", p=f // 2)).then_inc(s, 16)
            elif L == 1:
                v = gu_view(slot, 256)
                for j in range(2):
                    sp.dma_start(v[:, :, j * D:(j + 1) * D],
                                 io["L1_ffn_expert_weights"][2 * e + j].rearrange("(c p) n -> p c n", p=P)
                                 ).then_inc(s, 16)
            else:
                sp.dma_start(ring(slot)[:, 0:DC * P].rearrange("p (c n) -> p c n", c=DC),
                             io["L3_ffn_w1"][e].rearrange("(c p) n -> p c n", p=P)).then_inc(s, 16)
                sp.dma_start(ring(slot)[:, 1024:1024 + D], io["L3_ffn_w2"][e]).then_inc(s, 16)

        def load_ring2_loop(sp):
            with sp.Fori(1, 64 // RING) as it:
                for j in range(RING):
                    slot = j
                    s = ring_landed[slot]
                    f = FW[2]
                    plain_wait(sp, sem("ring_used"), it * RING + (NE0[2] + j - RING + 1))
                    v = gu_view(slot, f)
                    e = it * RING + j
                    sp.dma_start(v[:, :, 0:f], io["L2_ffn_w_gate"][bass.ds(e, 1)].rearrange(
                        "o (c p) n -> p (o c) n", p=P)).then_inc(s, 16)
                    sp.dma_start(v[:, :, f:2 * f], io["L2_ffn_w_up"][bass.ds(e, 1)].rearrange(
                        "o (c p) n -> p (o c) n", p=P)).then_inc(s, 16)
                    sp.dma_start(dn_view(slot, f), io["L2_ffn_w_down"][bass.ds(e, 1)].rearrange(
                        "o (c p) n -> p (o c) n", p=f // 2)).then_inc(s, 16)

        @block.sync
        def _(sp):
            for d, s in consts[:EARLY]:
                sp.dma_start(d, s).then_inc(sem("early_landed"), 16)

            def ctx_load(g, b):
                sp.dma_start(ctx_in[:, b], ctx_rows[:, bass.ds(g * G, G), :]).then_inc(in_landed[b], 16)

            def ctx_store(it, b):
                plain_wait(sp, sem("dve_split"), it * 2 + b + 1)
                plain_wait(sp, sem("pool_split"), it * 2 + (b + 1))
                sp.dma_start(stream[bass.ds(it * 2 + b, 1)].rearrange("o p g w -> p (o g) w"),
                             sbuf2[:, b]).then_inc(stream_out[b], 16)
            ctx_load(0, 0)
            ctx_load(1, 1)
            sp.dma_start(qf_a[:], io["kv23"][0:P, :]).then_inc(sem("kv_weights_landed"), 16)
            sp.dma_start(qf_b[0:CB + 1, :], io["kv23"][P:C + 1, :]).then_inc(sem("kv_weights_landed"), 16)
            load_xw(sp, 0)
            load_aw(sp, 0)
            for d, s in consts[EARLY:]:
                sp.dma_start(d, s).then_inc(const_landed, 16)
            for e in range(OWN):
                load_ring(sp, 0, e)

            def kv_store(it, b):
                g = it * 2 + b
                plain_wait(sp, sem("proj_lo"), g * PROJ + 8)
                for l in range(2):
                    for hl in range(2):
                        sp.dma_start(kst[l, hl, bass.ds(g, 1)].rearrange("o (m p) n -> p (o m) n", p=P),
                                     kstage[:, 2 * l:2 * l + 2, hl, :]).then_inc(sem("keys_written"), 16)
                plain_wait(sp, sem("proj_lo"), g * PROJ + PROJ)
                for l in range(2):
                    sp.dma_start(vst[l, bass.ds(g, 1)].rearrange("o p n -> p (o n)"),
                                 vstage[:, l].rearrange("p g h w -> p (g h w)")
                                 ).then_inc(sem("values_written"), 16)
            with sp.Fori(0, ITERS - 1) as it:
                for b in range(2):
                    ctx_store(it, b)
                    ctx_load(it * 2 + (2 + b), b)
                    kv_store(it, b)
            for b in range(2):
                ctx_store(ITERS - 1, b)
                kv_store(ITERS - 1, b)
            for b in range(2):
                sp.wait_ge(stream_out[b], 16 * ITERS)

            for L in range(layers):
                if L >= 2:
                    l = L - 2
                    sp.wait_ge(sem("keys_written"), 64 * GROUPS)
                    sp.wait_ge(sem("values_written"), 32 * GROUPS)

                    def k_load(g, b):
                        for j, hl in enumerate((0, 1, 0)):
                            sp.dma_start(kbuf[32 * j:32 * j + 32, b],
                                         kst[l, hl, bass.ds(g, 1)].rearrange("o (j r) n -> r (o j) n", r=32)
                                         ).then_inc(k_landed[b], 16)

                    def max_k_loads(it):
                        for b in range(2):
                            if isinstance(it, int):
                                sp.wait_ge(sem("attn_done"), L)
                            else:
                                plain_wait(sp, sem("low_max_scores"), it * UBODY + (UNITS * l + 2 * G * (b - 1)))
                            k_load(it * 2 + b, b)

                    def kv_loads(it):
                        for b in range(2):
                            if isinstance(it, int):
                                sp.wait_ge(sem("low_max_scores"), UNITS * (l + 1) - 2 * G * (1 - b))
                            else:
                                plain_wait(sp, sem("low_pv_done"), it * UBODY + (UNITS * l + 2 * G * (b - 1)))
                            k_load(it * 2 + b, b)
                            sp.dma_start(vbuf[:, b].rearrange("p g h w -> p (g h w)"),
                                         vst[l, bass.ds(it * 2 + b, 1)].rearrange("o p n -> p (o n)")
                                         ).then_inc(v_landed[b], 16)
                    sweep_loop(sp, max_k_loads, True, False)
                    sweep_loop(sp, kv_loads, True, False)
                for s in range(SWEEPS[L] if L < 2 else 0):
                    n = SWEEP0[L] + s

                    def max_loads(it):
                        for b in range(2):
                            g = it * 2 + b
                            plain_wait(sp, sem("max_scores_ready"), it * BODY + (TILES * n + G * (b - 1)))
                            sp.dma_start(sbuf1[:, b], stream[bass.ds(g, 1), :, :, 0:S_P1].rearrange(
                                "o p g w -> p (o g) w")).then_inc(p1_landed[b], 16)

                    def pv_loads(it):
                        for b in range(2):
                            g = it * 2 + b
                            if isinstance(it, int) and it == 0 and s == 0 and L > 0:
                                sp.wait_ge(sem("attn_done"), L)
                            plain_wait(sp, sem("pv_done"), it * BODY + (TILES * n + G * (b - 1)))
                            sp.dma_start(sbuf2[:, b], stream[bass.ds(g, 1)].rearrange(
                                "o p g w -> p (o g) w")).then_inc(p2_landed[b], 16)
                    sweep_loop(sp, max_loads, n == 0, False)
                    sweep_loop(sp, pv_loads, s == 0, False)
                if L + 1 < layers:
                    sp.wait_ge(sem("xattn_done"), L + 1)
                    load_xw(sp, L + 1)
                if L == 3 and has(1, L):
                    sp.wait_ge(sem("xattn_done"), L + 1)
                    for d, s in rel_loads:
                        sp.dma_start(d, s).then_inc(sem("rel_landed"), 16)
                if has(1, L) and L + 1 < layers:
                    sp.wait_ge(sem("attn_done"), L + 1)
                    load_aw(sp, L + 1)
                if has(2, L):
                    for e in range(OWN, RING):
                        load_ring(sp, L, e)
                    if L == 2:
                        load_ring2_loop(sp)
                        load_ring(sp, 2, 64)
                    else:
                        for e in range(RING, NE[L]):
                            load_ring(sp, L, e)
                    if L + 1 < LAYERS:
                        sp.wait_ge(sem("ring_used"), NE0[L + 1])
                    if L + 1 < LAYERS and has(2, L + 1):
                        for e in range(OWN):
                            load_ring(sp, L + 1, e)
            sp.wait_ge(sem("keys_written"), 64 * GROUPS)
            sp.wait_ge(sem("values_written"), 32 * GROUPS)
            sp.wait_ge(sem("x_final"), 1)
            sp.dma_start(out, x[:]).then_inc(sem("out_written"), 16)
            sp.wait_ge(sem("out_written"), 16)

        @block.gpsimd
        def _(pool):
            g = nc.gpsimd
            chain = [0]

            def link(ins):
                chain[0] += 1
                ins.then_inc(sem("pool_chain"), 1)
                pool.wait_ge(sem("pool_chain"), chain[0])
            link(g.memset(ident[:], 0.0))
            link(g.affine_select(out=ident[:], in_=ident[:], compare_op=ALU.not_equal, fill=1.0, base=0,
                                 pattern=[[-1, P]], channel_multiplier=1))
            link(g.memset(ones[:], 1.0))
            link(g.memset(zrow[:], 0.0))
            g.memset(onesb[:], 1.0).then_inc(sem("ident_made"), 1)
            pool.wait_ge(sem("ident_made"), 1)
            link(g.memset(sbuf2[CB:P, :, :, S_D:S_D + P], 0.0))
            link(g.memset(sbuf2[BIAS_HI:BIAS_HI + 1, :, :, S_D:S_D + P], 1.0))
            link(g.memset(sbuf2[BIAS_LO:BIAS_LO + 1, :, :, S_D:S_D + P], 1.0))
            g.memset(sbuf2[:, :, :, S_ONE:S_ONE + 2], 1.0).then_inc(sem("consts_made"), 1)
            pool.wait_ge(sem("consts_made"), 1)
            g.memset(vstage, 1.0).then_inc(sem("vstage_ones"), 1)
            pool.wait_ge(sem("vstage_ones"), 1)

            pool.wait_ge(sem("keep_ready"), 1)
            link(g.partition_all_reduce(alive[:], any_keep[:], P, RMAX))
            g.memset(nan1[:], 0.0).then_inc(sem("alive_ready"), 1)
            pool.wait_ge(sem("alive_ready"), 1)

            def rows(it):
                for b in range(2):
                    n = it * 2 + b
                    pool.wait_ge(sem("act_rows"), n + 1)
                    g.tensor_tensor(sbuf2[:, b, :, S_L:S_L + C], ctx_in[:, b], sbuf2[:, b, :, S_R:S_R + C],
                                    ALU.subtract).then_inc(sem("pool_split"), 1)
            sweep_loop(pool, rows, True, False)

            H2 = P // 2
            for w in windows:
                link(g.memset(w[:], 0.0))
            for w in (win_causal, win_band):
                link(g.affine_select(out=w[:], in_=w[:], compare_op=ALU.is_ge, fill=NEG_ATTN, base=0,
                                     pattern=[[-1, P]], channel_multiplier=1))
            link(g.memset(win_block[0:H2, H2:P], NEG_ATTN))
            link(g.memset(win_block[H2:P, 0:H2], NEG_ATTN))
            link(g.memset(win_causal[H2:P, 0:H2], NEG_ATTN))
            g.affine_select(out=win_band[:], in_=win_band[:], compare_op=ALU.is_ge, fill=NEG_ATTN, base=H2 - 1,
                            pattern=[[1, P]], channel_multiplier=-1).then_inc(sem("windows_ready"), 1)
            pool.wait_ge(sem("windows_ready"), 1)

            def low_pool(L):
                l = L - 2
                pool.wait_ge(sem("ffn_done"), L)
                g.memset(kbuf[96:P], 1.0).then_inc(sem("key_ones"), 1)
                pool.wait_ge(sem("key_ones"), l + 1)
                base = UNITS * l

                def units(it):
                    for u in range(UBODY):
                        if lo_maker(l, u) == "low_lo_dve":
                            continue
                        at = it * UBODY + (base + u)
                        pool.wait_ge(sem("low_exp_ready"), at + 1)
                        wait_count(pool, sem("low_pv_done"), at + (1 - LO_SLOTS))
                        g.tensor_tensor(low_lo(u), low_p(u), low_hi(u), ALU.subtract
                                        ).then_inc(sem("low_lo_pool"), 1)
                sweep_loop(pool, units, L == 2, False)
                if L == 2:
                    pool.wait_ge(sem("nan_local"), 1)
                    g.partition_all_reduce(nana[:], nan1[:], P, RMAX).then_inc(sem("nan_ready"), 1)

            for L in range(layers):
                if L == 1:
                    pool.wait_ge(sem("attn_done"), 1)
                    link(g.memset(win_block[:], 0.0))
                    g.affine_select(out=win_block[:], in_=win_block[:], compare_op=ALU.not_equal, fill=1.0,
                                    base=1 - P, pattern=[[1, P]], channel_multiplier=1
                                    ).then_inc(sem("reversal_ready"), 1)
                    pool.wait_ge(sem("reversal_ready"), 1)
                if L >= 2:
                    low_pool(L)

        @block.tensor
        def _(pe):
            t = nc.tensor

            def turn_x(s):
                pe.wait_ge(sem("xn_ready"), s + 1)
                for c in range(DC):
                    m = t.transpose(bank(0)[:, c * P:(c + 1) * P], xn[:, c * P:(c + 1) * P], ident[:])
                m.then_inc(sem("xnT_psum"), 1)
                pe.wait_ge(sem("xnT_ready"), s + 1)

            def turn_ctx(g, b):
                pe.wait_ge(in_landed[b], (g - b) * 8 + 16)
                wait_count(pe, sem("dve_split"), g)
                wait_count(pe, sem("act_split"), g * 3)
                for k in range(G):
                    t.transpose(bank(0, 2)[:, k * P:(k + 1) * P], ctx_in[:, b, k, 0:P], ident[:])
                for k in range(G):
                    m = t.transpose(bank(2, 2)[0:CB, k * P:(k + 1) * P], ctx_in[:, b, k, P:C], ident[:])
                m.then_inc(sem("ctxT_psum"), 1)

            def project_ctx(g, b):
                pe.wait_ge(sem("dve_split"), g + 1)
                pe.wait_ge(sem("act_split"), g * 3 + 3)
                u = 0
                for mt in range(4):
                    for lo, hi in ((0, 4), (4, G)):
                        wait_count(pe, sem("proj_lo"), g * PROJ + (u - 2 if u < 3 else u - 3))
                        o = bank(4 + u % 4)[:, 0:(hi - lo) * P]
                        for i, (w, c) in enumerate(PIECES):
                            m = t.matmul(o, w[:, mt * P:(mt + 1) * P], sbuf2[:, b, lo:hi, c:c + P],
                                         start=(i == 0), stop=(i == len(PIECES) - 1))
                        m.then_inc(sem("proj_psum"), 1)
                        u += 1
                for k in range(G):
                    wait_count(pe, sem("proj_lo"), g * PROJ + (u - 2 if u < 3 else u - 3))
                    for i, (w, c) in enumerate(PIECES):
                        m = t.matmul(bank(4 + u % 4), sbuf2[:, b, k, c:c + P], w[:, 512:1024],
                                     start=(i == 0), stop=(i == len(PIECES) - 1))
                    m.then_inc(sem("proj_psum"), 1)
                    u += 1

            def queries(L, first_bank):
                d = XD[L]
                pe.wait_ge(xw_landed, xw_at[L])
                for q in range(XH[L] // 4):
                    for j in range(4):
                        h = 4 * q + j
                        for c in range(DC):
                            m = t.matmul(bank(first_bank + q)[0:d, j * P:(j + 1) * P],
                                         xwq[:, c, h * d:(h + 1) * d], xnT[:, c, :], start=(c == 0),
                                         stop=(c == DC - 1))
                    m.then_inc(sem("qT_psum"), 1)

            pe.wait_ge(sem("ident_made"), 1)
            turn_x(0)
            turn_ctx(0, 0)
            queries(0, QUERY_BANK[0])
            pe.wait_ge(sem("qT_ready"), XH[0] // 4)
            pe.wait_ge(sem("kv_pieces_ready"), 1)
            pe.wait_ge(sem("consts_made"), 1)

            def prepare(it):
                last = isinstance(it, int) and it == ITERS - 1
                for b in range(2):
                    if not (last and b == 1):
                        turn_ctx(it * 2 + (b + 1), 1 - b)
                    project_ctx(it * 2 + b, b)
            sweep_loop(pe, prepare, True, True)
            pe.wait_ge(sem("proj_lo"), GROUPS * PROJ)

            def xattn(L):
                h_n, d = XH[L], XD[L]
                quads = h_n // 4
                if L:
                    turn_x(3 * L)
                    queries(L, QUERY_BANK[L])
                for s in range(SWEEPS[L]):
                    n = SWEEP0[L] + s
                    pe.wait_ge(sem("qT_ready"), sum(XH[:L]) // 4 + quads)
                    for j in range(HG):
                        h = HG * s + j
                        t.matmul(bank(4, 2)[:, j * P:(j + 1) * P], xwk[0:d, h, 0:P], qT[0:d, h, :],
                                 start=True, stop=True)
                    for j in range(HG):
                        h = HG * s + j
                        m = t.matmul(bank(6, 2)[0:CB + 1, j * P:(j + 1) * P], xwk[0:d, h, P:C + 1],
                                     qT[0:d, h, :], start=True, stop=True)
                    m.then_inc(sem("qk_psum"), 1)
                    pe.wait_ge(sem("q_hi_ready"), n + 1)
                    base = TILES * n

                    def max_tiles(it):
                        for k in range(BODY):
                            b = k // G
                            if k % G == 0:
                                pe.wait_ge(p1_landed[b], it * 16 + 16 * (ITERS * n + 1))
                            last = pair_before(k)
                            if last % 2:
                                wait_count(pe, sem("max_copied"), it * G + ((base + last + 1) // 2))
                            else:
                                wait_count(pe, sem("max_taken"), it * BODY + (base + last + 1))
                            sc = bank(2 * MAX_PAIR[k], 2)
                            for c, rhs in enumerate((qh_a, q_d1)):
                                for m2 in range(2):
                                    m = t.matmul(sc[:, m2 * BANK:(m2 + 1) * BANK],
                                                 sbuf1[:, b, k % G, c * P:(c + 1) * P],
                                                 rhs[:, m2 * BANK:(m2 + 1) * BANK], start=(c == 0), stop=(c == 1))
                            m.then_inc(sem("max_scores_ready"), 1)
                    sweep_loop(pe, max_tiles, n == 0, False)

                    pe.wait_ge(sem("max_merged"), n + 1)
                    for h in range(HG):
                        m = t.transpose(bank(0, 2)[:, h * P:(h + 1) * P], runmax[:, 0, h * P:(h + 1) * P], ident[:])
                    m.then_inc(sem("max_turned"), 1)
                    pe.wait_ge(sem("max_diagonals"), n + 1)
                    for b in range(2):
                        m = t.matmul(bank(2 + b), ones[:], runmax[:, 1, b * BANK:(b + 1) * BANK], start=True,
                                     stop=True)
                    m.then_inc(sem("max_ready"), 1)

                    pe.wait_ge(sem("q_all_ready"), n + 1)
                    for b in range(4):
                        t.matmul(bank(b), zrow[:, 0:P], zrow[:], start=True, stop=False, skip_group_check=True)

                    def scores(it, k):
                        b = k // G
                        if k % G == 0:
                            pe.wait_ge(p2_landed[b], it * 16 + 16 * (ITERS * n + 1))
                        wait_count(pe, sem("p32_ready"), it * BODY + (base + k - 1))
                        sc = bank(4 + 2 * (k % 2), 2)
                        v = sbuf2[:, b, k % G, :]
                        steps = [(S_A, qh_a), (S_A, ql_a), (S_C, qh_a), (S_B, q_bb), (S_D, q_d2)]
                        for i, (o, rhs) in enumerate(steps):
                            for m2 in range(2):
                                m = t.matmul(sc[:, m2 * BANK:(m2 + 1) * BANK], v[:, o:o + P],
                                             rhs[:, m2 * BANK:(m2 + 1) * BANK],
                                             start=(i == 0), stop=(i == len(steps) - 1))
                        m.then_inc(sem("scores_ready"), 1)

                    def pv(it, k):
                        b = k // G
                        pe.wait_ge(sem("p_ready"), it * BODY + (base + k + 1))
                        v = sbuf2[:, b, k % G, :]
                        for j in range(HG):
                            o = psf[:, j * 256:j * 256 + C + 1]
                            a = j * P
                            t.matmul(o, phi[:, k % 2, a:a + P], v[:, S_R:S_R + C + 1], start=False, stop=False,
                                     skip_group_check=True)
                            t.matmul(o[:, 0:C], phi[:, k % 2, a:a + P], v[:, S_L:S_L + C], start=False,
                                     stop=False, skip_group_check=True)
                            m = t.matmul(o, plo[:, k % 2, a:a + P], v[:, S_R:S_R + C + 1], start=False,
                                         stop=False, skip_group_check=True)
                        m.then_inc(sem("pv_done"), 1)

                    def pv_tiles(it):
                        last = isinstance(it, int) and it == ITERS - 1
                        for k in range(BODY):
                            if k < BODY - 1:
                                scores(it, k + 1)
                            elif not last:
                                scores(it + 1, 0)
                            pv(it, k)
                    scores(0, 0)
                    sweep_loop(pe, pv_tiles, n == 0, True)
                    pe.wait_ge(sem("o_rows_ready"), n + 1)
                q0 = sum(XH[:L]) // 4

                def turn_o(q):
                    if q >= 2:
                        pe.wait_ge(sem("oTa_ready"), q0 + q - 1)
                        pe.wait_ge(sem("oTb_ready"), q0 + q - 1)
                    for j in range(4):
                        t.transpose(bank(4 + q % 2)[:, j * P:(j + 1) * P], o_rows[:, 4 * q + j, 0:P], ident[:])
                    for j in range(4):
                        m = t.transpose(bank(6 + q % 2)[0:CB, j * P:(j + 1) * P], o_rows[:, 4 * q + j, P:C],
                                        ident[:])
                    m.then_inc(sem("oT_psum"), 1)

                def values(q):
                    pe.wait_ge(sem("oTa_ready"), q0 + q + 1)
                    pe.wait_ge(sem("oTb_ready"), q0 + q + 1)
                    if q >= 2:
                        pe.wait_ge(sem("avT_ready"), q0 + q - 1)
                    for j in range(4):
                        h = 4 * q + j
                        o = bank(q % 2)[0:d, j * P:(j + 1) * P]
                        t.matmul(o, xwva[:, h * d:(h + 1) * d], oT_a[:, q % 2, j * P:(j + 1) * P],
                                 start=True, stop=False)
                        m = t.matmul(o, xwvb[:, h * d:(h + 1) * d], oT_b[:, q % 2, j * P:(j + 1) * P],
                                     start=False, stop=True)
                    m.then_inc(sem("avT_psum"), 1)

                def project(q):
                    pe.wait_ge(sem("avT_ready"), q0 + q + 1)
                    for j in range(4):
                        h = 4 * q + j
                        m = t.matmul(bank(2)[:, 0:D], avT[0:d, q % 2, j * P:(j + 1) * P], xwo[0:d, h, :],
                                     start=(h == 0), stop=(h == h_n - 1))
                    m.then_inc(sem("wo_used"), 1)
                turn_o(0)
                for q in range(quads):
                    if q + 1 < quads:
                        turn_o(q + 1)
                    values(q)
                    project(q)
                pe.wait_ge(sem("xattn_done"), L + 1)

            def xattn_low(L):
                l = L - 2
                turn_x(3 * L)
                pe.wait_ge(xw_landed, xw_at[L])
                for j in range(WP):
                    for c in range(DC):
                        m = t.matmul(bank(4, 2)[:, j * P:(j + 1) * P],
                                     xwq[:, c, j * P:(j + 1) * P],
                                     xnT[:, c, :], start=(c == 0), stop=(c == DC - 1))
                m.then_inc(sem("low_q_psum"), 1)
                pe.wait_ge(sem("low_q_ready"), l + 1)
                pe.wait_ge(sem("key_ones"), l + 1)
                base = UNITS * l

                def pair_scores(b, k, half, pair):
                    sc = bank(2 * pair, 2)
                    for j in range(4):
                        m = t.matmul(sc[:, j * 256:(j + 1) * 256],
                                     kbuf[:, b, 4 * half + j, k * P:(k + 1) * P],
                                     mq[:, (4 * half + j) * 256:(4 * half + j + 1) * 256], start=True, stop=True)
                    return m

                def max_units(it):
                    for u in range(UBODY):
                        b, k, half = u // (2 * G), u // 2 % G, u % 2
                        if u % (2 * G) == 0:
                            pe.wait_ge(k_landed[b], it * 48 + 48 * (2 * ITERS * l + 1))
                        if u % 4 == 0:
                            wait_count(pe, sem("low_max_taken"), it * UBODY + (base + u - 3))
                        else:
                            wait_count(pe, sem("low_max_copied"), it * (3 * G) + low_copies(l, u) - 3)
                        pair_scores(b, k, half, u % 4).then_inc(sem("low_max_scores"), 1)
                sweep_loop(pe, max_units, l == 0, False)

                pe.wait_ge(sem("low_max_merged"), l + 1)
                rows = runmax.rearrange("p a n -> p (a n)")
                for h in range(WH):
                    m = t.transpose(bank(0, 4)[:, h * P:(h + 1) * P], rows[:, h * P:(h + 1) * P], ident[:])
                m.then_inc(sem("low_max_turned"), 1)
                pe.wait_ge(sem("low_diagonals"), l + 1)
                for b in range(4):
                    m = t.matmul(bank(b), ones[:], rows[:, b * BANK:(b + 1) * BANK], start=True, stop=True)
                m.then_inc(sem("low_max_ready"), 1)
                pe.wait_ge(sem("low_q_shifted"), l + 1)
                for b in range(4 if L == 2 else 2):
                    t.matmul(bank(b), zrow[:, 0:P], zrow[:], start=True, stop=False, skip_group_check=True)
                freed = sem("low_clipped") if L == 2 else sem("low_exp_ready")

                def scores(it, u):
                    b, k, half = u // (2 * G), u // 2 % G, u % 2
                    if u % (2 * G) == 0:
                        pe.wait_ge(k_landed[b], it * 48 + 48 * (2 * ITERS * l + ITERS + 1))
                    wait_count(pe, freed, it * UBODY + ((0 if L == 2 else base) + u - 1))
                    pair_scores(b, k, half, 2 + half).then_inc(sem("low_scores"), 1)

                def pv(it, u):
                    b, k, half = u // (2 * G), u // 2 % G, u % 2
                    if u % (2 * G) == 0:
                        pe.wait_ge(v_landed[b], it * 16 + 16 * (ITERS * l + 1))
                    pe.wait_ge(sem(lo_maker(l, u)), lo_made(l, it, u))
                    if L == 2 and half == 0:
                        for q in range(2):
                            t.matmul(bank(2 + q)[:, 0:8 * VW], onesb[:],
                                     vbuf[:, b, k, 8 * q:8 * q + 8, :].rearrange("p h w -> p (h w)"),
                                     start=False, stop=False, skip_group_check=True)
                    for j in range(HG):
                        o = bank(half)[:, j * 64:j * 64 + VW - 1]
                        v = vbuf[:, b, k, HG * half + j, :]
                        t.matmul(o, low_hi(u)[:, j * P:(j + 1) * P], v[:, 0:VW - 1], start=False,
                                 stop=False, skip_group_check=True)
                        m = t.matmul(o[:, 0:WH + 1], low_lo(u)[:, j * P:(j + 1) * P], v[:, 0:WH + 1],
                                     start=False, stop=False, skip_group_check=True)
                    m.then_inc(sem("low_pv_done"), 1)

                def units(it):
                    last = isinstance(it, int) and it == ITERS - 1
                    for u in range(UBODY):
                        if u + LEAD < UBODY:
                            scores(it, u + LEAD)
                        elif not last:
                            scores(it + 1, u + LEAD - UBODY)
                        pv(it, u)
                for u in range(LEAD):
                    scores(0, u)
                sweep_loop(pe, units, True, True)
                pe.wait_ge(sem("low_o_ready"), l + 1)
                for c in range(DC):
                    m = t.transpose(bank(5)[:, c * P:(c + 1) * P], a_o[:, c * P:(c + 1) * P], ident[:])
                m.then_inc(sem("low_oT_psum"), 1)
                pe.wait_ge(sem("low_oT_ready"), l + 1)
                for c in range(DC):
                    m = t.matmul(bank(6)[:, 0:D], a_oT[:, c, :], xwo2[:, c, :], start=(c == 0), stop=(c == DC - 1))
                m.then_inc(sem("low_out_psum"), 1)
                pe.wait_ge(sem("xattn_done"), L + 1)

            def attn(L):
                parts, d, heads = AH[L], AD[L], AS[L]
                turn_x(3 * L + 1)
                pe.wait_ge(aw_landed, aw_at[L])
                kv_in = xnT
                if L == 3:
                    pe.wait_ge(sem("reversal_ready"), 1)
                    for c in range(DC):
                        m = t.matmul(bank(1)[:, c * P:(c + 1) * P], xn[:, c * P:(c + 1) * P], win_block[:],
                                     start=True, stop=True)
                    m.then_inc(sem("xnT_rev_psum"), 1)
                    pe.wait_ge(sem("xnT_rev_ready"), 1)
                    kv_in = xnT_rev
                for w, first_bank in ((0, 0), (1, 4)):
                    for h in range(parts):
                        for c in range(DC):
                            m = t.matmul(bank(first_bank, 4)[0:d, h * P:(h + 1) * P],
                                         aw[:, c, w * D + h * d:w * D + (h + 1) * d], (kv_in if w else xnT)[:, c, :],
                                         start=(c == 0), stop=(c == DC - 1))
                    m.then_inc(sem("attn_qk_psum"), 1)
                pe.wait_ge(sem("attn_k_ready"), L + 1)
                for c in range(DC):
                    m = t.matmul(bank(7)[:, 0:D], kv_in[:, c, :], aw[:, c, 2 * D:3 * D], start=(c == 0),
                                 stop=(c == DC - 1))
                m.then_inc(sem("attn_v_psum"), 1)
                pe.wait_ge(sem("attn_q_ready"), L + 1)
                per = parts // heads
                for h in range(heads):
                    for c in range(per):
                        g = h * per + c
                        m = t.matmul(bank(0, 4)[:, h * P:(h + 1) * P], a_q[0:d, g * P:(g + 1) * P],
                                     a_k[0:d, g * P:(g + 1) * P], start=(c == 0), stop=(c == per - 1))
                m.then_inc(sem("attn_scores"), 1)
                pe.wait_ge(sem("attn_probs"), L + 1)
                for h in range(heads):
                    m = t.transpose(bank(0, 4)[:, h * P:(h + 1) * P], a_S[:, h * P:(h + 1) * P], ident[:])
                m.then_inc(sem("attn_pT_psum"), 1)
                pe.wait_ge(sem("attn_pT_ready"), L + 1)
                pe.wait_ge(sem("attn_v_ready"), L + 1)
                w = D // heads
                for h in range(heads):
                    m = t.matmul(bank(4)[:, h * w:(h + 1) * w], a_T[:, h * P:(h + 1) * P],
                                 a_v[:, h * w:(h + 1) * w], start=True, stop=True)
                m.then_inc(sem("attn_o_psum"), 1)
                pe.wait_ge(sem("attn_o_ready"), L + 1)
                for c in range(DC):
                    m = t.transpose(bank(5)[:, c * P:(c + 1) * P], a_o[:, c * P:(c + 1) * P], ident[:])
                m.then_inc(sem("attn_oT_psum"), 1)
                pe.wait_ge(sem("attn_oT_ready"), L + 1)
                for c in range(DC):
                    m = t.matmul(bank(6)[:, 0:D], a_oT[:, c, :], aw[:, c, 3 * D:4 * D], start=(c == 0),
                                 stop=(c == DC - 1))
                m.then_inc(sem("attn_out_psum"), 1)
                pe.wait_ge(sem("attn_done"), L + 1)

            def route(L, e):
                turn_x(3 * L + 2)
                if L == 0:
                    pe.wait_ge(const_landed, CONSTS_ALL - 16 * EARLY)
                for c in range(DC):
                    m = t.matmul(bank(1)[:, 0:e], xnT[:, c, :], rw[:, L, c, 0:e], start=(c == 0), stop=(c == DC - 1))
                m.then_inc(sem("logits_psum"), 1)

            def glu_experts(L, base):
                f = FW[L]
                fc = f // 2
                t.matmul(bank(2)[:, 0:D], zrow[:, 0:P], zrow[:, 0:D], start=True, stop=False,
                         skip_group_check=True)

                def gate_up(slot, landed, par, free):
                    pe.wait_ge(ring_landed[slot], landed)
                    wait_count(pe, sem("h_ready"), free)
                    v = gu_view(slot, f)
                    for half in range(2):
                        for c in range(DC):
                            m = t.matmul(bank(4 + 2 * par + half)[:, 0:f], xnT[:, c, :],
                                         v[:, c, half * f:(half + 1) * f], start=(c == 0), stop=(c == DC - 1))
                    m.then_inc(sem("gu_psum"), 1)

                def turn(par, h_at):
                    pe.wait_ge(sem("h_ready"), h_at)
                    for c in range(2):
                        m = t.transpose(bank(par)[0:fc, c * P:(c + 1) * P], h_s[:, par, c * fc:(c + 1) * fc],
                                        ident[:])
                    m.then_inc(sem("hT_psum"), 1)

                def down(slot, par, h_at):
                    pe.wait_ge(sem("hT_ready"), h_at)
                    dn = dn_view(slot, f)
                    for c in range(2):
                        m = t.matmul(bank(2)[:, 0:D], hT[0:fc, par, c * P:(c + 1) * P], dn[:, c, :],
                                     start=False, stop=False, skip_group_check=True)
                    m.then_inc(sem("ring_used"), 1)
                return gate_up, turn, down

            GLU0 = [0, 0, NE[0], 0]

            def ffn_glu(L):
                route(L, 8 if L == 0 else 64)
                gate_up, turn, down = glu_experts(L, GLU0[L])
                b0 = GLU0[L]
                n_e = NE[L]
                for e in range(2):
                    gate_up(e, landed_at(L, e), e % 2, b0 + e - 1)
                turn(0, b0 + 1)
                loops = 0
                if L == 2:
                    loops = 64 // RING - 1
                    step = 16 * RING_DMAS[L]
                    with pe.Fori(0, loops) as it:
                        for j in range(RING):
                            gate_up((j + 2) % RING, it * step + landed_at(L, j + 2), j % 2, it * RING + (b0 + j + 1))
                            turn((j + 1) % 2, it * RING + (b0 + j + 2))
                            down(j, j % 2, it * RING + (b0 + j + 1))
                for e in range(loops * RING, n_e):
                    if e + 2 < n_e:
                        gate_up((e + 2) % RING, landed_at(L, e + 2), e % 2, b0 + e + 1)
                    if e + 1 < n_e:
                        turn((e + 1) % 2, b0 + e + 2)
                    down(e % RING, e % 2, b0 + e + 1)
                pe.wait_ge(sem("ffn_done"), L + 1)

            def ffn1():
                route(1, 32)
                for e in range(NE[1]):
                    pe.wait_ge(ring_landed[e % RING], landed_at(1, e))
                    if e >= 2:
                        pe.wait_ge(sem("l1_step"), 2 * (e - 1))
                    v = gu_view(e % RING, 256)
                    for c in range(DC):
                        m = t.matmul(bank(4 + e % 2), xnT[:, c, :], v[:, c, :], start=(c == 0), stop=(c == DC - 1))
                    m.then_inc(sem("ring_used"), 1)
                pe.wait_ge(sem("ffn_done"), 2)

            def ffn3():
                pe.wait_ge(sem("csq_ready"), 1)
                for c in range(DC):
                    m = t.matmul(bank(3)[:, 0:8], ones[:], csq[:, c, :], start=(c == 0), stop=(c == DC - 1))
                m.then_inc(sem("cnorm_psum"), 1)
                route(3, 16)
                pe.wait_ge(sem("comb_ready"), 1)
                t.transpose(bank(2)[0:8, 0:P], comb[:, 0:8], ident[:]).then_inc(sem("gT_psum"), 1)
                pe.wait_ge(sem("gT_ready"), 1)
                t.matmul(bank(3)[:, 0:D], gT, b2r[:], start=True, stop=True).then_inc(sem("b2_psum"), 1)

                def up(e):
                    slot = e % RING
                    pe.wait_ge(ring_landed[slot], landed_at(3, e))
                    if e >= 2:
                        pe.wait_ge(sem("gelu_ready"), e - 1)
                    w1 = ring(slot)[:, 0:DC * P].rearrange("p (c n) -> p c n", c=DC)
                    for c in range(DC):
                        m = t.matmul(bank(4 + e % 2)[:, 0:P], w1[:, c, :], xnT[:, c, :], start=(c == 0),
                                     stop=(c == DC - 1))
                    m.then_inc(sem("w1_psum"), 1)

                def down(e):
                    slot = e % RING
                    pe.wait_ge(sem("gelu_ready"), e + 1)
                    if e >= 2:
                        pe.wait_ge(sem("l3_taken"), e - 1)
                    t.matmul(bank(6 + e % 2)[:, 0:D], hT[:, e % 2, 0:P], ring(slot)[:, 1024:1024 + D],
                             start=True, stop=True).then_inc(sem("ring_used"), 1)
                up(0)
                for e in range(8):
                    if e < 7:
                        up(e + 1)
                    down(e)

            for s in range(stages):
                L = s // 3
                if s % 3 == 0:
                    (xattn if L < 2 else xattn_low)(L)
                elif s % 3 == 1:
                    attn(L)
                elif L in (0, 2):
                    ffn_glu(L)
                elif L == 1:
                    ffn1()
                else:
                    ffn3()

        @block.scalar
        def _(act):
            a = nc.scalar

            def std(s):
                act.wait_ge(sem("var_ready"), s + 1)
                a.activation(rstd[:], rstd[:], ACT.Sqrt).then_inc(sem("std_ready"), 1)

            def split_ctx(g, b):
                act.wait_ge(sem("ctxT_psum"), g + 1)
                wait_count(act, stream_out[b], (g - b) * 8)
                a.activation(sbuf2[:, b, :, S_A:S_A + P],
                             bank(0, 2)[:, 0:GK].rearrange("p (g k) -> p g k", g=G), ACT.Copy
                             ).then_inc(sem("act_split"), 1)
                a.activation(sbuf2[0:CB, b, :, S_B:S_B + P],
                             bank(2, 2)[0:CB, 0:GK].rearrange("p (g k) -> p g k", g=G), ACT.Copy
                             ).then_inc(sem("act_split"), 1)
                a.activation(sbuf2[0:CB, b, :, S_D:S_D + P],
                             bank(2, 2)[0:CB, 0:GK].rearrange("p (g k) -> p g k", g=G), ACT.Copy
                             ).then_inc(sem("act_split"), 1)

            def rows_high(b):
                a.activation(sbuf2[:, b, :, S_R:S_R + C], ctx_in[:, b], ACT.Copy).then_inc(sem("act_rows"), 1)

            def proj_high(g, next_rows):
                u = 0
                wait_count(act, sem("keys_written"), g * 64)
                for mt in range(4):
                    for lo, hi in ((0, 4), (4, G)):
                        act.wait_ge(sem("proj_psum"), g * PROJ + (u + 1))
                        a.activation(kstage[:, mt, 0, lo * P:hi * P], bank(4 + u % 4)[:, 0:(hi - lo) * P], ACT.Copy
                                     ).then_inc(sem("proj_hi"), 1)
                        u += 1
                        if u == 3 and next_rows is not None:
                            rows_high(next_rows)
                act.wait_ge(sem("vstage_ones"), 1)
                wait_count(act, sem("values_written"), g * 32)
                for k in range(G):
                    act.wait_ge(sem("proj_psum"), g * PROJ + (u + 1))
                    a.activation(vstage[:, :, k, :, 0:WH],
                                 bank(4 + u % 4).rearrange("p (l h w) -> p l h w", l=2, h=WH), ACT.Copy
                                 ).then_inc(sem("proj_hi"), 1)
                    u += 1
            std(0)
            split_ctx(0, 0)
            rows_high(0)

            def prepare(it):
                last = isinstance(it, int) and it == ITERS - 1
                for b in range(2):
                    if not (last and b == 1):
                        split_ctx(it * 2 + (b + 1), 1 - b)
                    proj_high(it * 2 + b, None if last and b == 1 else 1 - b)
            sweep_loop(act, prepare, True, True)

            def xattn_low(L):
                l = L - 2
                base = UNITS * l

                def max_copies(it):
                    for u in range(UBODY):
                        if u % 4 == 0:
                            continue
                        act.wait_ge(sem("low_max_scores"), it * UBODY + (base + u + 1))
                        wait_count(act, sem("low_max_taken"), it * UBODY + (base + u - 3))
                        a.activation(max_copy(u % 4 - 1), bank(2 * (u % 4), 2), ACT.Copy
                                     ).then_inc(sem("low_max_copied"), 1)
                sweep_loop(act, max_copies, l == 0, False)

                def units(it):
                    for u in range(UBODY):
                        at = it * UBODY + (base + u)
                        if L == 2:
                            act.wait_ge(sem("low_clipped"), at + 1)
                            src = low_p(u)
                        else:
                            act.wait_ge(sem("low_scores"), at + 1)
                            act.wait_ge(sem("low_pv_done"), at + (1 - LOW_SLOTS))
                            src = bank(4 + 2 * (u % 2), 2)
                        a.activation(low_p(u), src, ACT.Exp).then_inc(sem("low_exp_ready"), 1)
                sweep_loop(act, units, True, False)

            def xattn(L):
                h_n, d = XH[L], XD[L]
                for s in range(SWEEPS[L]):
                    n = SWEEP0[L] + s
                    act.wait_ge(sem("qk_psum"), n + 1)
                    sc = d ** -0.5
                    if L == 0:
                        act.wait_ge(sem("qscale_ready"), 1)
                    a.activation(qf_a[:], bank(4, 2), ACT.Copy if L else ACT.Identity,
                                 scale=sc if L else qscale0[:, 0:1]).then_inc(sem("qf_ready"), 1)
                    a.activation(qf_b[0:CB + 1, :], bank(6, 2)[0:CB + 1, :], ACT.Copy if L else ACT.Identity,
                                 scale=sc if L else qscale0[0:CB + 1, 0:1]).then_inc(sem("qf_ready"), 1)
                    base = TILES * n

                    if n == 0:
                        act.wait_ge(sem("values_written"), 32 * GROUPS)

                    def max_copies(it):
                        for k in range(1, BODY, 2):
                            act.wait_ge(sem("max_scores_ready"), it * BODY + (base + k + 1))
                            wait_count(act, sem("max_taken"), it * BODY + (base + k - 5))
                            src = bank(2 * MAX_PAIR[k], 2)
                            dst = max_copy(k // 2 % STAGES_IN)
                            if L == 0:
                                m = a.activation(dst, src, ACT.Identity, bias=maskneg[:, bass.ds(it * BODY + k, 1)])
                            else:
                                m = a.activation(dst, src, ACT.Copy)
                            m.then_inc(sem("max_copied"), 1)
                    sweep_loop(act, max_copies, n == 0, False)

                    def exps(it):
                        for k in range(BODY):
                            act.wait_ge(sem("scores_ready"), it * BODY + (base + k + 1))
                            src = bank(4 + 2 * (k % 2), 2)
                            wait_count(act, sem("p_ready"), it * BODY + (base + k - 1))
                            bias = maskneg[:, bass.ds(it * BODY + k, 1)] if L == 0 else 0.0
                            a.activation(p32[:, k % 2], src, ACT.Exp, bias=bias).then_inc(sem("p32_ready"), 1)
                    sweep_loop(act, exps, True, False)
                q0 = sum(XH[:L]) // 4
                for q in range(h_n // 4):
                    act.wait_ge(sem("oT_psum"), q0 + q + 1)
                    if q >= 2:
                        act.wait_ge(sem("avT_psum"), q0 + q - 1)
                    a.activation(oT_b[:, q % 2, :], bank(6 + q % 2)[0:CB, :], ACT.Copy).then_inc(sem("oTb_ready"), 1)

            def attn(L):
                n = AS[L] * P
                if L == 2:
                    act.wait_ge(sem("l2_scaled"), 1)
                    a.activation(a_T, a_S, ACT.Sigmoid).then_inc(sem("l2_act"), 1)
                    act.wait_ge(sem("l2_act"), 1)
                    a.activation(a_T, a_T, ACT.Square).then_inc(sem("l2_act"), 1)
                    act.wait_ge(sem("l2_centred"), 1)
                    a.activation(a_U, a_U, ACT.Abs).then_inc(sem("l2_act"), 1)
                act.wait_ge(sem("attn_shifted"), L + 1)
                a.activation(a_S[:, 0:n], a_S[:, 0:n], ACT.Exp).then_inc(sem("attn_probs"), 1)
                act.wait_ge(sem("attn_pT_psum"), L + 1)
                a.activation(a_T[:, 0:n], bank(0, 4)[:, 0:n], ACT.Copy).then_inc(sem("attn_pT_ready"), 1)

            def ffn_glu(L):
                f = FW[L]
                act.wait_ge(sem("route_shifted"), L + 1)
                a.activation(prob[:, 0:8 if L == 0 else 64], logit[:, 0:8 if L == 0 else 64], ACT.Exp
                             ).then_inc(sem("route_exp"), 1)
                b0 = 0 if L == 0 else NE[0]

                def one(par, at):
                    act.wait_ge(sem("gu_psum"), at)
                    wait_count(act, sem("h_ready"), at - 2)
                    a.activation(g_s[:, par, 0:f], bank(4 + 2 * par)[:, 0:f], ACT.Silu).then_inc(sem("silu"), 1)
                if L == 0:
                    for e in range(NE[0]):
                        one(e % 2, e + 1)
                else:
                    with act.Fori(0, 64 // RING) as it:
                        for j in range(RING):
                            one(j % 2, it * RING + (b0 + j + 1))
                    one(0, b0 + 65)

            def ffn1():
                act.wait_ge(sem("route_shifted"), 2)
                a.activation(prob[:, 0:32], logit[:, 0:32], ACT.Exp).then_inc(sem("route_exp"), 1)

            def ffn3():
                act.wait_ge(sem("cnorm_psum"), 1)
                a.activation(cnorm[:], bank(3)[:, 0:8], ACT.Sqrt).then_inc(sem("norms_ready"), 1)
                act.wait_ge(sem("xsq_ready"), 1)
                a.activation(rsum[:], rsum[:], ACT.Sqrt).then_inc(sem("norms_ready"), 1)
                act.wait_ge(sem("route_shifted"), 4)
                a.activation(prob[:, 0:8], logit[:, 0:8], ACT.Exp).then_inc(sem("route_exp"), 1)
                for e in range(8):
                    act.wait_ge(sem("w1_psum"), e + 1)
                    if e >= 2:
                        act.wait_ge(sem("ring_used"), NE0[3] + e - 1)
                    a.activation(hT[:, e % 2, 0:P], bank(4 + e % 2)[:, 0:P], ACT.Gelu, bias=b1T[:, e:e + 1]
                                 ).then_inc(sem("gelu_ready"), 1)

            for s in range(stages):
                L = s // 3
                if s:
                    std(s)
                if s % 3 == 0:
                    (xattn if L < 2 else xattn_low)(L)
                elif s % 3 == 1:
                    attn(L)
                elif L in (0, 2):
                    ffn_glu(L)
                elif L == 1:
                    ffn1()
                else:
                    ffn3()

        @block.vector
        def _(dve):
            v = nc.vector
            chain = [0]

            def link(ins):
                chain[0] += 1
                ins.then_inc(sem("dve_chain"), 1)
                dve.wait_ge(sem("dve_chain"), chain[0])

            def spread_maxima(heads, dst, clamped):
                m = a_m[:, 0:heads]
                link(v.tensor_reduce(m, bank(0, heads // 4).rearrange("p (h n) -> p h n", h=heads), AX_X, ALU.max))
                if clamped:
                    link(v.tensor_scalar(a_s[:, 0:heads], m, 1.0 - MARGIN, None, ALU.mult))
                    link(v.scalar_tensor_tensor(m, m, 1.0 + MARGIN, a_s[:, 0:heads], ALU.mult, ALU.max))
                    link(v.tensor_scalar(m, m, CLAMP, -CLAMP, ALU.min, ALU.max))
                else:
                    link(v.tensor_scalar(m, m, LARGEST, -LARGEST, ALU.min, ALU.max))
                return v.tensor_tensor(dst.rearrange("p (h n) -> p h n", h=heads),
                                       ident[:].unsqueeze(1).to_broadcast([P, heads, P]),
                                       m.unsqueeze(2).to_broadcast([P, heads, P]), ALU.mult)

            def norm(s):
                link(v.bn_stats(stats[:], x[:]))
                link(v.bn_aggr(mv[:], stats[:]))
                v.tensor_scalar(rstd[:], mv[:, 1:2], EPS, None, ALU.add).then_inc(sem("var_ready"), 1)
                dve.wait_ge(sem("std_ready"), s + 1)
                link(v.reciprocal(rstd[:], rstd[:]))
                v.tensor_scalar(xn[:], x[:], mv[:, 0:1], rstd[:, 0:1], ALU.subtract, ALU.mult
                                ).then_inc(sem("xn_ready"), 1)
                dve.wait_ge(sem("xnT_psum"), s + 1)
                v.tensor_copy(xnT[:].rearrange("p c n -> p (c n)"), bank(0)[:, 0:D]).then_inc(sem("xnT_ready"), 1)
                dve.wait_ge(sem("xnT_ready"), s + 1)

            link(v.memset(q_d1[:], 0.0))
            link(v.memset(q_d2[:], 0.0))
            dve.wait_ge(sem("early_landed"), 16 * EARLY)
            link(v.tensor_copy(keep[:], keep_u8[:]))
            link(v.tensor_scalar(keep[:], keep[:], 0.0, None, ALU.is_gt))
            v.tensor_reduce(any_keep[:], keep[:], AX_X, ALU.max).then_inc(sem("keep_ready"), 1)
            norm(0)

            def split_weights():
                link(v.tensor_copy(qh_a[:], qf_a[:]))
                v.tensor_tensor(ql_a[:], qf_a[:], qh_a[:], ALU.subtract)
                v.tensor_copy(q_bb[0:CB, :], qf_b[0:CB, :])
                v.tensor_copy(q_bb[CB:P, :], qf_b[0:CB, :])
                link(v.tensor_copy(q_d1[0:CB + 1, :], qf_b[0:CB + 1, :]))
                v.tensor_tensor(q_d2[0:CB, :], qf_b[0:CB, :], q_d1[0:CB, :], ALU.subtract)
                v.tensor_copy(q_d2[BIAS_HI:BIAS_HI + 1, :], q_d1[BIAS_HI:BIAS_HI + 1, :])
                v.tensor_tensor(q_d2[BIAS_LO:BIAS_LO + 1, :], qf_b[BIAS_HI:BIAS_HI + 1, :],
                                q_d1[BIAS_HI:BIAS_HI + 1, :], ALU.subtract).then_inc(sem("kv_pieces_ready"), 1)
            dve.wait_ge(sem("kv_weights_landed"), 32)
            split_weights()

            def split_ctx(g, b):
                dve.wait_ge(sem("act_split"), g * 3 + 1)
                v.tensor_tensor(sbuf2[:, b, :, S_C:S_C + P],
                                bank(0, 2)[:, 0:GK].rearrange("p (g k) -> p g k", g=G),
                                sbuf2[:, b, :, S_A:S_A + P], ALU.subtract)
                dve.wait_ge(sem("act_split"), g * 3 + 3)
                v.tensor_tensor(sbuf2[CB:P, b, :, S_B:S_B + P],
                                bank(2, 2)[0:CB, 0:GK].rearrange("p (g k) -> p g k", g=G),
                                sbuf2[0:CB, b, :, S_B:S_B + P], ALU.subtract).then_inc(sem("dve_split"), 1)

            def proj_low(g):
                u = 0
                for mt in range(4):
                    for lo, hi in ((0, 4), (4, G)):
                        dve.wait_ge(sem("proj_hi"), g * PROJ + (u + 1))
                        v.tensor_tensor(kstage[:, mt, 1, lo * P:hi * P], bank(4 + u % 4)[:, 0:(hi - lo) * P],
                                        kstage[:, mt, 0, lo * P:hi * P], ALU.subtract
                                        ).then_inc(sem("proj_lo"), 1)
                        u += 1
                for k in range(G):
                    dve.wait_ge(sem("proj_hi"), g * PROJ + (u + 1))
                    v.tensor_tensor(vstage[:, :, k, :, WH + 1:2 * WH + 1],
                                    bank(4 + u % 4).rearrange("p (l h w) -> p l h w", l=2, h=WH),
                                    vstage[:, :, k, :, 0:WH], ALU.subtract).then_inc(sem("proj_lo"), 1)
                    u += 1
            def queries(L):
                q0 = sum(XH[:L]) // 4
                for q in range(XH[L] // 4):
                    dve.wait_ge(sem("qT_psum"), q0 + q + 1)
                    o = qT[0:XD[L], 4 * q:4 * q + 4, :]
                    i = bank(QUERY_BANK[L] + q)[0:XD[L], :].rearrange("p (h n) -> p h n", h=4)
                    v.tensor_copy(o, i).then_inc(sem("qT_ready"), 1)
            split_ctx(0, 0)
            queries(0)
            dve.wait_ge(sem("consts_made"), 1)
            by_half = ident[:].rearrange("p (a b c) -> p b a c", a=4, b=2)
            v.tensor_reduce(half_a[:], by_half[:, 0], mybir.AxisListType.XY, ALU.add)
            v.tensor_reduce(half_b[:], by_half[:, 1], mybir.AxisListType.XY, ALU.add)
            dve.wait_ge(sem("alive_ready"), 1)
            v.tensor_scalar(qscale0[:], alive[:], XD[0] ** -0.5, None, ALU.mult).then_inc(sem("qscale_ready"), 1)
            link(v.tensor_scalar(maskneg[:], keep[:], -NEG, NEG, ALU.mult, ALU.add))
            link(v.tensor_scalar(maskneg[:], maskneg[:], alive[:, 0:1], None, ALU.mult))

            def prepare(it):
                last = isinstance(it, int) and it == ITERS - 1
                for b in range(2):
                    if not (last and b == 1):
                        split_ctx(it * 2 + (b + 1), 1 - b)
                    proj_low(it * 2 + b)
            sweep_loop(dve, prepare, True, True)
            dve.wait_ge(const_landed, CONSTS_ALL - 16 * EARLY)

            def xattn(L):
                h_n, d = XH[L], XD[L]
                quads = h_n // 4
                q0 = sum(XH[:L]) // 4
                if L:
                    norm(3 * L)
                    queries(L)
                for s in range(SWEEPS[L]):
                    n = SWEEP0[L] + s
                    base = TILES * n
                    dve.wait_ge(sem("qf_ready"), 2 * n + 1)
                    link(v.tensor_copy(qh_a[:], qf_a[:]))
                    v.tensor_tensor(ql_a[:], qf_a[:], qh_a[:], ALU.subtract)
                    dve.wait_ge(sem("qf_ready"), 2 * n + 2)
                    v.tensor_copy(q_bb[0:CB, :], qf_b[0:CB, :])
                    v.tensor_copy(q_bb[CB:P, :], qf_b[0:CB, :])
                    link(v.tensor_copy(q_d1[0:CB + 1, :], qf_b[0:CB + 1, :]))
                    v.tensor_tensor(q_d2[0:CB, :], qf_b[0:CB, :], q_d1[0:CB, :], ALU.subtract)
                    v.tensor_tensor(q_d1[BIAS_LO:BIAS_LO + 1, :], qf_b[BIAS_HI:BIAS_HI + 1, :],
                                    q_d1[BIAS_HI:BIAS_HI + 1, :], ALU.subtract).then_inc(sem("q_hi_ready"), 1)
                    if n == 0:
                        dve.wait_ge(sem("keys_written"), 64 * GROUPS)
                        dve.wait_ge(sem("values_written"), 32 * GROUPS)
                    v.memset(acc16[:, 0], NEG)
                    link(v.memset(runmax[:, 0], NEG))

                    def take_max(it):
                        for k in range(BODY):
                            wait_count(dve, sem("max_taken"), it * BODY + (base + k - 1))
                            if k % 2:
                                dve.wait_ge(sem("max_copied"), it * G + ((base + k + 1) // 2))
                                m = v.tensor_tensor(acc16[:, 0], max_copy(k // 2 % STAGES_IN), acc16[:, 0], ALU.max)
                            else:
                                dve.wait_ge(sem("max_scores_ready"), it * BODY + (base + k + 1))
                                src = bank(2 * MAX_PAIR[k], 2)
                                if L == 0:
                                    m = v.scalar_tensor_tensor(runmax[:, 0], src,
                                                               maskneg[:, bass.ds(it * BODY + k, 1)], runmax[:, 0],
                                                               ALU.add, ALU.max)
                                else:
                                    m = v.tensor_tensor(runmax[:, 0], src, runmax[:, 0], ALU.max)
                            m.then_inc(sem("max_taken"), 1)
                    sweep_loop(dve, take_max, n == 0, False)
                    dve.wait_ge(sem("max_taken"), base + TILES)
                    v.tensor_tensor(runmax[:, 0], runmax[:, 0], acc16[:, 0], ALU.max
                                    ).then_inc(sem("max_merged"), 1)
                    dve.wait_ge(sem("max_turned"), n + 1)
                    spread_maxima(HG, runmax[:, 1], False).then_inc(sem("max_diagonals"), 1)
                    dve.wait_ge(sem("max_ready"), n + 1)
                    hi = slice(BIAS_HI, BIAS_HI + 1)
                    link(v.tensor_tensor(qf_b[hi, :], qf_b[hi, :], bank(2, 2)[hi, :], ALU.subtract))
                    link(v.tensor_copy(q_d2[hi, :], qf_b[hi, :]))
                    v.tensor_tensor(q_d2[BIAS_LO:BIAS_LO + 1, :], qf_b[hi, :], q_d2[hi, :],
                                    ALU.subtract).then_inc(sem("q_all_ready"), 1)

                    def split_p(it, k):
                        dve.wait_ge(sem("p32_ready"), it * BODY + (base + k + 1))
                        wait_count(dve, sem("pv_done"), it * BODY + (base + k - 1))
                        v.tensor_copy(phi[:, k % 2], p32[:, k % 2]).then_inc(sem("phi_ready"), 1)
                        dve.wait_ge(sem("phi_ready"), it * BODY + (base + k + 1))
                        v.tensor_tensor(plo[:, k % 2], p32[:, k % 2], phi[:, k % 2], ALU.subtract
                                        ).then_inc(sem("p_ready"), 1)

                    def p_tiles(it):
                        for k in range(BODY):
                            split_p(it, k)
                    sweep_loop(dve, p_tiles, n == 0, False)
                    dve.wait_ge(sem("pv_done"), base + TILES)
                    acc = bank(0, 4).rearrange("p (h n) -> p h n", h=HG)
                    dn = den[:, HG * s:HG * s + HG]
                    rd = rden[:, HG * s:HG * s + HG]
                    link(v.tensor_copy(dn, acc[:, :, C]))
                    link(v.reciprocal(rd, dn))
                    v.tensor_tensor(o_rows[:, HG * s:HG * s + HG, :], acc[:, :, 0:C],
                                    rd.unsqueeze(2).to_broadcast([P, HG, C]), ALU.mult
                                    ).then_inc(sem("o_rows_ready"), 1)
                for q in range(quads):
                    dve.wait_ge(sem("oT_psum"), q0 + q + 1)
                    if q >= 2:
                        dve.wait_ge(sem("avT_psum"), q0 + q - 1)
                    v.tensor_copy(oT_a[:, q % 2, :], bank(4 + q % 2)).then_inc(sem("oTa_ready"), 1)
                    dve.wait_ge(sem("avT_psum"), q0 + q + 1)
                    if q >= 2:
                        dve.wait_ge(sem("wo_used"), q0 + q - 1)
                    v.tensor_copy(avT[0:d, q % 2, :], bank(q % 2)[0:d, :]).then_inc(sem("avT_ready"), 1)
                link(v.tensor_tensor(x[:], x[:], bo_all[:, L, :], ALU.add))
                dve.wait_ge(sem("wo_used"), q0 + quads)
                v.tensor_tensor(x[:], bank(2)[:, 0:D], x[:], ALU.add).then_inc(sem("xattn_done"), 1)
                dve.wait_ge(sem("xattn_done"), L + 1)

            def xattn_low(L):
                l = L - 2
                base = UNITS * l
                norm(3 * L)
                q3 = qf_a[:].rearrange("p (j n) -> p j n", j=WP)
                mq4 = mq.rearrange("p (j b n) -> p j b n", j=WP, b=2)
                dve.wait_ge(sem("low_q_psum"), l + 1)
                link(v.tensor_tensor(q3, bank(4, 2).rearrange("p (j n) -> p j n", j=WP),
                                     xbq4[:, l, :].unsqueeze(2).to_broadcast([P, WP, P]), ALU.add))
                link(v.tensor_scalar(qf_a[:], qf_a[:], WH ** -0.5, None, ALU.mult))
                link(v.tensor_copy(qh_a[:], qf_a[:]))
                link(v.tensor_tensor(ql_a[:], qf_a[:], qh_a[:], ALU.subtract))
                for half, mine in ((0, half_a), (1, half_b)):
                    v.tensor_scalar(mq4[0:64, :, half, :], qh_a[0:64, :].rearrange("p (j n) -> p j n", j=WP),
                                    mine[0:64, 0:1], None, ALU.mult)
                    v.tensor_scalar(mq4[64:96, :, half, :], ql_a[64:96, :].rearrange("p (j n) -> p j n", j=WP),
                                    mine[64:96, 0:1], None, ALU.mult)
                v.memset(mq[96:P, :], 0.0).then_inc(sem("low_q_ready"), 1)
                v.memset(acc16, NEG)
                link(v.memset(runmax, NEG))

                def take_max(it):
                    for u in range(UBODY):
                        wait_count(dve, sem("low_max_taken"), it * UBODY + (base + u - 1))
                        if u % 4 == 0:
                            dve.wait_ge(sem("low_max_scores"), it * UBODY + (base + u + 1))
                            m = v.tensor_tensor(runmax[:, 0], bank(0, 2), runmax[:, 0], ALU.max)
                        else:
                            dve.wait_ge(sem("low_max_copied"), it * (3 * G) + low_copies(l, u))
                            m = v.tensor_tensor(acc16[:, u % 2], max_copy(u % 4 - 1), acc16[:, u % 2], ALU.max)
                        m.then_inc(sem("low_max_taken"), 1)
                sweep_loop(dve, take_max, l == 0, False)
                dve.wait_ge(sem("low_max_taken"), base + UNITS)
                v.tensor_tensor(runmax, runmax, acc16, ALU.max).then_inc(sem("low_max_merged"), 1)
                dve.wait_ge(sem("low_max_turned"), l + 1)
                spread_maxima(WH, runmax.rearrange("p a n -> p (a n)"), L == 2).then_inc(sem("low_diagonals"), 1)
                dve.wait_ge(sem("low_max_ready"), l + 1)
                maxima = bank(0, 4)
                r = slice(96, P)
                th = qf_a[:].bitcast(BF16)
                tl = qf_b[:].bitcast(BF16)
                link(v.tensor_scalar(th, maxima, -1.0, None, ALU.mult))
                link(v.scalar_tensor_tensor(tl, maxima, -1.0, th, ALU.mult, ALU.subtract))
                link(v.tensor_scalar(mq[r, :], tl[r, :], ident[r, 97:98], None, ALU.mult))
                v.scalar_tensor_tensor(mq[r, :], th[r, :], ident[r, 96:97], mq[r, :], ALU.mult, ALU.add
                                       ).then_inc(sem("low_q_shifted"), 1)
                dve.wait_ge(sem("low_q_shifted"), l + 1)
                if L == 2:
                    link(v.scalar_tensor_tensor(maxl, th, -CLAMP, tl, ALU.add, ALU.add))

                def low_part(u, at):
                    dve.wait_ge(sem("low_exp_ready"), at + 1)
                    wait_count(dve, sem("low_pv_done"), at + (1 - LO_SLOTS))
                    v.tensor_tensor(low_lo(u), low_p(u), low_hi(u), ALU.subtract).then_inc(sem("low_lo_dve"), 1)

                def units(it):
                    for u in range(UBODY):
                        at = it * UBODY + (base + u)
                        if L == 2:
                            dve.wait_ge(sem("low_scores"), at + 1)
                            wait_count(dve, sem("low_pv_done"), at + (1 - LOW_SLOTS))
                            v.scalar_tensor_tensor(low_p(u), bank(4 + 2 * (u % 2), 2), 0.0,
                                                   maxl[:, (u % 2) * QC:(u % 2 + 1) * QC], ALU.min, ALU.max
                                                   ).then_inc(sem("low_clipped"), 1)
                            if u >= 2 and lo_maker(l, u - 2) == "low_lo_dve":
                                low_part(u - 2, it * UBODY + (base + u - 2))
                        elif lo_maker(l, u) == "low_lo_dve":
                            low_part(u, at)
                sweep_loop(dve, units, L == 2, False)
                dve.wait_ge(sem("low_pv_done"), base + UNITS)

                def joined(acc, dst):
                    d3 = dst.rearrange("p (h n) -> p h n", h=WH)
                    link(v.tensor_copy(d3, acc[:, :, WH + 1:2 * WH + 1]))
                    link(v.tensor_tensor(d3, acc[:, :, 0:WH], d3, ALU.add))
                    link(v.tensor_copy(den[:], acc[:, :, WH]))
                    link(v.reciprocal(rden[:], den[:]))
                    return v.tensor_tensor(d3, d3, rden[:].unsqueeze(2).to_broadcast([P, WH, WH]), ALU.mult)
                if L == 2:
                    for q in range(2):
                        sums = bank(2 + q)[:, 0:8 * VW].rearrange("p (h w) -> p h w", h=8)
                        v.tensor_copy(vsum[:, 8 * q:8 * q + 8, :], sums)
                    link(v.memset(a_m[:], 0.0))
                    link(joined(vsum, vmean))
                acc = bank(0, 2).rearrange("p (h w) -> p h w", h=WH)
                done = joined(acc, a_o)
                if L == 2:
                    link(done)
                    link(v.tensor_tensor(nanf[:], den[:], den[:], ALU.not_equal))
                    v.tensor_reduce(nan1[:], nanf[:], AX_X, ALU.max).then_inc(sem("nan_local"), 1)
                    dve.wait_ge(sem("nan_ready"), 1)
                    done = v.copy_predicated(a_o, nana[:, 0:1].bitcast(U32).to_broadcast([P, D]), vmean)
                done.then_inc(sem("low_o_ready"), 1)
                dve.wait_ge(sem("low_oT_psum"), l + 1)
                v.tensor_copy(a_oT.rearrange("p c n -> p (c n)"), bank(5)[:, 0:D]).then_inc(sem("low_oT_ready"), 1)
                link(v.tensor_tensor(x[:], x[:], bo_all[:, L, :], ALU.add))
                dve.wait_ge(sem("low_out_psum"), l + 1)
                v.tensor_tensor(x[:], bank(6)[:, 0:D], x[:], ALU.add).then_inc(sem("xattn_done"), 1)
                dve.wait_ge(sem("xattn_done"), L + 1)

            def attn(L):
                parts, d, heads = AH[L], AD[L], AS[L]
                n = heads * P
                norm(3 * L + 1)
                if L == 3:
                    dve.wait_ge(sem("xnT_rev_psum"), 1)
                    v.tensor_copy(xnT_rev.rearrange("p c n -> p (c n)"), bank(1)[:, 0:D]
                                  ).then_inc(sem("xnT_rev_ready"), 1)
                for w, (dst, bias, name) in enumerate(((a_q, abq, "attn_q_ready"), (a_k, abk, "attn_k_ready"))):
                    dve.wait_ge(sem("attn_qk_psum"), 2 * L + w + 1)
                    o = dst[0:d, 0:parts * P].rearrange("p (h n) -> p h n", h=parts)
                    i = bank(4 * w, 4)[0:d, 0:parts * P].rearrange("p (h n) -> p h n", h=parts)
                    if L == 2:
                        v.tensor_copy(o, i).then_inc(sem(name), 1)
                    else:
                        v.tensor_tensor(o, i, bias[0:d, L, 0:parts].unsqueeze(2).to_broadcast([d, parts, P]),
                                        ALU.add).then_inc(sem(name), 1)
                dve.wait_ge(sem("attn_v_psum"), L + 1)
                if L == 2:
                    v.tensor_copy(a_v, bank(7)[:, 0:D]).then_inc(sem("attn_v_ready"), 1)
                else:
                    v.tensor_tensor(a_v, bank(7)[:, 0:D], abv[:, L, :], ALU.add).then_inc(sem("attn_v_ready"), 1)
                dve.wait_ge(sem("attn_scores"), L + 1)
                S3 = a_S[:, 0:n].rearrange("p (h n) -> p h n", h=heads)
                U3 = a_U[:, 0:n].rearrange("p (h n) -> p h n", h=heads)
                B3 = bank(0, 4)[:, 0:n].rearrange("p (h n) -> p h n", h=heads)

                def per_head(t2):
                    return t2[:, 0:heads].unsqueeze(2).to_broadcast([P, heads, P])
                if L < 3:
                    dve.wait_ge(sem("windows_ready"), 1)
                    win = windows[L][:].unsqueeze(1).to_broadcast([P, heads, P])
                if L < 2:
                    link(v.scalar_tensor_tensor(S3, B3, ASCALE[L], win, ALU.mult, ALU.add))
                elif L == 3:
                    dve.wait_ge(sem("rel_landed"), 16 * len(rel_loads))
                    link(v.scalar_tensor_tensor(S3, B3, ASCALE[L], rel, ALU.mult, ALU.add))
                else:
                    v.tensor_scalar(a_S, bank(0, 4), ASCALE[2], None, ALU.mult).then_inc(sem("l2_scaled"), 1)
                    dve.wait_ge(sem("l2_scaled"), 1)
                    link(v.tensor_reduce(a_m[:, 0:heads], S3, AX_X, ALU.add))
                    link(v.tensor_scalar(a_m[:, 0:heads], a_m[:, 0:heads], 1.0 / P, None, ALU.mult))
                    v.tensor_tensor(U3, S3, per_head(a_m), ALU.subtract).then_inc(sem("l2_centred"), 1)
                    link(v.tensor_scalar(ngates[:], gates[:], -1.0, None, ALU.mult))
                    dve.wait_ge(sem("l2_act"), 2)
                    link(v.scalar_tensor_tensor(a_T, a_T, ngates[:, 0:1], a_S, ALU.mult, ALU.add))
                    link(v.scalar_tensor_tensor(a_T, a_S, gates[:, 1:2], a_T, ALU.mult, ALU.add))
                    dve.wait_ge(sem("l2_act"), 3)
                    link(v.scalar_tensor_tensor(a_S, a_U, ngates[:, 2:3], a_T, ALU.mult, ALU.add))
                    link(v.tensor_tensor(S3, S3, win, ALU.add))
                link(v.tensor_reduce(a_m[:, 0:heads], S3, AX_X, ALU.max))
                v.tensor_tensor(S3, S3, per_head(a_m), ALU.subtract).then_inc(sem("attn_shifted"), 1)
                dve.wait_ge(sem("attn_probs"), L + 1)
                link(v.tensor_reduce(a_s[:, 0:heads], S3, AX_X, ALU.add))
                link(v.reciprocal(a_s[:, 0:heads], a_s[:, 0:heads]))
                dve.wait_ge(sem("attn_o_psum"), L + 1)
                w = D // heads
                v.tensor_tensor(a_o.rearrange("p (h n) -> p h n", h=heads),
                                bank(4)[:, 0:D].rearrange("p (h n) -> p h n", h=heads),
                                a_s[:, 0:heads].unsqueeze(2).to_broadcast([P, heads, w]), ALU.mult
                                ).then_inc(sem("attn_o_ready"), 1)
                dve.wait_ge(sem("attn_oT_psum"), L + 1)
                v.tensor_copy(a_oT.rearrange("p c n -> p (c n)"), bank(5)[:, 0:D]).then_inc(sem("attn_oT_ready"), 1)
                if L != 2:
                    link(v.tensor_tensor(x[:], x[:], bo_all[:, 4 + L, :], ALU.add))
                if L == 1:
                    link(v.tensor_tensor(x[:], x[:], xn[:], ALU.add))
                dve.wait_ge(sem("attn_out_psum"), L + 1)
                v.tensor_tensor(x[:], bank(6)[:, 0:D], x[:], ALU.add).then_inc(sem("attn_done"), 1)
                dve.wait_ge(sem("attn_done"), L + 1)

            def softmax_route(L, e):
                dve.wait_ge(sem("logits_psum"), L + 1)
                link(v.tensor_reduce(rmax[:], bank(1)[:, 0:e], AX_X, ALU.max))
                v.tensor_scalar(logit[:, 0:e], bank(1)[:, 0:e], rmax[:, 0:1], None, ALU.subtract
                                ).then_inc(sem("route_shifted"), 1)
                dve.wait_ge(sem("route_exp"), L + 1)
                link(v.tensor_reduce(rsum[:], prob[:, 0:e], AX_X, ALU.add))
                link(v.reciprocal(rinv[:], rsum[:]))
                link(v.tensor_scalar(prob[:, 0:e], prob[:, 0:e], rinv[:, 0:1], None, ALU.mult))

            def pick_top(e, k):
                link(v.memset(prob[:, e:e + 8], -1.0))
                link(v.max(top8[:], prob[:, 0:e]))
                if k < 8:
                    link(v.memset(top8[:, k:8], -1.0))
                link(v.match_replace(probr[:, 0:e + 8], top8[:], prob[:, 0:e + 8], -2.0))
                link(v.scalar_tensor_tensor(comb[:, 0:e], probr[:, 0:e], -2.0, prob[:, 0:e], ALU.is_equal, ALU.mult))

            def finish(L, value):
                v.tensor_tensor(x[:], value, x[:], ALU.add).then_inc(sem("ffn_done"), 1)
                dve.wait_ge(sem("ffn_done"), L + 1)

            def ffn_glu(L):
                f = FW[L]
                fc = f // 2
                e_n = 8 if L == 0 else 64
                norm(3 * L + 2)
                softmax_route(L, e_n)
                if L == 0:
                    pick_top(8, 2)
                    link(v.memset(comb[:, 8:10], 1.0))
                else:
                    pick_top(64, 8)
                    link(v.tensor_reduce(rsum[:], top8[:], AX_X, ALU.add))
                    link(v.reciprocal(rinv[:], rsum[:]))
                    link(v.tensor_scalar(comb[:, 0:64], comb[:, 0:64], rinv[:, 0:1], None, ALU.mult))
                    link(v.memset(comb[:, 64:65], 1.0))
                b0 = 0 if L == 0 else NE[0]

                def hidden(e, par, at):
                    dve.wait_ge(sem("silu"), at)
                    wait_count(dve, sem("hT_psum"), at - 2)
                    v.scalar_tensor_tensor(h_s[:, par, 0:f], g_s[:, par, 0:f], comb[:, bass.ds(e, 1)],
                                           bank(5 + 2 * par)[:, 0:f], ALU.mult, ALU.mult
                                           ).then_inc(sem("h_ready"), 1)

                def turned(par, at):
                    dve.wait_ge(sem("hT_psum"), at)
                    v.tensor_copy(hT[0:fc, par, :], bank(par)[0:fc, 0:2 * P]).then_inc(sem("hT_ready"), 1)
                for e in range(2):
                    hidden(e, e, b0 + e + 1)
                loops = 0
                if L == 2:
                    loops = 64 // RING - 1
                    with dve.Fori(0, loops) as it:
                        for j in range(RING):
                            turned(j % 2, it * RING + (b0 + j + 1))
                            hidden(it * RING + (j + 2), j % 2, it * RING + (b0 + j + 3))
                for e in range(loops * RING, NE[L]):
                    turned(e % 2, b0 + e + 1)
                    if e + 2 < NE[L]:
                        hidden(e + 2, e % 2, b0 + e + 3)
                dve.wait_ge(sem("ring_used"), NE0[L + 1])
                finish(L, bank(2)[:, 0:D])

            def ffn1():
                norm(5)
                softmax_route(1, 32)
                pick_top(32, 2)
                link(v.memset(y_acc, 0.0))
                for e in range(NE[1]):
                    dve.wait_ge(sem("ring_used"), NE0[1] + e + 1)
                    for j in range(2):
                        if e >= 1:
                            dve.wait_ge(sem("l1_step"), 2 * (e - 1) + j + 1)
                        g = v.scalar_tensor_tensor(y_acc[:, j, :], bank(4 + e % 2)[:, j * D:(j + 1) * D],
                                                   comb[:, 2 * e + j:2 * e + j + 1], y_acc[:, j, :],
                                                   ALU.mult, ALU.add)
                        g.then_inc(sem("l1_step"), 1)
                dve.wait_ge(sem("l1_step"), 2 * NE[1])
                link(v.tensor_tensor(y_acc[:, 0, :], y_acc[:, 0, :], y_acc[:, 1, :], ALU.add))
                finish(1, y_acc[:, 0, :])

            def ffn3():
                v.tensor_tensor(csq[:], rw[:, 3, :, 0:8], rw[:, 3, :, 0:8], ALU.mult).then_inc(sem("csq_ready"), 1)
                norm(11)
                link(v.tensor_tensor(xsq, xn[:], xn[:], ALU.mult))
                v.tensor_reduce(rsum[:], xsq, AX_X, ALU.add).then_inc(sem("xsq_ready"), 1)
                dve.wait_ge(sem("norms_ready"), 2)
                link(v.tensor_scalar(rsum[:], rsum[:], 1e-12, None, ALU.max))
                link(v.reciprocal(rinv[:], rsum[:]))
                link(v.tensor_scalar(cnorm[:], cnorm[:], 1e-12, None, ALU.max))
                link(v.reciprocal(cnorm[:], cnorm[:]))
                dve.wait_ge(sem("logits_psum"), 4)
                link(v.scalar_tensor_tensor(logit[:, 0:8], bank(1)[:, 0:8], rinv[:, 0:1], cnorm[:], ALU.mult, ALU.mult))
                link(v.tensor_tensor(logit[:, 0:8], bank(1)[:, 8:16], logit[:, 0:8], ALU.add))
                link(v.max(top8[:], logit[:, 0:8]))
                link(v.tensor_scalar(comb[:, 0:8], logit[:, 0:8], top8[:, 1:2], None, ALU.is_ge))
                v.tensor_scalar(logit[:, 0:8], logit[:, 0:8], top8[:, 0:1], None, ALU.subtract
                                ).then_inc(sem("route_shifted"), 1)
                dve.wait_ge(sem("route_exp"), 4)
                link(v.tensor_tensor(comb[:, 0:8], prob[:, 0:8], comb[:, 0:8], ALU.mult))
                link(v.tensor_reduce(rsum[:], comb[:, 0:8], AX_X, ALU.add))
                link(v.reciprocal(rinv[:], rsum[:]))
                v.tensor_scalar(comb[:, 0:8], comb[:, 0:8], rinv[:, 0:1], None, ALU.mult).then_inc(sem("comb_ready"), 1)
                dve.wait_ge(sem("comb_ready"), 1)
                dve.wait_ge(sem("gT_psum"), 1)
                v.tensor_copy(gT, bank(2)[0:8, 0:P]).then_inc(sem("gT_ready"), 1)
                dve.wait_ge(sem("b2_psum"), 1)
                link(v.tensor_copy(y_acc[:, 0, :], bank(3)[:, 0:D]))
                for e in range(8):
                    dve.wait_ge(sem("ring_used"), NE0[3] + e + 1)
                    if e:
                        dve.wait_ge(sem("l3_taken"), e)
                    v.scalar_tensor_tensor(y_acc[:, 0, :], bank(6 + e % 2)[:, 0:D], comb[:, e:e + 1],
                                           y_acc[:, 0, :], ALU.mult, ALU.add).then_inc(sem("l3_taken"), 1)
                dve.wait_ge(sem("l3_taken"), 8)
                finish(3, y_acc[:, 0, :])

            for s in range(stages):
                L = s // 3
                if s % 3 == 0:
                    (xattn if L < 2 else xattn_low)(L)
                elif s % 3 == 1:
                    attn(L)
                elif L in (0, 2):
                    ffn_glu(L)
                elif L == 1:
                    ffn1()
                else:
                    ffn3()
            v.tensor_scalar(x[:], x[:], 1.0, None, ALU.mult).then_inc(sem("x_final"), 1)


STAGES = 12


def kernel(**inputs):
    import numpy as np
    import concourse.bacc as bacc
    from concourse.bass_utils import run_bass_kernel_spmd

    nc = bacc.Bacc("TRN2", target_bir_lowering=False, num_devices=1)
    a = {n: np.asarray(v) for n, v in inputs.items()}
    lay = {"x": a["x"][0], "ctx": a["ctx_768"][0], "mask": a["mask_BxS2_bk0"][0]}
    xn = [("L0_xattn_W_q", "L0_xattn_W_k", "L0_xattn_W_v", "L0_xattn_W_o"),
          ("L1_xattn_w_q", None, None, "L1_xattn_w_out"),
          ("L2_xattn_Wq", "L2_xattn_Wk", "L2_xattn_Wv", "L2_xattn_Wo"),
          ("L3_xattn_wq", "L3_xattn_wk", "L3_xattn_wv", "L3_xattn_wo")]
    lay["kv23"] = np.concatenate([
        np.concatenate([a[f"L{L}_xattn_{'W' if L == 2 else 'w'}{n}"], a[f"L{L}_xattn_b{n}"][None]])
        for n in "kv" for L in (2, 3)], axis=1)
    for L, (q, k, v, o) in enumerate(xn):
        inner = XH[L] * XD[L]
        if L >= 2:
            lay[f"x{L}_wq"] = np.tile(a[q].reshape(D, WP, 1, 32), (1, 1, 4, 1)).reshape(D, WP * P)
            lay[f"x{L}_wo"] = a[o]
            continue
        kv = a["L1_xattn_w_kv"]
        lay[f"x{L}_wq"] = a[q]
        bk = np.zeros(inner, np.float32)
        wk = np.concatenate([(a[k] if k else kv[:, :inner]).T, bk[:, None]], axis=1)
        lay[f"x{L}_wkT"] = wk.reshape(XH[L], XD[L], C + 1).transpose(1, 0, 2)
        lay[f"x{L}_wv"] = a[v] if v else kv[:, inner:]
        lay[f"x{L}_wo"] = a[o]
    for n in "qkvo":
        lay[f"a0_w{n}"] = a[f"L0_attn_W{n}"]
        lay[f"a1_w{n}"] = a[f"L1_attn_W{n}"].T
        lay[f"a2_w{n}"] = a[f"L2_attn_W{n}"].T
    for i, n in enumerate("qkv"):
        lay[f"a3_w{n}"] = a["L3_attn_W_qkv"][:, i * D:(i + 1) * D]
    lay["a3_wo"] = a["L3_attn_W_out"]
    for n in ["L0_xattn_b_o", "L1_xattn_b_out", "L2_xattn_bo", "L3_xattn_bo", "L0_attn_bo", "L1_attn_bo",
              "L3_attn_b_out", "L0_ffn_router_w", "L0_ffn_gate_w", "L0_ffn_up_w",
              "L0_ffn_down_w", "L0_ffn_shared_gate_w", "L0_ffn_shared_up_w", "L0_ffn_shared_down_w",
              "L1_ffn_expert_weights", "L2_ffn_w_gate", "L2_ffn_w_up", "L2_ffn_w_down", "L2_ffn_ws_gate_up",
              "L2_ffn_ws_down", "L3_ffn_w1", "L3_ffn_w2", "L3_ffn_b2"]:
        lay[n] = a[n]
    for n in ["sep", "align", "coh"]:
        lay[f"L2_attn_{n}_gate"] = a[f"L2_attn_{n}_gate"].reshape(1)
    for n in ["L1_ffn_router_w", "L2_ffn_router_w", "L3_ffn_centroids", "L3_ffn_w_route"]:
        lay[n + "T"] = a[n].T
    for n in ["L2_xattn_bq", "L3_xattn_bq"]:
        lay[n + "T"] = a[n].reshape(WP, 32).T
    b3 = a["L3_attn_b_qkv"]
    for i, (q, k, v) in {0: (a["L0_attn_bq"], a["L0_attn_bk"], a["L0_attn_bv"]),
                         1: (a["L1_attn_bq"], a["L1_attn_bk"], a["L1_attn_bv"]),
                         3: (b3[0:D], b3[D:2 * D], b3[2 * D:3 * D])}.items():
        lay[f"a{i}_bqT"] = q.reshape(AH[i], AD[i]).T
        lay[f"a{i}_bkT"] = k.reshape(AH[i], AD[i]).T
        lay[f"a{i}_bv"] = v
    lay["L3_ffn_b1T"] = a["L3_ffn_b1"].T
    lay["L3_attn_rel_biasT"] = a["L3_attn_rel_bias"].T
    arrays, io = {}, {}
    for n, v in lay.items():
        v = np.ascontiguousarray(v)
        arrays[f"in_{n}"] = v
        io[n] = nc.dram_tensor(f"in_{n}", v.shape, mybir.dt.from_np(v.dtype), kind="ExternalInput").ap()
    out = nc.dram_tensor("out_x", (1, P, D), F32, kind="ExternalOutput").ap()
    build(nc, io, out.rearrange("a p d -> (a p) d"), STAGES)
    r = run_bass_kernel_spmd(nc, [arrays], core_ids=[0])
    return r.results[0]["out_x"]
```
